# Optimizing a Trainium2 kernel written in Bass

```python
import numpy as np
import jax
import jax.numpy as jnp

def _softmax(x, axis=-1):
    return jax.nn.softmax(x, axis=axis)

def _gelu(x):
    return jax.nn.gelu(x, approximate=True)

def _silu(x):
    return jax.nn.silu(x)

def _sigmoid(x):
    return jax.nn.sigmoid(x)

def _layernorm(x, axis=-1, eps=1e-05):
    m = jnp.mean(x, axis=axis, keepdims=True)
    v = jnp.var(x, axis=axis, keepdims=True)
    return (x - m) / jnp.sqrt(v + eps)

def _scatter_add(tgt, idx, src, axis=0):
    return tgt.at[idx].add(src)

def _segment_sum(src, seg, n):
    return jax.ops.segment_sum(src, seg, n)
kernel_name = 'mk_seq_preln_d4_jaxref_r8_28ea6c'

def setup_inputs(seed: int=0):
    np.random.seed(seed)
    _w = jnp.asarray

    def _L0_attn_setup():
        import jax, jax.numpy as jnp
        import numpy as np
        B, L, D, H = (4, 512, 128, 16)
        Dh = D // H
        DECAY_INIT, DECAY_RANGE = (5.0, 1.0)
        LN_EPS = 1e-05

        def _retention_scan(v, lam):
            a = jnp.broadcast_to(lam[None, None, :, None], v.shape)

            def combine(c1, c2):
                a1, b1 = c1
                a2, b2 = c2
                return (a1 * a2, a2 * b1 + b2)
            _, s = jax.lax.associative_scan(combine, (a, v), axis=1)
            return s

        def _layernorm(x, gamma, beta):
            mu = jnp.mean(x, axis=-1, keepdims=True)
            var = jnp.mean(jnp.square(x - mu), axis=-1, keepdims=True)
            return (x - mu) * jax.lax.rsqrt(var + LN_EPS) * gamma + beta
        key = jax.random.key(seed)
        ks = jax.random.split(key, 5)
        s = 1.0 / np.sqrt(D)
        x = jax.random.normal(ks[0], (B, L, D), dtype=jnp.float32)
        Wq = jax.random.normal(ks[1], (D, D), dtype=jnp.float32) * s
        Wv = jax.random.normal(ks[2], (D, D), dtype=jnp.float32) * s
        Wo = jax.random.normal(ks[3], (D, D), dtype=jnp.float32) * s
        Wg = jax.random.normal(ks[4], (D, D), dtype=jnp.float32) * s
        beta = DECAY_INIT + DECAY_RANGE * (jnp.arange(H, dtype=jnp.float32) / H)
        ln_gamma = jnp.ones((D,), dtype=jnp.float32)
        ln_beta = jnp.zeros((D,), dtype=jnp.float32)
        return {'x': x, 'Wq': Wq, 'Wv': Wv, 'Wo': Wo, 'Wg': Wg, 'beta': beta, 'ln_gamma': ln_gamma, 'ln_beta': ln_beta}
    _L0_attn_in = _L0_attn_setup()

    def _L0_ffn_setup():
        import jax, jax.numpy as jnp
        import numpy as np
        D_MODEL, D_FF, N_EXPERTS, TOP_K = (128, 512, 8, 2)
        key = jax.random.key(seed)
        k0, k1, k2, k3 = jax.random.split(key, 4)
        x = jax.random.normal(k0, (2, 256, D_MODEL), dtype=jnp.float32)
        Wg = jax.random.normal(k1, (D_MODEL, N_EXPERTS), dtype=jnp.float32) * 0.02
        W1 = jax.random.normal(k2, (N_EXPERTS, D_MODEL, D_FF), dtype=jnp.float32) * 0.02
        b1 = jnp.zeros((N_EXPERTS, D_FF), dtype=jnp.float32)
        W2 = jax.random.normal(k3, (N_EXPERTS, D_FF, D_MODEL), dtype=jnp.float32) * 0.02
        b2 = jnp.zeros((N_EXPERTS, D_MODEL), dtype=jnp.float32)
        return {'x': x, 'Wg': Wg, 'W1': W1, 'b1': b1, 'W2': W2, 'b2': b2}
    _L0_ffn_in = _L0_ffn_setup()

    def _L1_attn_setup():
        import jax, jax.numpy as jnp
        import numpy as np
        import math
        DIM, DIM_QK, DIM_V = (128, 128, 128)
        NUM_BUCKETS, MAX_DISTANCE = (32, 128)

        def silu(x):
            return x * jax.nn.sigmoid(x)

        def laplacian_attn_fn(x):
            mu = math.sqrt(0.5)
            std = math.sqrt(0.25 * math.pi)
            return (1.0 + jax.lax.erf((x - mu) / (std * math.sqrt(2.0)))) * 0.5

        def rel_pos_bias(seq_len, table, scale):
            q_pos = jnp.arange(seq_len)
            k_pos = jnp.arange(seq_len)
            rel_pos = k_pos[None, :] - q_pos[:, None]
            n = jnp.maximum(-rel_pos, 0)
            max_exact = NUM_BUCKETS // 2
            is_small = n < max_exact
            n_safe = jnp.maximum(n, 1).astype(jnp.float32)
            val_if_large = max_exact + (jnp.log(n_safe / max_exact) / math.log(MAX_DISTANCE / max_exact) * (NUM_BUCKETS - max_exact)).astype(jnp.int32)
            val_if_large = jnp.minimum(val_if_large, NUM_BUCKETS - 1)
            bucket = jnp.where(is_small, n, val_if_large)
            return table[bucket] * scale
        key = jax.random.key(seed)
        ks = jax.random.split(key, 8)
        B, S = (4, 256)
        lin_std_qk = 1.0 / math.sqrt(DIM)
        return {'x': jax.random.normal(ks[0], (B, S, DIM), dtype=jnp.float32), 'wqk': jax.random.uniform(ks[1], (DIM, DIM_QK), minval=-lin_std_qk, maxval=lin_std_qk, dtype=jnp.float32), 'bqk': jnp.zeros((DIM_QK,), dtype=jnp.float32), 'gamma': 1.0 + 0.02 * jax.random.normal(ks[2], (2, DIM_QK), dtype=jnp.float32), 'beta': jnp.zeros((2, DIM_QK), dtype=jnp.float32), 'wv': jax.random.uniform(ks[3], (DIM, DIM_V), minval=-lin_std_qk, maxval=lin_std_qk, dtype=jnp.float32), 'bv': jnp.zeros((DIM_V,), dtype=jnp.float32), 'rel_bias': jax.random.normal(ks[4], (NUM_BUCKETS,), dtype=jnp.float32)}
    _L1_attn_in = _L1_attn_setup()

    def _L1_ffn_setup():
        import jax, jax.numpy as jnp
        import numpy as np
        B, S, H, FFN, E = (2, 256, 128, 512, 8)
        key = jax.random.key(seed)
        k0, k1, k2, k3 = jax.random.split(key, 4)
        return {'hidden_states': jax.random.normal(k0, (B, S, H), dtype=jnp.float32), 'Wr': jax.random.normal(k1, (H, E), dtype=jnp.float32) * 0.02, 'br': jnp.zeros((E,), dtype=jnp.float32), 'W1': jax.random.normal(k2, (E, H, FFN), dtype=jnp.float32) * 0.02, 'W2': jax.random.normal(k3, (E, FFN, H), dtype=jnp.float32) * 0.02}
    _L1_ffn_in = _L1_ffn_setup()

    def _L2_attn_setup():
        import jax, jax.numpy as jnp
        import numpy as np
        DT = 0.1

        def _reference_tuple_inner(x_seq, omega_raw, B_weight):
            dt = DT
            omega = jax.nn.softplus(omega_raw)
            Bx_seq = jnp.einsum('btd,ed->bte', x_seq, B_weight)
            Bsz, T, D = x_seq.shape
            u0 = jnp.zeros((Bsz, D), dtype=x_seq.dtype)
            v0 = jnp.zeros((Bsz, D), dtype=x_seq.dtype)

            def step(carry, Bx_t):
                u_prev, v_prev = carry
                u_next = u_prev + dt * (-omega * v_prev + Bx_t)
                v_next = v_prev + dt * u_next
                return ((u_next, v_next), (u_next, v_next))
            _, (u_seq, v_seq) = jax.lax.scan(step, (u0, v0), jnp.swapaxes(Bx_seq, 0, 1))
            u_seq = jnp.swapaxes(u_seq, 0, 1)
            v_seq = jnp.swapaxes(v_seq, 0, 1)
            y_seq = v_seq
            return (y_seq, u_seq, v_seq)
        key = jax.random.key(seed)
        k1, k2, k3 = jax.random.split(key, 3)
        Bsz, T, D = (4, 512, 128)
        x_seq = jax.random.normal(k1, (Bsz, T, D), dtype=jnp.float32)
        omega_raw = jax.random.normal(k2, (D,), dtype=jnp.float32)
        B_weight = jax.random.normal(k3, (D, D), dtype=jnp.float32) * (1.0 / np.sqrt(D))
        return {'x_seq': x_seq, 'omega_raw': omega_raw, 'B_weight': B_weight}
    _L2_attn_in = _L2_attn_setup()

    def _L2_ffn_setup():
        import jax, jax.numpy as jnp
        import numpy as np
        N_EXPERTS = 8
        TOP_K = 2
        D_MODEL = 128
        HIDDEN = 512
        ROUTED_H = 128
        BATCH, SEQ = (2, 512)
        key = jax.random.key(seed)
        ks = jax.random.split(key, 8)
        std = 0.02
        return {'x': jax.random.normal(ks[0], (BATCH, SEQ, D_MODEL), dtype=jnp.float32), 'w12': std * jax.random.normal(ks[1], (N_EXPERTS, 2 * ROUTED_H, D_MODEL), dtype=jnp.float32), 'w3': std * jax.random.normal(ks[2], (N_EXPERTS, D_MODEL, ROUTED_H), dtype=jnp.float32), 'shared_w1': std * jax.random.normal(ks[3], (HIDDEN, D_MODEL), dtype=jnp.float32), 'shared_w2': std * jax.random.normal(ks[4], (HIDDEN, D_MODEL), dtype=jnp.float32), 'shared_w3': std * jax.random.normal(ks[5], (D_MODEL, HIDDEN), dtype=jnp.float32), 'router_w': std * jax.random.normal(ks[6], (N_EXPERTS, D_MODEL), dtype=jnp.float32), 'expert_bias': jnp.zeros((N_EXPERTS,), dtype=jnp.float32)}
    _L2_ffn_in = _L2_ffn_setup()

    def _L3_attn_setup():
        import jax, jax.numpy as jnp
        import numpy as np
        DIM = 128
        NUM_HEADS = 16
        HEAD_DIM = DIM // NUM_HEADS
        ROPE_BASE = 10000.0

        def rope_cos_sin(seq_len, dim):
            inv_freq = 1.0 / ROPE_BASE ** (jnp.arange(0, dim, 2, dtype=jnp.float32) / dim)
            t = jnp.arange(seq_len, dtype=jnp.float32)
            freqs = t[:, None] * inv_freq[None, :]
            emb = jnp.concatenate([freqs, freqs], axis=-1)
            return (jnp.cos(emb), jnp.sin(emb))

        def apply_rotary(x, cos, sin):
            x1 = x[..., ::2]
            x2 = x[..., 1::2]
            x_rot = jnp.stack((-x2, x1), axis=-1).reshape(x.shape)
            return x * cos + x_rot * sin
        key = jax.random.key(seed)
        ks = jax.random.split(key, 5)
        B, L, C = (4, 256, DIM)
        s = 1.0 / np.sqrt(C)
        return {'x': jax.random.normal(ks[0], (B, L, C), dtype=jnp.float32), 'qkv_w': jax.random.normal(ks[1], (3 * C, C), dtype=jnp.float32) * s, 'qkv_b': jax.random.normal(ks[2], (3 * C,), dtype=jnp.float32) * 0.02, 'proj_w': jax.random.normal(ks[3], (C, C), dtype=jnp.float32) * s, 'proj_b': jax.random.normal(ks[4], (C,), dtype=jnp.float32) * 0.02}
    _L3_attn_in = _L3_attn_setup()

    def _L3_ffn_setup():
        import jax, jax.numpy as jnp
        import numpy as np
        E, D, H = (8, 128, 512)
        B, S = (4, 512)
        TEMPERATURE = 1.0
        key = jax.random.key(seed)
        ks = jax.random.split(key, 7)
        sc = 0.02
        return {'x': jax.random.normal(ks[0], (B, S, D), dtype=jnp.float32), 'W1': jax.random.normal(ks[1], (E, D, H), dtype=jnp.float32) * sc, 'b1': jax.random.normal(ks[2], (E, H), dtype=jnp.float32) * sc, 'W2': jax.random.normal(ks[3], (E, H, D), dtype=jnp.float32) * sc, 'b2': jax.random.normal(ks[4], (E, D), dtype=jnp.float32) * sc, 'Wr': jax.random.normal(ks[5], (D, E), dtype=jnp.float32) * sc, 'br': jax.random.normal(ks[6], (E,), dtype=jnp.float32) * sc}
    _L3_ffn_in = _L3_ffn_setup()
    _d = {'L0_attn_x': _L0_attn_in['x'], 'L0_attn_Wq': _L0_attn_in['Wq'], 'L0_attn_Wv': _L0_attn_in['Wv'], 'L0_attn_Wo': _L0_attn_in['Wo'], 'L0_attn_Wg': _L0_attn_in['Wg'], 'L0_attn_beta': _L0_attn_in['beta'], 'L0_attn_ln_gamma': _L0_attn_in['ln_gamma'], 'L0_attn_ln_beta': _L0_attn_in['ln_beta'], 'L0_ffn_Wg': _L0_ffn_in['Wg'], 'L0_ffn_W1': _L0_ffn_in['W1'], 'L0_ffn_b1': _L0_ffn_in['b1'], 'L0_ffn_W2': _L0_ffn_in['W2'], 'L0_ffn_b2': _L0_ffn_in['b2'], 'L1_attn_wqk': _L1_attn_in['wqk'], 'L1_attn_bqk': _L1_attn_in['bqk'], 'L1_attn_gamma': _L1_attn_in['gamma'], 'L1_attn_beta': _L1_attn_in['beta'], 'L1_attn_wv': _L1_attn_in['wv'], 'L1_attn_bv': _L1_attn_in['bv'], 'L1_attn_rel_bias': _L1_attn_in['rel_bias'], 'L1_ffn_Wr': _L1_ffn_in['Wr'], 'L1_ffn_br': _L1_ffn_in['br'], 'L1_ffn_W1': _L1_ffn_in['W1'], 'L1_ffn_W2': _L1_ffn_in['W2'], 'L2_attn_omega_raw': _L2_attn_in['omega_raw'], 'L2_attn_B_weight': _L2_attn_in['B_weight'], 'L2_ffn_w12': _L2_ffn_in['w12'], 'L2_ffn_w3': _L2_ffn_in['w3'], 'L2_ffn_shared_w1': _L2_ffn_in['shared_w1'], 'L2_ffn_shared_w2': _L2_ffn_in['shared_w2'], 'L2_ffn_shared_w3': _L2_ffn_in['shared_w3'], 'L2_ffn_router_w': _L2_ffn_in['router_w'], 'L2_ffn_expert_bias': _L2_ffn_in['expert_bias'], 'L3_attn_qkv_w': _L3_attn_in['qkv_w'], 'L3_attn_qkv_b': _L3_attn_in['qkv_b'], 'L3_attn_proj_w': _L3_attn_in['proj_w'], 'L3_attn_proj_b': _L3_attn_in['proj_b'], 'L3_ffn_W1': _L3_ffn_in['W1'], 'L3_ffn_b1': _L3_ffn_in['b1'], 'L3_ffn_W2': _L3_ffn_in['W2'], 'L3_ffn_b2': _L3_ffn_in['b2'], 'L3_ffn_Wr': _L3_ffn_in['Wr'], 'L3_ffn_br': _L3_ffn_in['br']}
    _x0 = _d['L0_attn_x']
    _d['L0_attn_x'] = jax.random.normal(jax.random.fold_in(jax.random.key(seed), 1), (8, 256, 128), dtype=_x0.dtype)
    del _x0
    return _d

def reference(L0_attn_x, L0_attn_Wq, L0_attn_Wv, L0_attn_Wo, L0_attn_Wg, L0_attn_beta, L0_attn_ln_gamma, L0_attn_ln_beta, L0_ffn_Wg, L0_ffn_W1, L0_ffn_b1, L0_ffn_W2, L0_ffn_b2, L1_attn_wqk, L1_attn_bqk, L1_attn_gamma, L1_attn_beta, L1_attn_wv, L1_attn_bv, L1_attn_rel_bias, L1_ffn_Wr, L1_ffn_br, L1_ffn_W1, L1_ffn_W2, L2_attn_omega_raw, L2_attn_B_weight, L2_ffn_w12, L2_ffn_w3, L2_ffn_shared_w1, L2_ffn_shared_w2, L2_ffn_shared_w3, L2_ffn_router_w, L2_ffn_expert_bias, L3_attn_qkv_w, L3_attn_qkv_b, L3_attn_proj_w, L3_attn_proj_b, L3_ffn_W1, L3_ffn_b1, L3_ffn_W2, L3_ffn_b2, L3_ffn_Wr, L3_ffn_br):

    def _L0_attn_ref(x, Wq, Wv, Wo, Wg, beta, ln_gamma, ln_beta):
        import jax, jax.numpy as jnp
        import numpy as np
        B, L, D, H = (4, 512, 128, 16)
        Dh = D // H
        DECAY_INIT, DECAY_RANGE = (5.0, 1.0)
        LN_EPS = 1e-05

        def _retention_scan(v, lam):
            a = jnp.broadcast_to(lam[None, None, :, None], v.shape)

            def combine(c1, c2):
                a1, b1 = c1
                a2, b2 = c2
                return (a1 * a2, a2 * b1 + b2)
            _, s = jax.lax.associative_scan(combine, (a, v), axis=1)
            return s

        def _layernorm(x, gamma, beta):
            mu = jnp.mean(x, axis=-1, keepdims=True)
            var = jnp.mean(jnp.square(x - mu), axis=-1, keepdims=True)
            return (x - mu) * jax.lax.rsqrt(var + LN_EPS) * gamma + beta
        b, l, d = x.shape
        tiny = jnp.finfo(jnp.float32).tiny
        lam = jnp.clip(1.0 - jnp.exp2(-beta), tiny, 1.0 - 1e-09)
        q = (x @ Wq.T).reshape(b, l, H, Dh)
        v = (x @ Wv.T).reshape(b, l, H, Dh)
        state = _retention_scan(v, lam)
        ret = (q * state).reshape(b, l, d)
        y = _layernorm(ret, ln_gamma, ln_beta)
        g = jax.nn.silu(x @ Wg.T)
        out = y * g @ Wo.T
        return out

    def _L0_ffn_ref(x, Wg, W1, b1, W2, b2):
        import jax, jax.numpy as jnp
        import numpy as np
        D_MODEL, D_FF, N_EXPERTS, TOP_K = (128, 512, 8, 2)
        B = x.shape[:-1]
        xs = x.reshape(-1, x.shape[-1])
        T = xs.shape[0]
        gate_logits = xs @ Wg
        weights, sel = jax.lax.top_k(gate_logits, TOP_K)
        weights = jax.nn.softmax(weights.astype(jnp.float32), axis=1).astype(x.dtype)
        h = jax.nn.relu(jnp.einsum('td,edf->etf', xs, W1) + b1[:, None, :])
        out_e = jnp.einsum('etf,efd->etd', h, W2) + b2[:, None, :]
        tok = jnp.arange(T)
        picked = out_e[sel, tok[:, None]]
        out = jnp.einsum('tk,tkd->td', weights, picked)
        return out.reshape(*B, x.shape[-1])

    def _L1_attn_ref(x, wqk, bqk, gamma, beta, wv, bv, rel_bias):
        import jax, jax.numpy as jnp
        import numpy as np
        import math
        DIM, DIM_QK, DIM_V = (128, 128, 128)
        NUM_BUCKETS, MAX_DISTANCE = (32, 128)

        def silu(x):
            return x * jax.nn.sigmoid(x)

        def laplacian_attn_fn(x):
            mu = math.sqrt(0.5)
            std = math.sqrt(0.25 * math.pi)
            return (1.0 + jax.lax.erf((x - mu) / (std * math.sqrt(2.0)))) * 0.5

        def rel_pos_bias(seq_len, table, scale):
            q_pos = jnp.arange(seq_len)
            k_pos = jnp.arange(seq_len)
            rel_pos = k_pos[None, :] - q_pos[:, None]
            n = jnp.maximum(-rel_pos, 0)
            max_exact = NUM_BUCKETS // 2
            is_small = n < max_exact
            n_safe = jnp.maximum(n, 1).astype(jnp.float32)
            val_if_large = max_exact + (jnp.log(n_safe / max_exact) / math.log(MAX_DISTANCE / max_exact) * (NUM_BUCKETS - max_exact)).astype(jnp.int32)
            val_if_large = jnp.minimum(val_if_large, NUM_BUCKETS - 1)
            bucket = jnp.where(is_small, n, val_if_large)
            return table[bucket] * scale
        B, S, _ = x.shape
        qk = silu(x @ wqk + bqk)
        q = qk * gamma[0] + beta[0]
        k = qk * gamma[1] + beta[1]
        v = silu(x @ wv + bv)
        scale = 1.0 / S
        sim = jnp.einsum('bid,bjd->bij', q, k) * scale
        sim = sim + rel_pos_bias(S, rel_bias, DIM_QK ** 0.5)[None, :, :]
        attn = laplacian_attn_fn(sim)
        causal_mask = jnp.triu(jnp.ones((S, S), dtype=bool), k=1)
        attn = jnp.where(causal_mask[None, :, :], 0.0, attn)
        return jnp.einsum('bij,bjd->bid', attn, v)

    def _L1_ffn_ref(hidden_states, Wr, br, W1, W2):
        import jax, jax.numpy as jnp
        import numpy as np
        B, S, H, FFN, E = (2, 256, 128, 512, 8)
        b, s, h = hidden_states.shape
        x = hidden_states.reshape(-1, h)
        route = jax.nn.sigmoid(x @ Wr + br)
        max_prob = jnp.max(route, axis=1, keepdims=True)
        max_ind = jnp.argmax(route, axis=1)
        out = jnp.zeros_like(x)
        n_experts = Wr.shape[1]
        for e in range(n_experts):
            mask = (max_ind == e)[:, None].astype(x.dtype)
            y = jax.nn.gelu(x @ W1[e], approximate=False) @ W2[e]
            out = out + mask * y
        out = out * max_prob
        return out.reshape(b, s, h)

    def _L2_attn_ref(x_seq, omega_raw, B_weight):
        import jax, jax.numpy as jnp
        import numpy as np
        DT = 0.1

        def _reference_tuple_inner(x_seq, omega_raw, B_weight):
            dt = DT
            omega = jax.nn.softplus(omega_raw)
            Bx_seq = jnp.einsum('btd,ed->bte', x_seq, B_weight)
            Bsz, T, D = x_seq.shape
            u0 = jnp.zeros((Bsz, D), dtype=x_seq.dtype)
            v0 = jnp.zeros((Bsz, D), dtype=x_seq.dtype)

            def step(carry, Bx_t):
                u_prev, v_prev = carry
                u_next = u_prev + dt * (-omega * v_prev + Bx_t)
                v_next = v_prev + dt * u_next
                return ((u_next, v_next), (u_next, v_next))
            _, (u_seq, v_seq) = jax.lax.scan(step, (u0, v0), jnp.swapaxes(Bx_seq, 0, 1))
            u_seq = jnp.swapaxes(u_seq, 0, 1)
            v_seq = jnp.swapaxes(v_seq, 0, 1)
            y_seq = v_seq
            return (y_seq, u_seq, v_seq)
        return _reference_tuple_inner(x_seq, omega_raw, B_weight)[0]

    def _L2_ffn_ref(x, w12, w3, shared_w1, shared_w2, shared_w3, router_w, expert_bias):
        import jax, jax.numpy as jnp
        import numpy as np
        N_EXPERTS = 8
        TOP_K = 2
        D_MODEL = 128
        HIDDEN = 512
        ROUTED_H = 128
        BATCH, SEQ = (2, 512)
        b, s, d = x.shape
        xf = x.reshape(-1, d)
        shared = jax.nn.silu(xf @ shared_w1.T) * (xf @ shared_w2.T) @ shared_w3.T
        scores = jax.nn.sigmoid(xf @ router_w.T)
        _, top_idx = jax.lax.top_k(scores + expert_bias, TOP_K)
        mask = jax.nn.one_hot(top_idx, N_EXPERTS, dtype=xf.dtype).sum(axis=-2)
        gates = scores * mask
        h12 = jnp.einsum('td,ehd->teh', xf, w12)
        h1, h2 = jnp.split(h12, 2, axis=-1)
        h = jax.nn.silu(h1) * h2 * gates[:, :, None]
        routed = jnp.einsum('teh,edh->td', h, w3)
        return (shared + routed).reshape(b, s, d)

    def _L3_attn_ref(x, qkv_w, qkv_b, proj_w, proj_b):
        import jax, jax.numpy as jnp
        import numpy as np
        DIM = 128
        NUM_HEADS = 16
        HEAD_DIM = DIM // NUM_HEADS
        ROPE_BASE = 10000.0

        def rope_cos_sin(seq_len, dim):
            inv_freq = 1.0 / ROPE_BASE ** (jnp.arange(0, dim, 2, dtype=jnp.float32) / dim)
            t = jnp.arange(seq_len, dtype=jnp.float32)
            freqs = t[:, None] * inv_freq[None, :]
            emb = jnp.concatenate([freqs, freqs], axis=-1)
            return (jnp.cos(emb), jnp.sin(emb))

        def apply_rotary(x, cos, sin):
            x1 = x[..., ::2]
            x2 = x[..., 1::2]
            x_rot = jnp.stack((-x2, x1), axis=-1).reshape(x.shape)
            return x * cos + x_rot * sin
        B, L, C = x.shape
        H, D = (NUM_HEADS, HEAD_DIM)
        scale = D ** (-0.5)
        qkv = x @ qkv_w.T + qkv_b
        qkv = qkv.reshape(B, L, 3, H, D).transpose(2, 0, 3, 1, 4)
        q, k, v = (qkv[0], qkv[1], qkv[2])
        cos, sin = rope_cos_sin(L, D)
        q = apply_rotary(q, cos, sin)
        k = apply_rotary(k, cos, sin)
        attn = jnp.einsum('bhqd,bhkd->bhqk', q, k) * scale
        attn = jax.nn.softmax(attn, axis=-1)
        out = jnp.einsum('bhqk,bhkd->bhqd', attn, v)
        out = out.transpose(0, 2, 1, 3).reshape(B, L, C)
        return out @ proj_w.T + proj_b

    def _L3_ffn_ref(x, W1, b1, W2, b2, Wr, br):
        import jax, jax.numpy as jnp
        import numpy as np
        E, D, H = (8, 128, 512)
        B, S = (4, 512)
        TEMPERATURE = 1.0
        routing_logits = (x @ Wr + br) / TEMPERATURE
        routing_probs = jax.nn.softmax(routing_logits, axis=-1)
        indices = jnp.argmax(routing_probs, axis=-1)
        out = jnp.zeros_like(x)
        num_experts = W1.shape[0]
        for i in range(num_experts):
            mask = (indices == i).astype(x.dtype)[..., None]
            xi = x * mask
            h = jax.nn.relu(xi @ W1[i] + b1[i])
            out = out + (h @ W2[i] + b2[i])
        return out
    x = L0_attn_x
    x = x + _L0_attn_ref(_layernorm(x, axis=-1), L0_attn_Wq, L0_attn_Wv, L0_attn_Wo, L0_attn_Wg, L0_attn_beta, L0_attn_ln_gamma, L0_attn_ln_beta)
    x = x + _L0_ffn_ref(_layernorm(x, axis=-1), L0_ffn_Wg, L0_ffn_W1, L0_ffn_b1, L0_ffn_W2, L0_ffn_b2)
    x = x + _L1_attn_ref(_layernorm(x, axis=-1), L1_attn_wqk, L1_attn_bqk, L1_attn_gamma, L1_attn_beta, L1_attn_wv, L1_attn_bv, L1_attn_rel_bias)
    x = x + _L1_ffn_ref(_layernorm(x, axis=-1), L1_ffn_Wr, L1_ffn_br, L1_ffn_W1, L1_ffn_W2)
    x = x + _L2_attn_ref(_layernorm(x, axis=-1), L2_attn_omega_raw, L2_attn_B_weight)
    x = x + _L2_ffn_ref(_layernorm(x, axis=-1), L2_ffn_w12, L2_ffn_w3, L2_ffn_shared_w1, L2_ffn_shared_w2, L2_ffn_shared_w3, L2_ffn_router_w, L2_ffn_expert_bias)
    x = x + _L3_attn_ref(_layernorm(x, axis=-1), L3_attn_qkv_w, L3_attn_qkv_b, L3_attn_proj_w, L3_attn_proj_b)
    x = x + _L3_ffn_ref(_layernorm(x, axis=-1), L3_ffn_W1, L3_ffn_b1, L3_ffn_W2, L3_ffn_b2, L3_ffn_Wr, L3_ffn_br)
    return x

_drawn_inputs = setup_inputs


def setup_inputs(seed=0):
    import zlib

    import numpy as np

    out = dict(_drawn_inputs(seed))
    spreads = {'L0_attn_ln_gamma': (1.0, 0.2),
     'L0_attn_ln_beta': (0.0, 0.1),
     'L0_ffn_b1': (0.0, 0.404),
     'L0_ffn_b2': (0.0, 0.1),
     'L1_attn_bqk': (0.0, 2.0),
     'L1_attn_beta': (0.0, 2.0),
     'L1_attn_bv': (0.0, 0.1),
     'L1_ffn_br': (0.0, 0.8),
     'L2_ffn_expert_bias': (0.0, 0.8)}
    factors = {'L0_ffn_W1': 3.89,
     'L1_attn_wqk': 35.225,
     'L1_attn_gamma': 64.0,
     'L1_ffn_Wr': 8.0,
     'L1_ffn_W1': 8.0,
     'L1_ffn_W2': 8.0,
     'L2_ffn_w12': 8.0,
     'L2_ffn_w3': 8.0,
     'L2_ffn_shared_w1': 8.0,
     'L2_ffn_shared_w2': 8.0,
     'L2_ffn_shared_w3': 8.0,
     'L2_ffn_router_w': 8.0,
     'L3_attn_qkv_b': 8.0,
     'L3_attn_proj_b': 8.0,
     'L3_ffn_W1': 8.0,
     'L3_ffn_b1': 8.0,
     'L3_ffn_W2': 8.0,
     'L3_ffn_b2': 21.437,
     'L3_ffn_Wr': 8.0,
     'L3_ffn_br': 8.0,
     'L1_attn_rel_bias': 3.445}
    for name, (base, spread) in spreads.items():
        noise = np.random.default_rng([zlib.crc32(name.encode()), seed]).standard_normal(out[name].shape)
        drawn = base * np.exp(spread * noise) if base else spread * noise
        out[name] = jnp.asarray(drawn.astype(out[name].dtype))
    for name, factor in factors.items():
        out[name] = (out[name] * factor).astype(out[name].dtype)
    return out
```

```python
from contextlib import ExitStack
import math

import numpy as np

import concourse.bass as bass
from concourse import mybir

F32 = mybir.dt.float32
BF16 = mybir.dt.bfloat16
I32 = mybir.dt.int32
ALU = mybir.AluOpType
ACT = mybir.ActivationFunctionType
AX = mybir.AxisListType

P = 128
D = 128
NB, L = 8, 256
T = NB * L
NTILE = T // P
CH = 512
NCH = T // CH
TPC = CH // P
E = 8
FF = 512
KF = FF // P
EPS = 1e-5
NEG = -3.0e38
HEADS, HD = 16, 8
UNITS = KF + E
RH = 16
DT = 0.1

NBUCKET, MAX_DISTANCE = 32, 128
BIASW = 3 * P
MU, STD = math.sqrt(0.5), math.sqrt(0.25 * math.pi)
TINY = 1e-30

STAGES = 8


def rope_tables():
    inv = 1.0 / 10000.0 ** (np.arange(0, HD, 2, dtype=np.float32) / HD)
    ang = np.arange(L, dtype=np.float32)[None, :] * np.concatenate([inv, inv]).astype(np.float32)[:, None]
    cos, sin = (np.tile(f(ang).astype(np.float32), (HEADS, 1)) for f in (np.cos, np.sin))
    scale = np.float32(HD ** -0.5)
    return np.ascontiguousarray(np.stack([-cos * scale, -sin * scale, cos, sin], axis=1))


def pair_matrix():
    m = np.zeros((P, P), np.float32)
    for i in range(0, P, 2):
        m[i + 1, i], m[i, i + 1] = -1.0, 1.0
    return m


def bucket_rows():
    n = np.maximum(np.arange(BIASW) - (P - 1), 0)
    exact = NBUCKET // 2
    ratio = (np.log(np.maximum(n, 1).astype(np.float32) / np.float32(exact))
             / np.float32(math.log(MAX_DISTANCE / exact)) * np.float32(NBUCKET - exact))
    large = np.minimum(exact + ratio.astype(np.int32), NBUCKET - 1)
    b = np.where(n < exact, n, large)
    return (b[None, :] == np.arange(NBUCKET)[:, None]).astype(np.float32)


def moe_tiles(k):
    n = k * T // P + E
    return (n + 3) // 4 * 4


def build(nc, a, out):
    ctx = ExitStack()

    def sb(name, shape, dt=F32):
        return ctx.enter_context(nc.sbuf_tensor(name, shape, dt))

    sems = {}

    def S(name):
        if name not in sems:
            sems[name] = ctx.enter_context(nc.semaphore(name))
        return sems[name]

    with ctx:
        x_sb = sb("x_sb", [P, NTILE, D])
        xn = sb("xn", [P, NTILE, D])
        xt = sb("xt", [P, T])
        buf_a = sb("buf_a", [P, T])
        buf_b = sb("buf_b", [P, T])
        buf_c = sb("buf_c", [P, T])
        ident = sb("ident", [P, P])
        ones = sb("ones", [P, P])
        before = sb("before", [P, P])
        stats = sb("stats", [P, NTILE, 6])
        stats2 = sb("stats2", [P, NTILE, 6])
        lnt = sb("lnt", [P, 8, NTILE])
        psum = ctx.enter_context(nc.psum_tensor("psum", [P, 8, CH], F32))

        w_q = sb("w_q", [P, D])
        w_v = sb("w_v", [P, D])
        w_g = sb("w_g", [P, D])
        w_o = sb("w_o", [P, D])
        state = sb("state", [P, CH])
        lam_col = sb("lam_col", [P, 4])
        lam = sb("lam", [P, L])
        gb = sb("gb", [P, 2])

        w_qk1 = sb("w_qk1", [P, D])
        w_v1 = sb("w_v1", [P, D])
        cols1 = sb("cols1", [P, 5])
        bv1 = sb("bv1", [P, D])
        table = sb("table", [NBUCKET, 1])
        table_all = sb("table_all", [NBUCKET, P])
        bucket = sb("bucket", [NBUCKET, BIASW])
        bias_row = sb("bias_row", [P, BIASW])
        rel = sb("rel", [P, L])
        causal = sb("causal", [P, P])
        att = sb("att", [P, 3, 2, 3 * P])
        att_z, att_g, att_r = (att[:, z] for z in range(3))

        w_b2 = sb("w_b2", [P, D])
        om = sb("om", [P, 8])
        wave = sb("wave", [P, 2, 8])

        w1_a = sb("w1_a", [P, E, FF])
        w2_a = sb("w2_a", [P, E, KF, D])
        w1_b = sb("w1_b", [P, E, FF])
        w2_b = sb("w2_b", [P, E, KF, D])
        b1_all = sb("b1_all", [P, E, FF])
        b2_all = sb("b2_all", [P, E, D])
        b1_cols = sb("b1_cols", [P, KF, E])
        idle = att[:].rearrange("p z u t -> p (z u t)")[:, 0:2 * KF * P].rearrange("p (k d) -> p k d", d=P)
        wave_a = w1_b[:].rearrange("p e f -> p (e f)")[:, 0:NB * 3 * P].rearrange("p (b t) -> p b t", b=NB)
        wave_b = w2_b[:].rearrange("p e k d -> p (e k d)")[:, 0:NB * 3 * P].rearrange("p (b t) -> p b t", b=NB)
        q_slab = w1_b[:].rearrange("p e f -> p (e f)")[:, 0:2 * 4 * L].rearrange("p (u h t) -> p u h t", u=2, h=4)
        k_slab = w2_b[:].rearrange("p e k d -> p (e k d)")[:, 0:2 * 4 * L].rearrange("p (u h t) -> p u h t", u=2, h=4)

        w5 = sb("w5", [P, E * 3 * P + 3 * FF])
        w12 = w5[:, 0:E * 2 * P].rearrange("p (e h) -> p e h", e=E)
        w3 = w5[:, E * 2 * P:E * 3 * P].rearrange("p (e d) -> p e d", e=E)
        w_s1, w_s2 = (w5[:, E * 3 * P + z * FF:E * 3 * P + (z + 1) * FF] for z in range(2))
        w_s3 = w5[:, E * 3 * P + 2 * FF:].rearrange("p (k d) -> p k d", k=KF)
        probs, probs_t = (w5[:, z * 2 * CH:(z + 1) * 2 * CH].rearrange("p (u t) -> p u t", u=2) for z in range(2))
        heads_t = w5[:, 4 * CH:6 * CH].rearrange("p (z t) -> p z t", z=2)
        v_seq = w5[:, 6 * CH:6 * CH + 4 * HEADS * (HD + 1)].rearrange("p (u t h d) -> p u t h d", u=2, t=2, h=HEADS)

        own6 = w1_b[:].rearrange("p e f -> p (e f)")[:, NB * 3 * P:]
        rope = own6.rearrange("p (z t) -> p z t", z=4)
        own6 = w2_b[:].rearrange("p e k d -> p (e k d)")[:, NB * 3 * P:]
        w_qkv, w_rot = own6[:, 0:3 * D], own6[:, 3 * D:5 * D]
        bv6, pb6, w_p6 = (own6[:, z * D:(z + 1) * D] for z in (5, 6, 7))
        b_qk = sb("b_qk", [P, 3])
        b_rot = sb("b_rot", [P, 2])
        pair_turn = sb("pair_turn", [P, P])
        low = sb("low", [P, 2, 2])
        inv_sum = sb("inv_sum", [P, 2, HEADS])
        wr = [sb(f"wr{n}", [P, E]) for n in range(4)]
        rbias = [None] + [sb(f"rbias{n}", [P, E]) for n in (1, 2, 3)]

        desc = sb("desc", [P, E])
        thr = sb("thr", [P, NTILE])
        tile_no = sb("tile_no", [1, 40])
        rt = sb("rt", [P, 24, E * NTILE])
        rs = sb("rs", [P, 24, NTILE])
        slot = sb("slot", [P, 2, NTILE], I32)
        eid_f = sb("eid_f", [1, 40, E])
        eid_s = sb("eid_s", [1, 40])
        eid = sb("eid", [1, 40], I32)

        xs = sb("xs", [P, 4, D])
        xst = sb("xst", [P, 2, P])
        hid = sb("hid", [P, 2, FF])
        hidt = sb("hidt", [P, 2, FF])
        ys = sb("ys", [P, 4, D])

        q_dram = nc.dram_tensor("q_dram", [D, T], F32, kind="Internal").ap()
        k_dram = nc.dram_tensor("k_dram", [D, T], F32, kind="Internal").ap()
        bias_dram = nc.dram_tensor("bias_dram", [P * BIASW], F32, kind="Internal").ap()
        sorted_x = nc.dram_tensor("sorted_x", [40 * P, D], F32, kind="Internal").ap()
        sorted_y = nc.dram_tensor("sorted_y", [40 * P, D], F32, kind="Internal").ap()

        def bank(n, lo=0, hi=CH):
            return psum[:, n, lo:hi]

        def tile_cols(i):
            return slice(i * P, (i + 1) * P)

        def chunk_cols(c):
            return slice(c * CH, (c + 1) * CH)

        def em(r):
            return rt[:, r, :].rearrange("p (e i) -> p e i", e=E)

        def by_tile(r):
            return rt[:, r, :].rearrange("p (e i) -> p i e", e=E)

        def over_e(ap):
            return ap.rearrange("p (o i) -> p o i", o=1).to_broadcast([P, E, NTILE])

        def over_i(ap):
            return ap.rearrange("p (e o) -> p e o", o=1).to_broadcast([P, E, NTILE])

        def x_rows(i):
            return x_sb[:, i, :]

        def x_chunk(c):
            return x_sb[:, TPC * c:TPC * (c + 1), :].rearrange("p i d -> p (i d)")

        x_flat = a["L0_attn_x"].rearrange("b l d -> (b l) d").rearrange("(i p) d -> p i d", p=P)
        out_flat = out.rearrange("b l d -> (b l) d").rearrange("(i p) d -> p i d", p=P)

        block = ctx.enter_context(nc.Block())

        class Chain:
            def __init__(self, eng, name):
                self.eng, self.sem, self.n = eng, S(name), 0

            def __call__(self, ins):
                ins.then_inc(self.sem, 1)
                self.n += 1

            def wait(self):
                self.eng.wait_ge(self.sem, self.n)

            def link(self, ins):
                self(ins)
                self.wait()

        def norm_no(n, tag):
            return n + 1 + (n > 0 or tag == "r")

        moe_cfg = {
            1: dict(k=2, w1=w1_a, w2=w2_a, bias=True, act=ACT.Relu, r=0),
            3: dict(k=1, w1=w1_b, w2=w2_b, bias=False, act=ACT.Gelu, r=1),
            7: dict(k=1, w1=w1_a, w2=w2_a, bias=True, act=ACT.Relu, r=3),
        }

        moe_cfg[1].update(t0=0, k0=0)
        moe_cfg[3].update(t0=moe_tiles(2), k0=2)
        moe_cfg[7].update(t0=moe_tiles(2) + moe_tiles(1), k0=3)

        def sp_moe(sp, n):
            nt, t0 = moe_tiles(moe_cfg[n]["k"]), moe_cfg[n]["t0"]

            def load(j, u):
                sp.dma_start(xs[:, u, :], sorted_x[bass.ds(j * P, P), :]).then_inc(S(f"xs_in{u}"), 16)

            def store(j, u):
                sp.wait_ge(S("moe_y_sb"), j + (t0 + 1))
                sp.dma_start(sorted_y[bass.ds(j * P, P), :], ys[:, u, :]).then_inc(S(f"y_out{u}"), 16)

            sp.wait_ge(S(f"scattered{n}"), 16 * NTILE * moe_cfg[n]["k"])
            for u in range(4):
                load(u, u)
            with sp.Fori(0, nt // 4 - 1) as g:
                for u in range(4):
                    store(g * 4 + u, u)
                    load(g * 4 + 4 + u, u)
            for u in range(4):
                store(nt - 4 + u, u)

        def sp_block6(sp):
            for c in range(NCH):
                sp.wait_ge(S("q6"), c + 1)
                sp.dma_start(q_dram[:, chunk_cols(c)], buf_a[:, chunk_cols(c)]).then_inc(S("qk_out"), 16)
                sp.wait_ge(S("k6"), c + 1)
                sp.dma_start(k_dram[:, chunk_cols(c)], buf_b[:, chunk_cols(c)]).then_inc(S("qk_out"), 16)

            def load(s, u):
                for slab, dram in ((q_slab, q_dram), (k_slab, k_dram)):
                    rows = dram[:, bass.ds(s * L, L)].rearrange("(g h d) t -> g d h t", g=4, d=HD)
                    for g in range(4):
                        sp.dma_start(slab[32 * g:32 * g + HD, u, :, :], rows[g]).then_inc(S(f"slab_in{u}"), 16)

            sp.wait_ge(S("qk_out"), 16 * 2 * NCH)
            load(0, 0)
            load(1, 1)
            with sp.Fori(1, NB // 2) as g:
                for u in range(2):
                    sp.wait_ge(S("s6"), g * (2 * HEADS) - (1 - u) * HEADS)
                    load(g * 2 + u, u)

        @block.sync
        def _(sp):
            for c in range(NCH):
                sp.dma_start(x_sb[:, TPC * c:TPC * (c + 1), :], x_flat[:, TPC * c:TPC * (c + 1), :])\
                    .then_inc(S(f"x_in{c}"), 16)
            for name, w in (("L0_attn_WqT", w_q), ("L0_attn_WvT", w_v), ("L0_attn_WgT", w_g), ("L0_attn_WoT", w_o)):
                sp.dma_start(w[:], a[name]).then_inc(S("w0_in"), 16)
            for col, name in enumerate(("L0_attn_ln_gamma", "L0_attn_ln_beta")):
                sp.dma_start(gb[:, col:col + 1], a[name].rearrange("(p o) -> p o", o=1)).then_inc(S("w0_in"), 16)
            sp.dma_start(wr[0][:], a["L0_ffn_Wg"]).then_inc(S("wr_in"), 16)
            sp.dma_start(wr[1][:], a["L1_ffn_Wr"]).then_inc(S("wr_in"), 16)
            sp.dma_start(wr[2][:], a["L2_ffn_router_wT"]).then_inc(S("wr_in"), 16)
            sp.dma_start(wr[3][:], a["L3_ffn_Wr"]).then_inc(S("wr_in"), 16)
            for n, name in ((1, "L1_ffn_br"), (2, "L2_ffn_expert_bias"), (3, "L3_ffn_br")):
                sp.dma_start(rbias[n][:], a[name].rearrange("(o e) -> o e", o=1).to_broadcast([P, E]))\
                    .then_inc(S("wr_in"), 16)
            sp.dma_start(w1_a[:], a["L0_ffn_W1"].rearrange("e p f -> p e f")).then_inc(S("w_moe1_in"), 16)
            sp.dma_start(w2_a[:], a["L0_ffn_W2"].rearrange("e (k p) d -> p e k d", p=P)).then_inc(S("w_moe1_in"), 16)
            sp.dma_start(b1_all[:], a["L0_ffn_b1"].rearrange("(o e) f -> o e f", o=1).to_broadcast([P, E, FF]))\
                .then_inc(S("w_moe1_in"), 16)
            sp.dma_start(b2_all[:], a["L0_ffn_b2"].rearrange("(o e) f -> o e f", o=1).to_broadcast([P, E, D]))\
                .then_inc(S("w_moe1_in"), 16)
            sp.dma_start(w_qk1[:], a["L1_attn_wqk"]).then_inc(S("w2_in"), 16)
            sp.dma_start(w_v1[:], a["L1_attn_wv"]).then_inc(S("w2_in"), 16)
            sp.dma_start(cols1[:, 0:1], a["L1_attn_bqk"].rearrange("(p o) -> p o", o=1)).then_inc(S("w2_in"), 16)
            sp.dma_start(cols1[:, 1:3], a["L1_attn_gammaT"]).then_inc(S("w2_in"), 16)
            sp.dma_start(cols1[:, 3:5], a["L1_attn_betaT"]).then_inc(S("w2_in"), 16)
            sp.dma_start(bv1[:], a["L1_attn_bv"].rearrange("(o d) -> o d", o=1).to_broadcast([P, D])).then_inc(S("w2_in"), 16)
            sp.dma_start(table[:], a["L1_attn_rel_bias"].rearrange("(b o) -> b o", o=1)).then_inc(S("w2_in"), 16)
            sp.dma_start(bucket[:], a["const_bucket"]).then_inc(S("w2_in"), 16)
            sp.dma_start(w1_b[:], a["L1_ffn_W1"].rearrange("e p f -> p e f")).then_inc(S("w_moe3_in"), 16)
            sp.dma_start(w2_b[:], a["L1_ffn_W2"].rearrange("e (k p) d -> p e k d", p=P)).then_inc(S("w_moe3_in"), 16)
            sp.dma_start(w_b2[:], a["L2_attn_B_weightT"]).then_inc(S("w4_in"), 16)
            sp.dma_start(om[:, 0:1], a["L2_attn_omega_raw"].rearrange("(p o) -> p o", o=1)).then_inc(S("w4_in"), 16)
            for dst, name in ((w12[:], "L2_ffn_w12T"), (w3[:], "L2_ffn_w3T"), (w_s1[:], "L2_ffn_shared_w1T"),
                              (w_s2[:], "L2_ffn_shared_w2T"),
                              (w_s3[:], a["L2_ffn_shared_w3T"].rearrange("(k p) d -> p k d", p=P))):
                sp.dma_start(dst, a[name] if isinstance(name, str) else name).then_inc(S("w5_in"), 16)
            sp.wait_ge(S("zeros"), 1)
            zeros = buf_c[:, 0:5 * D].rearrange("p (j d) -> p j d", d=D)
            for g in range(8):
                sp.dma_start(sorted_x[g * 5 * P:(g + 1) * 5 * P, :].rearrange("(j p) d -> p j d", p=P), zeros)\
                    .then_inc(S("zeroed"), 16)
            if STAGES > 2:
                sp.wait_ge(S("bias_row"), 1)
                sp.dma_start(bias_dram.rearrange("(p m) -> p m", m=BIASW), bias_row[:]).then_inc(S("bias_out"), 16)
                sp.wait_ge(S("bias_out"), 16)
                skew = bias_dram[P - 1:P - 1 + P * (BIASW - 1)].rearrange("(p m) -> p m", m=BIASW - 1)
                sp.dma_start(rel[:], skew[:, 0:L]).then_inc(S("rel_in"), 16)
            if STAGES > 1:
                sp_moe(sp, 1)
                for dst, src in ((w1_a[:], a["L3_ffn_W1"].rearrange("e p f -> p e f")),
                                 (w2_a[:], a["L3_ffn_W2"].rearrange("e (k p) d -> p e k d", p=P)),
                                 (b1_all[:], a["L3_ffn_b1"].rearrange("(o e) f -> o e f", o=1).to_broadcast([P, E, FF])),
                                 (b2_all[:], a["L3_ffn_b2"].rearrange("(o e) d -> o e d", o=1).to_broadcast([P, E, D])),
                                 (b1_cols[:], a["L3_ffn_b1T"].rearrange("(k p) e -> p k e", p=P))):
                    sp.dma_start(dst, src).then_inc(S("w_moe7_in"), 16)
            if STAGES > 3:
                sp_moe(sp, 3)
                for dst, src in ((w_qkv, a["L3_attn_qkv_wT"]), (b_qk[:], a["L3_attn_qkv_bT"]), (pair_turn[:], a["const_pair"]),
                                 (rope, a["const_rope"]),
                                 (bv6, a["L3_attn_qkv_b"][2 * D:3 * D].rearrange("(o d) -> o d", o=1).to_broadcast([P, D])),
                                 (pb6, a["L3_attn_proj_b"].rearrange("(o d) -> o d", o=1).to_broadcast([P, D])),
                                 (w_p6, a["L3_attn_proj_wT"])):
                    sp.dma_start(dst, src).then_inc(S("w6_in"), 16)
            if STAGES > 6:
                sp_block6(sp)
            if STAGES > 7:
                sp_moe(sp, 7)
            sp.wait_ge(S(f"x_done{STAGES - 1}"), NCH)
            sp.dma_start(out_flat, x_sb[:]).then_inc(S("stored"), 16)
            sp.wait_ge(S("stored"), 16)
            sp.wait_ge(S("zeroed"), 16 * 8)

        def pool_moe(gp, n):
            cfg = moe_cfg[n]
            for k in range(cfg["k"]):
                gp.wait_ge(S(f"slots{n}"), k + 1)
                for i in range(NTILE):
                    gp.indirect_dma_start(
                        out=sorted_x[:, :], out_offset=bass.IndirectOffsetOnAxis(ap=slot[:, k, i:i + 1], axis=0),
                        in_=xn[:, i, :], in_offset=None).then_inc(S(f"scattered{n}"), 16)
            nt, t0 = moe_tiles(cfg["k"]), cfg["t0"]
            for u in range(4):
                gp.wait_ge(S(f"y_out{u}"), (t0 + nt) * 4)
            for i in range(NTILE):
                for k in range(cfg["k"]):
                    dst = (buf_a, buf_b)[k]
                    gp.indirect_dma_start(
                        out=dst[:, tile_cols(i)], out_offset=None, in_=sorted_y[:, :],
                        in_offset=bass.IndirectOffsetOnAxis(ap=slot[:, k, i:i + 1], axis=0))\
                        .then_inc(S(f"back{i // TPC}"), 16)

        @block.gpsimd
        def _(gp):
            gp.memset(ident[:], 0.0).then_inc(S("consts"), 1)
            gp.memset(ones[:], 1.0).then_inc(S("consts"), 1)
            gp.memset(buf_c[:, 0:5 * D], 0.0).then_inc(S("zeros"), 1)
            gp.wait_ge(S("consts"), 2)
            gp.affine_select(out=ident[:], in_=ident[:], compare_op=ALU.not_equal, fill=1.0, base=0,
                             pattern=[[-1, P]], channel_multiplier=1).then_inc(S("consts"), 1)
            gp.affine_select(out=before[:], in_=ones[:], compare_op=ALU.is_gt, fill=0.0, base=0,
                             pattern=[[1, P]], channel_multiplier=-1).then_inc(S("consts"), 1)
            gp.affine_select(out=causal[:], in_=ones[:], compare_op=ALU.is_ge, fill=0.0, base=0,
                             pattern=[[1, P]], channel_multiplier=-1).then_inc(S("consts"), 1)
            gp.iota(desc[:], [[-1, E]], base=E, channel_multiplier=0, allow_small_or_imprecise_dtypes=True)\
                .then_inc(S("consts"), 1)
            gp.iota(thr[:], [[P, NTILE]], base=0, channel_multiplier=0, allow_small_or_imprecise_dtypes=True)\
                .then_inc(S("consts"), 1)
            gp.iota(tile_no[:], [[1, 40]], base=0, channel_multiplier=0, allow_small_or_imprecise_dtypes=True)\
                .then_inc(S("consts"), 1)
            gp.dma_start(lam_col[:, 0:1], a["L0_attn_beta"].rearrange("(h o) -> h o", o=1).to_broadcast([RH, D // RH]))\
                .then_inc(S("lam_in"), 16)
            gp.wait_ge(S("zeroed"), 16 * 8)
            if STAGES > 1:
                pool_moe(gp, 1)
            if STAGES > 3:
                pool_moe(gp, 3)
            if STAGES > 7:
                pool_moe(gp, 7)

        def act_norm(act, n, tag="x"):
            act.wait_ge(S("var"), norm_no(n, tag))
            act.activation(lnt[:, 7, :], lnt[:, 6, :], ACT.Sqrt).then_inc(S("sd"), 1)

        def act_xt(act, n, c):
            act.wait_ge(S("xt_ps"), NCH * n + c + 1)
            act.activation(xt[:, chunk_cols(c)], bank(c % 2), ACT.Copy).then_inc(S("xt"), 1)

        def act_block0(act):
            act_norm(act, 0)

            def silu(c):
                act.wait_ge(S("g_ps"), c + 1)
                act.activation(buf_a[:, chunk_cols(c)], bank(4), ACT.Silu).then_inc(S("gate"), 1)

            def ret_rows(c):
                act.wait_ge(S("ret_ps"), c + 1)
                act.activation(buf_c[:, chunk_cols(c)], bank(5), ACT.Copy).then_inc(S("ret_rows"), 1)

            act.wait_ge(S("zeroed"), 16 * 8)
            act_xt(act, 0, 0)
            for c in range(NCH):
                if c + 1 < NCH:
                    act_xt(act, 0, c + 1)
                silu(c)
                if c >= 1:
                    ret_rows(c - 1)
            ret_rows(NCH - 1)
            act_norm(act, 0, "r")
            for c in range(NCH):
                act.wait_ge(S("rn_ps"), c + 1)
                act.activation(buf_b[:, chunk_cols(c)], bank(c % 2), ACT.Identity, scale=gb[:, 0:1], bias=gb[:, 1:2])\
                    .then_inc(S("rn"), 1)

        def act_moe(act, n):
            cfg = moe_cfg[n]
            nt, t0 = moe_tiles(cfg["k"]), cfg["t0"]
            act_norm(act, n)
            for c in range(NCH):
                act_xt(act, n, c)
            if n == 1:
                act.wait_ge(S("gap1"), 1)
                act.activation(rs[:, 11, :], rs[:, 10, :], ACT.Exp).then_inc(S("gap_exp1"), 1)
            if n == 3:
                act.wait_ge(S("logits3"), 1)
                act.activation(rt[:, 0, :], rt[:, 7, :], ACT.Sigmoid).then_inc(S("scores3"), 1)

            def rows(j, u):
                act.wait_ge(S("moe_xst_ps"), j + (t0 + 1))
                if not (isinstance(j, int) and j < 2):
                    act.wait_ge(S("moe_h_ps"), j + (t0 - 1))
                act.activation(xst[:, u, :], bank(u, 0, P), ACT.Copy).then_inc(S("moe_xst"), 1)

            def hidden(j, u):
                act.wait_ge(S("moe_ht_ps"), j + (t0 + 1))
                if not (isinstance(j, int) and j < 2):
                    act.wait_ge(S("moe_y_ps"), j + (t0 - 1))
                act.activation(hidt[:, u, :], bank(4 + u), cfg["act"]).then_inc(S("moe_ht"), 1)

            rows(0, 0)
            rows(1, 1)

            def steps(g, last=False):
                for u in range(4):
                    j = g * 4 + u
                    hidden(j, u % 2)
                    if not (last and u >= 2):
                        rows(j + 2, u % 2)

            steps(0)
            with act.Fori(1, nt // 4 - 1) as g:
                steps(g)
            steps(nt // 4 - 1, last=True)

        def act_block2(act):
            act_norm(act, 2)

            def qk(c):
                if c >= 2:
                    act.wait_ge(S("k2"), c - 1)
                act.wait_ge(S("qk_ps2"), c + 1)
                act.activation(hid[:, c % 2, :], bank(2 + c % 2), ACT.Silu, bias=cols1[:, 0:1]).then_inc(S("qk2"), 1)

            def values(c):
                act.wait_ge(S("v_lin2"), c + 1)
                act.activation(buf_c[:, chunk_cols(c)], hidt[:, c % 2, :], ACT.Silu).then_inc(S("v2"), 1)

            act_xt(act, 2, 0)
            for c in range(NCH):
                if c + 1 < NCH:
                    act_xt(act, 2, c + 1)
                qk(c)
                if c >= 1:
                    values(c - 1)
            values(NCH - 1)
            for b in range(NB):
                if b >= 2:
                    act.wait_ge(S("phi2"), b - 1)
                act.wait_ge(S("z2"), b + 1)
                act.activation(att_g[:, b % 2, :], att_z[:, b % 2, :], ACT.Gelu).then_inc(S("gelu2"), 1)

        def act_block4(act):
            act.activation(om[:, 1:2], om[:, 0:1], ACT.Abs).then_inc(S("abs4"), 1)
            act.wait_ge(S("abs4"), 1)
            act.activation(om[:, 2:3], om[:, 1:2], ACT.Exp, scale=-1.0).then_inc(S("exp4"), 1)
            act.wait_ge(S("exp4"), 1)
            act.activation(om[:, 3:4], om[:, 2:3], ACT.Ln, bias=1.0).then_inc(S("ln4"), 1)
            act_norm(act, 4)
            act_xt(act, 4, 0)
            for c in range(NCH):
                if c + 1 < NCH:
                    act_xt(act, 4, c + 1)
                if c == 0:
                    act.wait_ge(S("pads4"), 2)
                act.wait_ge(S("force_ps4"), c + 1)
                act.activation(wave_a[:, 2 * c:2 * c + 2, P:], bank(2 + c % 2).rearrange("p (b t) -> p b t", t=L),
                               ACT.Copy, scale=float(np.float32(DT) ** 2)).then_inc(S("force4"), 1)

        def act_proj6(act):
            for c in range(NCH):
                act.wait_ge(S("ot_ps6"), c + 1)
                act.activation(buf_a[:, chunk_cols(c)], bank(c % 2), ACT.Copy).then_inc(S("ot6"), 1)

        def act_block5(act):
            act_norm(act, 5)
            for c in range(NCH):
                act_xt(act, 5, c)
            act.wait_ge(S("logit_ps"), 3)
            act.activation(em(0), bank(2, 0, NTILE * E).rearrange("p (i e) -> p e i", e=E), ACT.Sigmoid)\
                .then_inc(S("scores5"), 1)

            def chunk(c):
                for m in range(UNITS):
                    n, u = UNITS * c + m, m % 2
                    if not (isinstance(c, int) and n < 2):
                        act.wait_ge(S("h5"), n - 1)
                    act.wait_ge(S("up5"), n + 1)
                    act.activation(hid[:, u, :], bank(u), ACT.Silu).then_inc(S("silu5"), 1)

            chunk(0)
            with act.Fori(1, NCH) as c:
                chunk(c)

        def act_block6(act):
            act_norm(act, 6)

            for c in range(NCH):
                act_xt(act, 6, c)

            def steps(g, first=False):
                for i in range(2 * HEADS):
                    n = g * (2 * HEADS) + i
                    act.wait_ge(S("low6"), n + 1)
                    if not (first and i < 2):
                        act.wait_ge(S("t6"), n - 1)
                    for t in range(2):
                        last = act.activation(probs[:, i % 2, t * L:(t + 1) * L], bank(i % 2, t * L, (t + 1) * L), ACT.Exp,
                                              scale=-1.0, bias=low[:, i % 2, t:t + 1])
                    last.then_inc(S("exp6"), 1)
                    if i % 8 == 2 and not (first and i == 2):
                        s = g * 2 + (i - 10) // (2 * 8) if i > 2 else g * 2 - 1
                        evac(s, (i // 8 + 1) % 2, n - 2)

            def evac(s, half, heads):
                act.wait_ge(S("pv6"), heads)
                if not (isinstance(s, int) and s < 1):
                    act.wait_ge(S("tok6"), s)
                act.activation(heads_t[:, half, :], bank(4 + half), ACT.Copy).then_inc(S("heads6"), 1)

            steps(0, first=True)
            with act.Fori(1, NB // 2) as g:
                steps(g)
            evac(NB - 1, 1, NB * HEADS)

        @block.scalar
        def _(act):
            act.wait_ge(S("lam_in"), 16)
            act.activation(lam_col[:, 1:2], lam_col[:, 0:1], ACT.Exp, scale=-math.log(2.0)).then_inc(S("lam_exp"), 1)
            act_block0(act)
            if STAGES > 1:
                act_moe(act, 1)
            if STAGES > 2:
                act_block2(act)
            if STAGES > 3:
                act_moe(act, 3)
            if STAGES > 4:
                act_block4(act)
            if STAGES > 5:
                act_block5(act)
            if STAGES > 6:
                act_block6(act)
                act_proj6(act)
            if STAGES > 7:
                act_moe(act, 7)

        def pe_xt(pe, n, c):
            pe.wait_ge(S("xn"), NTILE * n + TPC * (c + 1))
            if c >= 2:
                pe.wait_ge(S("xt"), NCH * n + c - 1)
            for j in range(TPC):
                last = pe.transpose(bank(c % 2, j * P, (j + 1) * P), xn[:, TPC * c + j, :], ident[:])
            last.then_inc(S("xt_ps"), 1)

        def pe_block0(pe):
            pe.wait_ge(S("w0_in"), 16 * 6)

            def project(c):
                pe.wait_ge(S("xt"), NCH * 0 + c + 1)
                for w, b, used, done in ((w_v, 3, "state", "v_ps"), (w_q, 2, "ret", "q_ps"), (w_g, 4, "gate", "g_ps")):
                    if c >= 1:
                        pe.wait_ge(S(used), 2 * c if used == "state" else c)
                    pe.matmul(bank(b), w[:], xt[:, chunk_cols(c)], start=True, stop=True).then_inc(S(done), 1)

            def turn(c):
                pe.wait_ge(S("ret"), c + 1)
                if c >= 1:
                    pe.wait_ge(S("ret_rows"), c)
                for j in range(TPC):
                    last = pe.transpose(bank(5, j * P, (j + 1) * P), buf_b[:, tile_cols(TPC * c + j)], ident[:])
                last.then_inc(S("ret_ps"), 1)

            pe_xt(pe, 0, 0)
            for c in range(NCH):
                if c + 1 < NCH:
                    pe_xt(pe, 0, c + 1)
                project(c)
                if c >= 1:
                    turn(c - 1)
            turn(NCH - 1)
            def turn_back(c):
                pe.wait_ge(S("rn_rows"), TPC * (c + 1))
                if c >= 2:
                    pe.wait_ge(S("rn"), c - 1)
                for j in range(TPC):
                    last = pe.transpose(bank(c % 2, j * P, (j + 1) * P), xn[:, TPC * c + j, :], ident[:])
                last.then_inc(S("rn_ps"), 1)

            turn_back(0)
            for c in range(NCH):
                if c + 1 < NCH:
                    turn_back(c + 1)
                pe.wait_ge(S("gated"), c + 1)
                if c >= 2:
                    pe.wait_ge(S("x_done0"), c - 1)
                for j in range(TPC):
                    last = pe.matmul(bank(2 + c % 2, j * P, (j + 1) * P), buf_b[:, tile_cols(TPC * c + j)], w_o[:],
                                     start=True, stop=True)
                last.then_inc(S("o_ps"), 1)

        def pe_route(pe, n, w):
            if n == 1:
                pe.wait_ge(S("wr_in"), 16 * 7)
            pe_xt(pe, n, 0)
            for c in range(NCH):
                if c + 1 < NCH:
                    pe_xt(pe, n, c + 1)
                pe.wait_ge(S("xt"), NCH * n + c + 1)
                for i in range(TPC * c, TPC * (c + 1)):
                    last = pe.matmul(bank(2, i * E, (i + 1) * E), xt[:, tile_cols(i)], w[:], start=True, stop=True)
            last.then_inc(S("logit_ps"), 1)

        def pe_moe(pe, n):
            cfg = moe_cfg[n]
            nt, t0 = moe_tiles(cfg["k"]), cfg["t0"]
            w1, w2 = cfg["w1"], cfg["w2"]
            pe_route(pe, n, wr[cfg["r"]])
            pe.wait_ge(S(f"chosen{n}"), 1)
            pe.matmul(bank(3, 0, P), before[:], rt[:, 3, :], start=True, stop=True)
            pe.matmul(bank(3, P, 2 * P), ones[:], rt[:, 3, :], start=True, stop=True).then_inc(S(f"rank_ps{n}"), 1)
            pe.wait_ge(S(f"eid{n}"), 1)
            pe.wait_ge(S(f"w_moe{n}_in"), 16 * {1: 4, 3: 2, 7: 5}[n])

            def turn_rows(g, u4, u):
                pe.wait_ge(S(f"xs_in{u4}"), g * 16 + (t0 * 4 + 16))
                pe.transpose(bank(u, 0, P), xs[:, u4, :], ident[:]).then_inc(S("moe_xst_ps"), 1)

            def up(j, u):
                e = pe.value_load(eid[0:1, bass.ds(j, 1)], min_val=0, max_val=E - 1)
                pe.wait_ge(S("moe_xst"), j + (t0 + 1))
                pe.matmul(bank(2 + u), xst[:, u, :], w1[:, bass.ds(e, 1), :], start=True, stop=True)\
                    .then_inc(S("moe_h_ps"), 1)

            def turn_hidden(j, u):
                pe.wait_ge(S("moe_h"), j + (t0 + 1))
                if not (isinstance(j, int) and j < 2):
                    pe.wait_ge(S("moe_ht"), j + (t0 - 1))
                for k in range(KF):
                    last = pe.transpose(bank(4 + u, k * P, (k + 1) * P), hid[:, u, k * P:(k + 1) * P], ident[:])
                last.then_inc(S("moe_ht_ps"), 1)

            def down(j, u):
                e = pe.value_load(eid[0:1, bass.ds(j, 1)], min_val=0, max_val=E - 1)
                if not (isinstance(j, int) and j < 2):
                    pe.wait_ge(S("moe_y_sb"), j + (t0 - 1))
                pe.wait_ge(S("moe_ht"), j + (t0 + 1))
                for k in range(KF):
                    last = pe.matmul(bank(6 + u, 0, D), hidt[:, u, k * P:(k + 1) * P], w2[:, bass.ds(e, 1), k, :],
                                     start=(k == 0), stop=(k == KF - 1))
                last.then_inc(S("moe_y_ps"), 1)

            turn_rows(0, 0, 0)
            turn_rows(0, 1, 1)
            up(0, 0)

            def steps(g, last=False):
                for u in range(4):
                    j = g * 4 + u
                    turn_hidden(j, u % 2)
                    if not (last and u == 3):
                        up(j + 1, (u + 1) % 2)
                    down(j, u % 2)
                    if not (last and u >= 2):
                        turn_rows(g + (u + 2) // 4, (u + 2) % 4, u % 2)

            steps(0)
            with pe.Fori(1, nt // 4 - 1) as g:
                steps(g)
            steps(nt // 4 - 1, last=True)

        def pe_rel_bias(pe):
            pe.wait_ge(S("table"), 1)
            pe.matmul(bank(7, 0, BIASW), table_all[:], bucket[:], start=True, stop=True).then_inc(S("bias_ps"), 1)

        def pe_block2(pe):
            pe_xt(pe, 2, 0)
            for c in range(NCH):
                if c + 1 < NCH:
                    pe_xt(pe, 2, c + 1)
                pe.wait_ge(S("xt"), NCH * 2 + c + 1)
                if c >= 2:
                    pe.wait_ge(S("qk2"), c - 1)
                pe.matmul(bank(2 + c % 2), w_qk1[:], xt[:, chunk_cols(c)], start=True, stop=True).then_inc(S("qk_ps2"), 1)
                if c >= 2:
                    pe.wait_ge(S("v_lin2"), c - 1)
                for j in range(TPC):
                    last = pe.matmul(bank(4 + c % 2, j * P, (j + 1) * P), xt[:, tile_cols(TPC * c + j)], w_v1[:],
                                     start=True, stop=True)
                last.then_inc(S("v_ps2"), 1)

            def scores(b):
                if b >= 2:
                    pe.wait_ge(S("z2"), b - 1)
                pe.wait_ge(S("k2"), b // 2 + 1)
                t0 = b * L
                pe.matmul(bank(6 + b % 2, 0, L), buf_b[:, t0:t0 + P], buf_a[:, t0:t0 + L], start=True, stop=True)
                pe.matmul(bank(6 + b % 2, L, L + P), buf_b[:, t0 + P:t0 + L], buf_a[:, t0 + P:t0 + L],
                          start=True, stop=True).then_inc(S("s_ps2"), 1)

            scores(0)
            for b in range(NB):
                if b + 1 < NB:
                    scores(b + 1)
                pe.wait_ge(S("v2"), b // 2 + 1)
                if b >= 2:
                    pe.wait_ge(S("x_add2"), b - 1)
                pe.wait_ge(S("phi2"), b + 1)
                i = 2 * b
                o = 2 + b % 2
                pe.matmul(bank(o, 0, P), att_z[:, b % 2, 0:P], buf_c[:, tile_cols(i)], start=True, stop=True)
                pe.matmul(bank(o, P, 2 * P), att_z[:, b % 2, P:2 * P], buf_c[:, tile_cols(i)], start=True, stop=False)
                pe.matmul(bank(o, P, 2 * P), att_z[:, b % 2, 2 * P:3 * P], buf_c[:, tile_cols(i + 1)],
                          start=False, stop=True).then_inc(S("o_ps2"), 1)

        def pe_block4(pe):
            pe_xt(pe, 4, 0)
            for c in range(NCH):
                if c + 1 < NCH:
                    pe_xt(pe, 4, c + 1)
                pe.wait_ge(S("xt"), NCH * 4 + c + 1)
                if c >= 2:
                    pe.wait_ge(S("force4"), c - 1)
                pe.matmul(bank(2 + c % 2), w_b2[:], xt[:, chunk_cols(c)], start=True, stop=True).then_inc(S("force_ps4"), 1)
            for c in range(NCH):
                pe.wait_ge(S("solved4"), c // 2 + 1)
                for j in range(TPC):
                    b, h = 2 * c + j // 2, j % 2
                    last = pe.transpose(bank(4 + c, j * P, (j + 1) * P), wave_b[:, b, (1 + h) * P:(2 + h) * P], ident[:])
                last.then_inc(S("v_ps4"), 1)

        def pe_block5(pe):
            pe_route(pe, 5, wr[2])
            pe.wait_ge(S("w5_in"), 16 * 5)
            pe.wait_ge(S("scores5"), 1)

            def up(c, m):
                n, u = UNITS * c + m, m % 2
                if not (isinstance(c, int) and n < 2):
                    pe.wait_ge(S("h5"), n - 1)
                wa = w_s1[:, tile_cols(m)] if m < KF else w12[:, m - KF, 0:P]
                wb = w_s2[:, tile_cols(m)] if m < KF else w12[:, m - KF, P:2 * P]
                rhs = xt[:, bass.ds(c * CH, CH)]
                pe.matmul(bank(u), wa, rhs, start=True, stop=True)
                pe.matmul(bank(4 + u), wb, rhs, start=True, stop=True).then_inc(S("up5"), 1)

            def down(c, m):
                n, u, e = UNITS * c + m, m % 2, m - KF
                first = isinstance(c, int) and c == 0
                if m == 0 and not first:
                    pe.wait_ge(S("acc5"), (E + 1) * c)
                if e >= 2:
                    pe.wait_ge(S("acc5"), (E + 1) * c + e)
                pe.wait_ge(S("h5"), n + 1)
                for j in range(TPC):
                    if m < KF:
                        last = pe.matmul(bank(3, j * P, (j + 1) * P), hidt[:, u, tile_cols(j)], w_s3[:, m, :],
                                         start=(m == 0 and j == 0), stop=(m == KF - 1), skip_group_check=True)
                    else:
                        last = pe.matmul(bank(6 + e % 2, j * P, (j + 1) * P), hidt[:, u, tile_cols(j)], w3[:, e, :],
                                         start=True, stop=True)
                last.then_inc(S("down5"), 1)

            def chunk(c):
                up(c, 0)
                for m in range(UNITS):
                    if m + 1 < UNITS:
                        up(c, m + 1)
                    down(c, m)

            chunk(0)
            with pe.Fori(1, NCH) as c:
                chunk(c)

        def pe_offsets(pe):
            pe.wait_ge(S("w_moe7_in"), 16 * 5)
            for e in range(E):
                pe.wait_ge(S("idle"), e + 1)
                for k in range(KF):
                    last = pe.matmul(bank(6 + e // 4, (e % 4) * P, (e % 4 + 1) * P), idle[:, (e % 2) * KF + k, :],
                                     w2_a[:, e, k, :], start=(k == 0), stop=(k == KF - 1))
                last.then_inc(S("idle_ps"), 1)

        def pe_block6(pe):
            pe.wait_ge(S("w_rot"), 2)
            pe.wait_ge(S("w6_in"), 16 * 7)
            pe.matmul(bank(7, 0, 2), pair_turn[:], b_qk[:, 0:2], start=True, stop=True).then_inc(S("b_rot_ps"), 1)
            pe_xt(pe, 6, 0)
            for c in range(NCH):
                if c + 1 < NCH:
                    pe_xt(pe, 6, c + 1)
                pe.wait_ge(S("xt"), NCH * 6 + c + 1)
                for b, w, free in ((2, w_qkv[:, 0:D], "q6"), (3, w_rot[:, 0:D], "q6"),
                                   (4, w_qkv[:, D:2 * D], "k6"), (5, w_rot[:, D:2 * D], "k6")):
                    if c >= 1:
                        pe.wait_ge(S(free), c)
                    pe.matmul(bank(b), w, xt[:, chunk_cols(c)], start=True, stop=True).then_inc(S("qk_ps6"), 1)
                if c >= 1:
                    pe.wait_ge(S("v6"), c)
                for j in range(TPC):
                    last = pe.matmul(bank(6, j * P, (j + 1) * P), xt[:, tile_cols(TPC * c + j)], w_qkv[:, 2 * D:3 * D],
                                     start=True, stop=True)
                last.then_inc(S("v_ps6"), 1)
            pe.wait_ge(S("v6"), NCH)

            def score(g, i, skip=False):
                g, i = (g + 1, i - 2 * HEADS) if i >= 2 * HEADS else (g, i)
                n, u, h = g * (2 * HEADS) + i, i // HEADS, i % HEADS
                r = slice(32 * (h // 4), 32 * (h // 4) + HD)
                if h == 0:
                    pe.wait_ge(S(f"slab_in{u}"), g * 128 + 128)
                if not (isinstance(n, int) and n < 2):
                    pe.wait_ge(S("exp6"), n - 1)
                for t in range(2):
                    last = pe.matmul(bank(i % 2, t * L, (t + 1) * L), q_slab[r, u, h % 4, t * P:(t + 1) * P],
                                     k_slab[r, u, h % 4, :], start=True, stop=True, tile_position=(32 * (h // 4), 0))
                last.then_inc(S("s6"), 1)

            def turn(g, i):
                g, i = (g + 1, i - 2 * HEADS) if i >= 2 * HEADS else (g, i)
                n = g * (2 * HEADS) + i
                pe.wait_ge(S("exp6"), n + 1)
                if not (isinstance(n, int) and n < 2):
                    pe.wait_ge(S("pt6"), n - 1)
                for t in range(2):
                    for kt in range(2):
                        last = pe.transpose(bank(2 + i % 2, kt * L + t * P, kt * L + (t + 1) * P),
                                            probs[:, i % 2, t * L + kt * P:t * L + (kt + 1) * P], ident[:])
                last.then_inc(S("t6"), 1)

            def weigh(g, i):
                n, u, h = g * (2 * HEADS) + i, i // HEADS, i % HEADS
                s = g * 2 + u
                if h == 0:
                    pe.wait_ge(S("v_seq6"), s + 1)
                if h % 8 == 0 and not (isinstance(s, int) and s == 0):
                    pe.wait_ge(S("heads6"), s * 2 - 1 + h // 8)
                pe.wait_ge(S("pt6"), n + 1)
                for kt in range(2):
                    last = pe.matmul(psum[32 * (h % 4):32 * (h % 4) + HD + 1, 4 + h // 8,
                                          (h // 4 % 2) * L:(h // 4 % 2 + 1) * L],
                                     v_seq[:, u, kt, h, :], probs_t[:, i % 2, kt * L:(kt + 1) * L],
                                     start=(kt == 0), stop=(kt == 1), tile_position=(0, 32 * (h % 4)))
                last.then_inc(S("pv6"), 1)

            def back(s):
                pe.wait_ge(S("heads6"), s * 2 + 2)
                if not (isinstance(s, int) and s < 1):
                    pe.wait_ge(S("o6"), s)
                for t in range(2):
                    for g4 in range(4):
                        last = pe.transpose(bank(6 + t, g4 * P, (g4 + 1) * P),
                                            heads_t[:, g4 // 2, (g4 % 2) * L + t * P:(g4 % 2) * L + (t + 1) * P], ident[:])
                last.then_inc(S("tok6"), 1)

            pe.wait_ge(S("clear6"), 2)
            score(0, 0)
            score(0, 1)
            turn(0, 0)

            def steps(g, last=False):
                for i in range(2 * HEADS):
                    if not (last and i + 2 >= 2 * HEADS):
                        score(g, i + 2)
                    if not (last and i + 1 >= 2 * HEADS):
                        turn(g, i + 1)
                    weigh(g, i)
                    if i == 5 and not (isinstance(g, int) and g == 0):
                        back(g * 2 - 1)
                    if i == HEADS + 5:
                        back(g * 2)

            steps(0)
            with pe.Fori(1, NB // 2 - 1) as g:
                steps(g)
            steps(NB // 2 - 1, last=True)
            back(NB - 1)

            for c in range(NCH):
                pe.wait_ge(S("o6"), 2 * c + 2)
                if c >= 2:
                    pe.wait_ge(S("ot6"), c - 1)
                for j in range(TPC):
                    last = pe.transpose(bank(c % 2, j * P, (j + 1) * P), xn[:, TPC * c + j, :], ident[:])
                last.then_inc(S("ot_ps6"), 1)
                pe.wait_ge(S("ot6"), c + 1)
                if c >= 2:
                    pe.wait_ge(S("x_done6"), c - 1)
                for j in range(TPC):
                    last = pe.matmul(bank(2 + c % 2, j * P, (j + 1) * P), buf_a[:, tile_cols(TPC * c + j)], w_p6,
                                     start=True, stop=True)
                last.then_inc(S("proj_ps6"), 1)

        @block.tensor
        def _(pe):
            pe.wait_ge(S("consts"), 8)
            if STAGES > 2:
                pe_rel_bias(pe)
            pe_block0(pe)
            if STAGES > 1:
                pe_moe(pe, 1)
            if STAGES > 2:
                pe_block2(pe)
            if STAGES > 3:
                pe_moe(pe, 3)
            if STAGES > 4:
                pe_block4(pe)
            if STAGES > 7:
                pe_offsets(pe)
            if STAGES > 5:
                pe_block5(pe)
            if STAGES > 6:
                pe_block6(pe)
            if STAGES > 7:
                pe_moe(pe, 7)

        def dve_stats(v, ch, n, c, dst, src):
            for i in range(TPC * c, TPC * (c + 1)):
                last = v.bn_stats(dst[:, i, :], src(i))
            ch(last)

        def dve_var(v, ch, n, st, tag="x"):
            ch.wait()
            me, mo, qe, qo = st[:, :, 1], st[:, :, 4], st[:, :, 2], st[:, :, 5]
            ch(v.tensor_tensor(lnt[:, 1, :], me, mo, ALU.add))
            ch(v.tensor_tensor(lnt[:, 2, :], me, mo, ALU.subtract))
            ch.link(v.tensor_tensor(lnt[:, 3, :], qe, qo, ALU.add))
            ch(v.tensor_scalar(lnt[:, 0, :], lnt[:, 1, :], 0.5, None, ALU.mult))
            ch.link(v.tensor_tensor(lnt[:, 4, :], lnt[:, 2, :], lnt[:, 2, :], ALU.mult))
            ch.link(v.scalar_tensor_tensor(out=lnt[:, 2, :], in0=lnt[:, 4, :], scalar=D / 4.0, in1=lnt[:, 3, :],
                                           op0=ALU.mult, op1=ALU.add))
            v.tensor_scalar(lnt[:, 6, :], lnt[:, 2, :], 1.0 / D, EPS, ALU.mult, ALU.add).then_inc(S("var"), 1)
            v.wait_ge(S("sd"), norm_no(n, tag))
            ch.link(v.reciprocal(lnt[:, 5, :], lnt[:, 7, :]))

        def dve_norm(v, ch, n, src, done):
            for i in range(NTILE):
                v.tensor_scalar(xn[:, i, :], src(i), lnt[:, 0, i:i + 1], lnt[:, 5, i:i + 1], ALU.subtract, ALU.mult)\
                    .then_inc(S(done), 1)

        def dve_block0(v, ch):
            v.wait_ge(S("lam_exp"), 1)
            ch.link(v.tensor_scalar(lam_col[:, 2:3], lam_col[:, 1:2], -1.0, 1.0, ALU.mult, ALU.add))
            ch.link(v.tensor_scalar(lam_col[:, 3:4], lam_col[:, 2:3], float(np.finfo(np.float32).tiny),
                                    float(np.float32(1.0 - 1e-9)), ALU.max, ALU.min))
            v.wait_ge(S("consts"), 8)
            for r in range(L // P):
                ch(v.tensor_scalar(lam[:, tile_cols(r)], ones[:], lam_col[:, 3:4], None, ALU.mult))
            for c in range(NCH):
                v.wait_ge(S(f"x_in{c}"), 16)
                dve_stats(v, ch, 0, c, stats, x_rows)
            dve_var(v, ch, 0, stats)
            dve_norm(v, ch, 0, x_rows, "xn")
            for c in range(NCH):
                v.wait_ge(S("v_ps"), c + 1)
                if c >= 1:
                    v.wait_ge(S("ret"), c)
                for s in range(CH // L):
                    v.tensor_tensor_scan(state[:, s * L:(s + 1) * L], lam[:],
                                         bank(3, s * L, (s + 1) * L), 0.0, ALU.mult, ALU.add).then_inc(S("state"), 1)
                v.wait_ge(S("state"), 2 * c + 2)
                v.wait_ge(S("q_ps"), c + 1)
                v.tensor_tensor(buf_b[:, chunk_cols(c)], state[:], bank(2), ALU.mult).then_inc(S("ret"), 1)
                if c >= 1:
                    v.wait_ge(S("ret_rows"), c)
                    dve_stats(v, ch, 0, c - 1, stats2, lambda i: buf_c[:, tile_cols(i)])
            v.wait_ge(S("ret_rows"), NCH)
            dve_stats(v, ch, 0, NCH - 1, stats2, lambda i: buf_c[:, tile_cols(i)])
            dve_var(v, ch, 0, stats2, "r")
            dve_norm(v, ch, 0, lambda i: buf_c[:, tile_cols(i)], "rn_rows")
            def finish(c):
                v.wait_ge(S("o_ps"), c + 1)
                v.tensor_tensor(x_chunk(c), x_chunk(c), bank(2 + c % 2), ALU.add).then_inc(S("x_done0"), 1)
                v.wait_ge(S("x_done0"), c + 1)
                dve_stats(v, ch, 1, c, stats, x_rows)

            for c in range(NCH):
                v.wait_ge(S("rn"), c + 1)
                v.wait_ge(S("gate"), c + 1)
                v.tensor_tensor(buf_b[:, chunk_cols(c)], buf_b[:, chunk_cols(c)], buf_a[:, chunk_cols(c)], ALU.mult)\
                    .then_inc(S("gated"), 1)
                if c >= 1:
                    finish(c - 1)
            finish(NCH - 1)

        def dve_choose(v, ch, logits, best, top, one_hot):
            ch.link(v.tensor_reduce(rs[:, best, :], by_tile(logits), AX.X, ALU.max))
            ch.link(v.tensor_tensor(em(6), em(logits), over_e(rs[:, best, :]), ALU.is_equal))
            ch.link(v.tensor_tensor(em(6), em(6), over_i(desc[:]), ALU.mult))
            ch.link(v.tensor_reduce(rs[:, top, :], by_tile(6), AX.X, ALU.max))
            ch.link(v.tensor_tensor(em(one_hot), over_i(desc[:]), over_e(rs[:, top, :]), ALU.is_equal))

        def dve_slots(v, ch, n, k):
            nt = moe_tiles(k)
            v.wait_ge(S(f"rank_ps{n}"), 1)
            counts = bank(3, P, 2 * P)
            ch(v.tensor_tensor_scan(rt[:, 8, :], ones[:], counts, 0.0, ALU.mult, ALU.add))
            ch.link(v.tensor_reduce(rs[:, 4, 0:E], counts.rearrange("p (e i) -> p e i", e=E), AX.X, ALU.add))
            ch(v.tensor_tensor(em(9), over_i(rs[:, 4, 0:E]), over_e(thr[:]), ALU.is_gt))
            ch.link(v.tensor_tensor_scan(rs[:, 5, 0:E], ones[:, 0:E], rs[:, 4, 0:E], 0.0, ALU.mult, ALU.add))
            ch(v.tensor_tensor(rs[:, 5, 8:16], rs[:, 5, 0:E], rs[:, 4, 0:E], ALU.subtract))
            ch.link(v.tensor_reduce(rs[:, 6, 0:E], em(9), AX.X, ALU.add))
            ch.link(v.tensor_tensor_scan(rs[:, 7, 0:E], ones[:, 0:E], rs[:, 6, 0:E], 0.0, ALU.mult, ALU.add))
            ch(v.tensor_tensor(rs[:, 8, 0:E], rs[:, 7, 0:E], rs[:, 6, 0:E], ALU.subtract))
            ends = rs[0:1, 7, 0:E].rearrange("p (o e) -> p o e", o=1).to_broadcast([1, nt, E])
            nos = tile_no[:, 0:nt].rearrange("p (j o) -> p j o", o=1).to_broadcast([1, nt, E])
            ch.link(v.tensor_tensor(eid_f[:, 0:nt, :], ends, nos, ALU.is_le))
            ch.link(v.tensor_reduce(eid_s[:, 0:nt], eid_f[:, 0:nt, :], AX.X, ALU.add))
            v.tensor_scalar(eid[:, 0:nt], eid_s[:, 0:nt], float(E - 1), None, ALU.min).then_inc(S(f"eid{n}"), 1)
            ch(v.scalar_tensor_tensor(out=rs[:, 9, 0:E], in0=rs[:, 8, 0:E], scalar=float(P), in1=rs[:, 5, 8:16],
                                      op0=ALU.mult, op1=ALU.subtract))
            ch.link(v.tensor_tensor(em(9), em(8), counts.rearrange("p (e i) -> p e i", e=E), ALU.subtract))
            ch.link(v.tensor_tensor(em(8), em(9), over_i(rs[:, 9, 0:E]), ALU.add))
            ch.link(v.tensor_tensor(rt[:, 9, :], rt[:, 8, :], bank(3, 0, P), ALU.add))
            for c in range(k):
                ch.link(v.tensor_tensor(rt[:, 8, :], rt[:, 9, :], rt[:, 1 + c, :] if k > 1 else rt[:, 3, :], ALU.mult))
                ch.link(v.tensor_reduce(rs[:, 13, :], by_tile(8), AX.X, ALU.add))
                v.tensor_copy(slot[:, c, :], rs[:, 13, :]).then_inc(S(f"slots{n}"), 1)
            v.wait_ge(S(f"slots{n}"), k)
            v.wait_ge(S(f"eid{n}"), 1)

        def dve_moe(v, ch, n):
            cfg = moe_cfg[n]
            k, nt, k0, t0 = cfg["k"], moe_tiles(cfg["k"]), cfg["k0"], cfg["t0"]
            dve_var(v, ch, n, stats)
            dve_norm(v, ch, n, x_rows, "xn")
            v.wait_ge(S("logit_ps"), (n + 1) // 2)
            logits_ps = bank(2, 0, NTILE * E).rearrange("p (i e) -> p e i", e=E)
            if n == 7:
                ch.link(v.tensor_tensor(em(0), logits_ps, over_i(rbias[3][:]), ALU.add))
                dve_choose(v, ch, 0, 0, 1, 3)
                v.sem_inc(S(f"chosen{n}"), 1)
            elif n == 1:
                ch.link(v.tensor_copy(em(0), logits_ps))
                dve_choose(v, ch, 0, 0, 1, 1)
                ch.link(v.scalar_tensor_tensor(out=em(5), in0=em(1), scalar=NEG, in1=em(0), op0=ALU.mult, op1=ALU.add))
                dve_choose(v, ch, 5, 2, 3, 2)
                v.tensor_tensor(rt[:, 3, :], rt[:, 1, :], rt[:, 2, :], ALU.add).then_inc(S(f"chosen{n}"), 1)
                v.tensor_tensor(rs[:, 10, :], rs[:, 2, :], rs[:, 0, :], ALU.subtract).then_inc(S("gap1"), 1)
            elif n == 3:
                v.tensor_tensor(em(7), logits_ps, over_i(rbias[1][:]), ALU.add).then_inc(S("logits3"), 1)
                v.wait_ge(S("scores3"), 1)
                dve_choose(v, ch, 0, 14, 1, 3)
                ch(v.tensor_copy(rs[:, 15, :], rs[:, 14, :]))
                ch.wait()
                v.sem_inc(S(f"chosen{n}"), 1)
            dve_slots(v, ch, n, k)
            if n == 1:
                v.wait_ge(S("gap_exp1"), 1)
                ch.link(v.tensor_scalar(rs[:, 12, :], rs[:, 11, :], 1.0, None, ALU.add))
                ch.link(v.reciprocal(rs[:, 14, :], rs[:, 12, :]))
                ch.link(v.tensor_tensor(rs[:, 15, :], rs[:, 11, :], rs[:, 14, :], ALU.mult))

            def hidden(j, u):
                if cfg["bias"]:
                    e = v.value_load(eid[0:1, bass.ds(j, 1)], min_val=0, max_val=E - 1)
                if not (isinstance(j, int) and j < 2):
                    v.wait_ge(S("moe_ht_ps"), j + (t0 - 1))
                v.wait_ge(S("moe_h_ps"), j + (t0 + 1))
                if cfg["bias"]:
                    ins = v.tensor_tensor(hid[:, u, :], bank(2 + u), b1_all[:, bass.ds(e, 1), :], ALU.add)
                else:
                    ins = v.tensor_copy(hid[:, u, :], bank(2 + u))
                ins.then_inc(S("moe_h"), 1)

            def result(g, j, u4):
                if cfg["bias"]:
                    e = v.value_load(eid[0:1, bass.ds(j, 1)], min_val=0, max_val=E - 1)
                if not isinstance(g, int) or g > 0:
                    v.wait_ge(S(f"y_out{u4}"), g * 16 + t0 * 4)
                v.wait_ge(S("moe_y_ps"), j + (t0 + 1))
                if cfg["bias"]:
                    ins = v.tensor_tensor(ys[:, u4, :], bank(6 + u4 % 2, 0, D), b2_all[:, bass.ds(e, 1), :], ALU.add)
                else:
                    ins = v.tensor_copy(ys[:, u4, :], bank(6 + u4 % 2, 0, D))
                ins.then_inc(S("moe_y_sb"), 1)

            hidden(0, 0)

            def steps(g, last=False):
                for u in range(4):
                    if not (last and u == 3):
                        hidden(g * 4 + u + 1, (u + 1) % 2)
                    result(g, g * 4 + u, u)

            steps(0)
            with v.Fori(1, nt // 4 - 1) as g:
                steps(g)
            steps(nt // 4 - 1, last=True)

            for c in range(NCH):
                v.wait_ge(S(f"back{c}"), 16 * TPC * (k0 + k))
                for kk in range(k):
                    for i in range(TPC * c, TPC * (c + 1)):
                        back = (buf_a, buf_b)[kk][:, tile_cols(i)]
                        if n == 7:
                            ch(v.tensor_tensor(x_sb[:, i, :], x_sb[:, i, :], back, ALU.add))
                        else:
                            ch(v.scalar_tensor_tensor(out=x_sb[:, i, :], in0=back, scalar=rs[:, 14 + kk, i:i + 1],
                                                      in1=x_sb[:, i, :], op0=ALU.mult, op1=ALU.add))
                    ch.wait()
                v.sem_inc(S(f"x_done{n}"), 1)
                if n < 7:
                    dve_stats(v, ch, n + 1, c, stats, x_rows)

        def dve_rel_bias(v, ch):
            v.wait_ge(S("w2_in"), 16 * 8)
            v.wait_ge(S("consts"), 8)
            v.tensor_scalar(table_all[:], ones[0:NBUCKET, :], table[:, 0:1], None, ALU.mult).then_inc(S("table"), 1)
            v.wait_ge(S("bias_ps"), 1)
            v.tensor_scalar(bias_row[:], bank(7, 0, BIASW), math.sqrt(D) / STD, -MU / STD, ALU.mult, ALU.add)\
                .then_inc(S("bias_row"), 1)

        def dve_block2(v, ch):
            dve_var(v, ch, 2, stats)
            dve_norm(v, ch, 2, x_rows, "xn")
            for c in range(NCH):
                if c >= 2:
                    v.wait_ge(S("v2"), c - 1)
                v.wait_ge(S("v_ps2"), c + 1)
                v.tensor_tensor(hidt[:, c % 2, :].rearrange("p (i d) -> p i d", d=D),
                                bank(4 + c % 2).rearrange("p (i d) -> p i d", d=D),
                                bv1[:].rearrange("p (o d) -> p o d", o=1).to_broadcast([P, TPC, D]), ALU.add)\
                    .then_inc(S("v_lin2"), 1)
                v.wait_ge(S("qk2"), c + 1)
                v.tensor_scalar(buf_a[:, chunk_cols(c)], hid[:, c % 2, :], cols1[:, 1:2], cols1[:, 3:4], ALU.mult, ALU.add)\
                    .then_inc(S("k2_q"), 1)
                v.wait_ge(S("k2_q"), c + 1)
                v.tensor_scalar(buf_b[:, chunk_cols(c)], hid[:, c % 2, :], cols1[:, 2:3], cols1[:, 4:5], ALU.mult, ALU.add)\
                    .then_inc(S("k2"), 1)

            v.wait_ge(S("rel_in"), 16)

            def zed(b):
                u = b % 2
                if b >= 2:
                    v.wait_ge(S("o_ps2"), b - 1)
                v.wait_ge(S("s_ps2"), b + 1)
                scale = 1.0 / L / STD
                ch(v.scalar_tensor_tensor(out=att_z[:, u, 0:L], in0=bank(6 + u, 0, L), scalar=scale, in1=rel[:],
                                          op0=ALU.mult, op1=ALU.add))
                ch.link(v.scalar_tensor_tensor(out=att_z[:, u, L:L + P], in0=bank(6 + u, L, L + P), scalar=scale,
                                               in1=rel[:, 0:P], op0=ALU.mult, op1=ALU.add))
                v.tensor_scalar(att_z[:, u, :], att_z[:, u, :], TINY, None, ALU.add).then_inc(S("z2"), 1)
                v.wait_ge(S("z2"), b + 1)
                ch.link(v.reciprocal(att_r[:, u, :], att_z[:, u, :]))
                ch.link(v.tensor_tensor(att_r[:, u, 0:P], att_r[:, u, 0:P], causal[:], ALU.mult))
                ch.link(v.tensor_tensor(att_r[:, u, L:L + P], att_r[:, u, L:L + P], causal[:], ALU.mult))

            def phi(b):
                u = b % 2
                v.wait_ge(S("gelu2"), b + 1)
                v.tensor_tensor(att_z[:, u, :], att_g[:, u, :], att_r[:, u, :], ALU.mult).then_inc(S("phi2"), 1)

            def add(b):
                v.wait_ge(S("o_ps2"), b + 1)
                rows = x_sb[:, 2 * b:2 * b + 2, :].rearrange("p i d -> p (i d)")
                v.tensor_tensor(rows, rows, bank(2 + b % 2, 0, 2 * P), ALU.add).then_inc(S("x_add2"), 1)
                if b % 2:
                    v.wait_ge(S("x_add2"), b + 1)
                    v.sem_inc(S("x_done2"), 1)
                    dve_stats(v, ch, 3, b // 2, stats, x_rows)

            zed(0)
            phi(0)
            for b in range(NB):
                if b + 1 < NB:
                    zed(b + 1)
                    phi(b + 1)
                add(b)


        def dve_block4(v, ch):
            v.wait_ge(S("ln4"), 1)
            ch.link(v.tensor_scalar(om[:, 4:5], om[:, 0:1], 0.0, None, ALU.max))
            ch.link(v.tensor_tensor(om[:, 5:6], om[:, 4:5], om[:, 3:4], ALU.add))
            ch.link(v.tensor_scalar(wave[:, 0, 0:1], om[:, 5:6], float(np.float32(DT) ** 2) / 2, None, ALU.mult))
            for k in range(8):
                d = wave[:, 0, k:k + 1]
                ch.link(v.tensor_scalar(wave[:, 1, k:k + 1], d, -2.0, 2.0, ALU.mult, ALU.add))
                if k < 7:
                    ch.link(v.tensor_scalar(om[:, 6:7], d, -2.0, 4.0, ALU.mult, ALU.add))
                    ch.link(v.tensor_tensor(wave[:, 0, k + 1:k + 2], d, om[:, 6:7], ALU.mult))
            v.memset(wave_a[:, :, 0:P], 0.0).then_inc(S("pads4"), 1)
            v.memset(wave_b[:, :, 0:P], 0.0).then_inc(S("pads4"), 1)
            dve_var(v, ch, 4, stats)
            dve_norm(v, ch, 4, x_rows, "xn")
            src, dst = wave_a, wave_b
            NH = NB // 2
            marks = [0, 0]

            def step(h, ins):
                ch(ins)
                marks[h] = ch.n

            for k in range(7):
                s_ = 1 << k
                two_c = wave[:, 1, k:k + 1]
                for part in range(2):
                    for h in range(2):
                        q = slice(NH * h, NH * (h + 1))
                        if k == 0 and part == 0:
                            v.wait_ge(S("force4"), 2 * h + 2)
                        else:
                            v.wait_ge(S("dve_steps"), marks[h])
                        if part == 0:
                            step(h, v.scalar_tensor_tensor(out=dst[:, q, P:], in0=src[:, q, P - s_:3 * P - s_], scalar=two_c,
                                                           in1=src[:, q, P:], op0=ALU.mult, op1=ALU.add))
                        else:
                            lo = P if s_ < P // 2 else 2 * P
                            step(h, v.tensor_tensor(dst[:, q, lo:], dst[:, q, lo:], src[:, q, lo - 2 * s_:3 * P - 2 * s_],
                                                    ALU.add))
                src, dst = dst, src
            for h in range(2):
                q = slice(NH * h, NH * (h + 1))
                v.wait_ge(S("dve_steps"), marks[h])
                v.scalar_tensor_tensor(out=src[:, q, 2 * P:], in0=src[:, q, P:2 * P], scalar=wave[:, 1, 7:8],
                                       in1=src[:, q, 2 * P:], op0=ALU.mult, op1=ALU.add).then_inc(S("solved4"), 1)
            assert src is wave_b
            for c in range(NCH):
                v.wait_ge(S("v_ps4"), c + 1)
                v.tensor_tensor(x_chunk(c), x_chunk(c), bank(4 + c), ALU.add).then_inc(S("x_done4"), 1)
                v.wait_ge(S("x_done4"), c + 1)
                dve_stats(v, ch, 5, c, stats, x_rows)

        def dve_offsets(v, ch):
            v.wait_ge(S("w_moe7_in"), 16 * 5)
            for e in range(E):
                if e >= 2:
                    v.wait_ge(S("idle_ps"), e - 1)
                for k in range(KF):
                    last = v.tensor_scalar(idle[:, (e % 2) * KF + k, :], ones[:], b1_cols[:, k, e:e + 1], 0.0,
                                           ALU.mult, ALU.max)
                    ch(last)
                ch.wait()
                v.sem_inc(S("idle"), 1)
            v.wait_ge(S("idle_ps"), E)
            total = idle[:, 0, :]
            by_expert = psum[:, 6:8, :].rearrange("p b (e d) -> p d (b e)", e=4)
            ch(v.tensor_reduce(total, by_expert, AX.X, ALU.add))
            ch(v.tensor_reduce(idle[:, 1, :], b2_all[:].rearrange("p e d -> p d e"), AX.X, ALU.add))
            ch.wait()
            ch.link(v.tensor_tensor(idle[:, 2, :], total, idle[:, 1, :], ALU.add))
            for half in range(2):
                ch(v.tensor_tensor(b2_all[:, 4 * half:4 * half + 4, :],
                                   idle[:, 2:3, :].to_broadcast([P, 4, D]),
                                   bank(6 + half).rearrange("p (e d) -> p e d", e=4), ALU.subtract))
            ch.wait()
            v.sem_inc(S("offsets"), 1)

        def dve_block5(v, ch):
            dve_var(v, ch, 5, stats)
            dve_norm(v, ch, 5, x_rows, "xn")
            v.wait_ge(S("scores5"), 1)
            ch.link(v.tensor_tensor(em(7), em(0), over_i(rbias[2][:]), ALU.add))
            dve_choose(v, ch, 7, 0, 1, 1)
            ch.link(v.scalar_tensor_tensor(out=em(5), in0=em(1), scalar=NEG, in1=em(7), op0=ALU.mult, op1=ALU.add))
            dve_choose(v, ch, 5, 2, 3, 2)
            ch.link(v.tensor_tensor(rt[:, 9, :], rt[:, 1, :], rt[:, 2, :], ALU.add))
            ch.link(v.tensor_tensor(rt[:, 10, :], rt[:, 0, :], rt[:, 9, :], ALU.mult))

            def product(c, m):
                n, u = c * UNITS + m, m % 2
                v.wait_ge(S("silu5"), n + 1)
                if not (isinstance(n, int) and n < 2):
                    v.wait_ge(S("down5"), n - 1)
                v.tensor_tensor(hidt[:, u, :], hid[:, u, :], bank(4 + u), ALU.mult).then_inc(S("h5"), 1)

            def add(c, m):
                n = c * UNITS + m
                v.wait_ge(S("down5"), n + 1)
                if not (isinstance(c, int) and c == 0 and m < KF):
                    v.wait_ge(S("acc5"), c * (E + 1) + (m - KF + 1 if m >= KF else 0))
                rows = x_sb[:, bass.ds(c * TPC, TPC), :]
                if m < KF:
                    v.tensor_tensor(rows, rows, bank(3).rearrange("p (i d) -> p i d", d=D), ALU.add)\
                        .then_inc(S("acc5"), 1)
                    return
                e = m - KF
                for j in range(TPC):
                    row = x_sb[:, bass.ds(c * TPC + j, 1), :].rearrange("p o d -> p (o d)")
                    last = v.scalar_tensor_tensor(out=row, in0=bank(6 + e % 2, j * P, (j + 1) * P),
                                                  scalar=rt[:, 10, bass.ds(c * TPC + (e * NTILE + j), 1)],
                                                  in1=row, op0=ALU.mult, op1=ALU.add)
                last.then_inc(S("acc5"), 1)

            def chunk(c):
                for m in range(UNITS):
                    product(c, m)
                    if m > KF - 1 and m - 1 >= KF - 1:
                        add(c, m - 1)
                add(c, UNITS - 1)

            chunk(0)
            with v.Fori(1, NCH) as c:
                chunk(c)
            v.wait_ge(S("acc5"), NCH * (E + 1))
            v.sem_inc(S("x_done5"), NCH)
            for c in range(NCH):
                dve_stats(v, ch, 6, c, stats, x_rows)

        def dve_block6(v, ch):
            v.wait_ge(S("w6_in"), 16 * 7)
            pairs = w_qkv[:, 0:2 * D].rearrange("p (i z) -> p z i", z=2)
            turned = w_rot.rearrange("p (i z) -> p z i", z=2)
            v.tensor_scalar(turned[:, 0, :], pairs[:, 1, :], -1.0, None, ALU.mult).then_inc(S("w_rot"), 1)
            v.tensor_copy(turned[:, 1, :], pairs[:, 0, :]).then_inc(S("w_rot"), 1)
            dve_var(v, ch, 6, stats)
            dve_norm(v, ch, 6, x_rows, "xn")
            v.wait_ge(S("b_rot_ps"), 1)
            v.tensor_copy(b_rot[:], bank(7, 0, 2)).then_inc(S("b_rot"), 1)
            v.wait_ge(S("b_rot"), 1)
            both = [P, 2, L]

            def two(ap):
                return ap.rearrange("p (b t) -> p b t", t=L)

            for c in range(NCH):
                for z, dst, done in ((0, buf_a, "q6"), (1, buf_b, "k6")):
                    v.wait_ge(S("qk_ps6"), 4 * c + 2 * z + 2)
                    cos, sin = (rope[:, 2 * z + y:2 * z + y + 1, :].to_broadcast(both) for y in range(2))
                    ch(v.scalar_tensor_tensor(out=two(hid[:, z, :]), in0=two(bank(2 + 2 * z)), scalar=b_qk[:, z:z + 1],
                                              in1=cos, op0=ALU.add, op1=ALU.mult))
                    ch(v.scalar_tensor_tensor(out=two(hidt[:, z, :]), in0=two(bank(3 + 2 * z)), scalar=b_rot[:, z:z + 1],
                                              in1=sin, op0=ALU.add, op1=ALU.mult))
                    ch.wait()
                    v.tensor_tensor(dst[:, chunk_cols(c)], hid[:, z, :], hidt[:, z, :], ALU.add).then_inc(S(done), 1)
                    v.wait_ge(S(done), c + 1)
                v.wait_ge(S("v_ps6"), c + 1)
                v.tensor_tensor(buf_c[:, chunk_cols(c)].rearrange("p (i d) -> p i d", d=D),
                                bank(6).rearrange("p (i d) -> p i d", d=D),
                                bv6.rearrange("p (o d) -> p o d", o=1).to_broadcast([P, TPC, D]), ALU.add)\
                    .then_inc(S("v6"), 1)
            v.wait_ge(S("v6"), NCH)
            for z in range(2):
                v.memset(bank(4 + z), 0.0).then_inc(S("clear6"), 1)
            v.memset(v_seq.rearrange("p u t h d -> p (u t h d)"), 1.0).then_inc(S("v_ones"), 1)
            v.wait_ge(S("v_ones"), 1)

            def values(g, u):
                s = g * 2 + u
                if not (isinstance(s, int) and s < 2):
                    v.wait_ge(S("pv6"), s * HEADS - HEADS)
                for t in range(2):
                    last = v.tensor_scalar(v_seq[:, u, t, :, 0:HD],
                                           buf_c[:, bass.ds(s * L + t * P, P)].rearrange("p (h d) -> p h d", h=HEADS),
                                           ones[:, 0:1], None, ALU.mult)
                last.then_inc(S("v_seq6"), 1)

            def lows(g, i):
                g, i = (g + 1, i - 2 * HEADS) if i >= 2 * HEADS else (g, i)
                n = g * (2 * HEADS) + i
                if not (isinstance(n, int) and n < 2):
                    v.wait_ge(S("exp6"), n - 1)
                v.wait_ge(S("s6"), n + 1)
                v.tensor_reduce(low[:, i % 2, :], bank(i % 2).rearrange("p (t k) -> p t k", t=2), AX.X, ALU.min)\
                    .then_inc(S("low6"), 1)

            def weights(g, i):
                n = g * (2 * HEADS) + i
                v.wait_ge(S("t6"), n + 1)
                if not (isinstance(n, int) and n < 2):
                    v.wait_ge(S("pv6"), n - 1)
                v.tensor_copy(probs_t[:, i % 2, :], bank(2 + i % 2)).then_inc(S("pt6"), 1)

            def divide(s):
                v.wait_ge(S("tok6"), s + 1)
                v.reciprocal(inv_sum[:], psum[:, 6:8, HD::32]).then_inc(S("inv6"), 1)
                v.wait_ge(S("inv6"), s + 1)
                for t in range(2):
                    last = v.tensor_tensor(xn[:, bass.ds(s * 2 + t, 1), :].rearrange("p o (h d) -> p (o h) d", h=HEADS),
                                           bank(6 + t).rearrange("p (h z) -> p h z", z=32)[:, :, 0:HD],
                                           inv_sum[:, t, :].rearrange("p (h o) -> p h o", o=1).to_broadcast([P, HEADS, HD]),
                                           ALU.mult)
                last.then_inc(S("o6"), 1)

            values(0, 0)
            values(0, 1)
            lows(0, 0)

            def steps(g, last=False):
                for i in range(2 * HEADS):
                    if not (last and i + 1 >= 2 * HEADS):
                        lows(g, i + 1)
                    weights(g, i)
                    if i == 6 and not (isinstance(g, int) and g == 0):
                        divide(g * 2 - 1)
                    if i == HEADS + 6:
                        divide(g * 2)
                    if i == HEADS + 1 and not last:
                        values(g + 1, 0)
                    if i == 1 and not (isinstance(g, int) and g == 0):
                        values(g, 1)

            steps(0)
            with v.Fori(1, NB // 2 - 1) as g:
                steps(g)
            steps(NB // 2 - 1, last=True)
            divide(NB - 1)
            for c in range(NCH):
                v.wait_ge(S("proj_ps6"), c + 1)
                ch.link(v.tensor_tensor(x_chunk(c), x_chunk(c), bank(2 + c % 2), ALU.add))
                rows = x_sb[:, TPC * c:TPC * (c + 1), :]
                v.tensor_tensor(rows, rows, pb6.rearrange("p (o d) -> p o d", o=1).to_broadcast([P, TPC, D]), ALU.add)\
                    .then_inc(S("x_done6"), 1)
                v.wait_ge(S("x_done6"), c + 1)
                dve_stats(v, ch, 7, c, stats, x_rows)

        @block.vector
        def _(v):
            ch = Chain(v, "dve_steps")
            if STAGES > 2:
                dve_rel_bias(v, ch)
            dve_block0(v, ch)
            if STAGES > 1:
                dve_moe(v, ch, 1)
            if STAGES > 2:
                dve_block2(v, ch)
            if STAGES > 3:
                dve_moe(v, ch, 3)
            if STAGES > 4:
                dve_block4(v, ch)
            if STAGES > 7:
                dve_offsets(v, ch)
            if STAGES > 5:
                dve_block5(v, ch)
            if STAGES > 6:
                dve_block6(v, ch)
            if STAGES > 7:
                dve_moe(v, ch, 7)


_SHAPE = (NB, L, D)
_T = {"L0_attn_Wq", "L0_attn_Wv", "L0_attn_Wg", "L0_attn_Wo", "L2_ffn_router_w", "L2_attn_B_weight",
      "L1_attn_gamma", "L1_attn_beta", "L2_ffn_shared_w1", "L2_ffn_shared_w2", "L2_ffn_shared_w3",
      "L3_attn_qkv_w", "L3_attn_proj_w"}


def kernel(**inputs):
    import concourse.bacc as _bacc
    from concourse.bass_utils import run_bass_kernel_spmd as _run

    data = {(name + "T" if name in _T else name): (value.T if name in _T else value) for name, value in inputs.items()}
    data.update(const_bucket=bucket_rows(), const_pair=pair_matrix(), const_rope=rope_tables())
    if "L2_ffn_w12" in inputs:
        data["L2_ffn_w12T"] = inputs["L2_ffn_w12"].transpose(2, 0, 1)
        data["L2_ffn_w3T"] = inputs["L2_ffn_w3"].transpose(2, 0, 1)
    if "L3_attn_qkv_b" in inputs:
        data["L3_ffn_b1T"] = inputs["L3_ffn_b1"].T
        data["L3_attn_qkv_bT"] = inputs["L3_attn_qkv_b"].reshape(3, D).T
    nc = _bacc.Bacc("TRN2", target_bir_lowering=False, num_devices=1)
    arrays, aps = {}, {}
    for name, value in data.items():
        value = np.ascontiguousarray(value)
        arrays[f"in_{name}"] = value
        aps[name] = nc.dram_tensor(f"in_{name}", value.shape, mybir.dt.from_np(value.dtype), kind="ExternalInput").ap()
    out = nc.dram_tensor("out_x", _SHAPE, F32, kind="ExternalOutput").ap()
    build(nc, aps, out)
    r = _run(nc, [arrays], core_ids=[0])
    return r.results[0]["out_x"]
```

```python
from contextlib import ExitStack
import math

import numpy as np

import concourse.bass as bass
from concourse import mybir

F32 = mybir.dt.float32
BF16 = mybir.dt.bfloat16
I32 = mybir.dt.int32
ALU = mybir.AluOpType
ACT = mybir.ActivationFunctionType
AX = mybir.AxisListType

P = 128
D = 128
NB, L = 8, 256
T = NB * L
NTILE = T // P
CH = 512
NCH = T // CH
TPC = CH // P
E = 8
FF = 512
KF = FF // P
EPS = 1e-5
NEG = -3.0e38
HEADS, HD = 16, 8
Q_TERMS = (0, 0, 1, 1, 0, 2)
K_TERMS = (0, 1, 0, 1, 2, 0)
UNITS = KF + E
RH = 16
DT = 0.1

NBUCKET, MAX_DISTANCE = 32, 128
BIASW = 3 * P
ROUND128 = 1.5 * 2.0 ** 30
MU, STD = math.sqrt(0.5), math.sqrt(0.25 * math.pi)
TINY = 1e-30

STAGES = 8


def rope_tables():
    inv = 1.0 / 10000.0 ** (np.arange(0, HD, 2, dtype=np.float32) / HD)
    ang = np.arange(L, dtype=np.float32)[None, :] * np.concatenate([inv, inv]).astype(np.float32)[:, None]
    cos, sin = (np.tile(f(ang).astype(np.float32), (HEADS, 1)) for f in (np.cos, np.sin))
    scale = np.float32(HD ** -0.5)
    return np.ascontiguousarray(np.stack([-cos * scale, -sin * scale, cos, sin], axis=1))


def pair_matrix():
    m = np.zeros((P, P), np.float32)
    for i in range(0, P, 2):
        m[i + 1, i], m[i, i + 1] = -1.0, 1.0
    return m


def bucket_rows():
    n = np.maximum(np.arange(BIASW) - (P - 1), 0)
    exact = NBUCKET // 2
    ratio = (np.log(np.maximum(n, 1).astype(np.float32) / np.float32(exact))
             / np.float32(math.log(MAX_DISTANCE / exact)) * np.float32(NBUCKET - exact))
    large = np.minimum(exact + ratio.astype(np.int32), NBUCKET - 1)
    b = np.where(n < exact, n, large)
    return (b[None, :] == np.arange(NBUCKET)[:, None]).astype(np.float32)


def moe_tiles(k):
    n = k * T // P + E
    return (n + 3) // 4 * 4


def build(nc, a, out):
    ctx = ExitStack()

    def sb(name, shape, dt=F32):
        return ctx.enter_context(nc.sbuf_tensor(name, shape, dt))

    sems = {}

    def S(name):
        if name not in sems:
            sems[name] = ctx.enter_context(nc.semaphore(name))
        return sems[name]

    with ctx:
        x_sb = sb("x_sb", [P, NTILE, D])
        xn = sb("xn", [P, NTILE, D])
        xt = sb("xt", [P, T])
        buf_a = sb("buf_a", [P, T])
        buf_b = sb("buf_b", [P, T])
        buf_c = sb("buf_c", [P, T])
        ident = sb("ident", [P, P])
        ones = sb("ones", [P, P])
        before = sb("before", [P, P])
        stats = sb("stats", [P, NTILE, 6])
        stats2 = sb("stats2", [P, NTILE, 6])
        lnt = sb("lnt", [P, 8, NTILE])
        psum = ctx.enter_context(nc.psum_tensor("psum", [P, 8, CH], F32))

        w_q = sb("w_q", [P, D])
        w_v = sb("w_v", [P, D])
        w_g = sb("w_g", [P, D])
        w_o = sb("w_o", [P, D])
        state = sb("state", [P, CH])
        lam_col = sb("lam_col", [P, 4])
        lam = sb("lam", [P, L])
        gb = sb("gb", [P, 2])

        w_qk1 = sb("w_qk1", [P, D])
        w_v1 = sb("w_v1", [P, D])
        cols1 = sb("cols1", [P, 5])
        bv1 = sb("bv1", [P, D])
        table = sb("table", [NBUCKET, 1])
        table_all = sb("table_all", [NBUCKET, P])
        bucket = sb("bucket", [NBUCKET, BIASW])
        bias_row = sb("bias_row", [P, BIASW])
        rel = sb("rel", [P, L])
        causal = sb("causal", [P, P])
        att = sb("att", [P, 3, 2, 3 * P])
        att_z, att_g, att_r = (att[:, z] for z in range(3))

        w_b2 = sb("w_b2", [P, D])
        om = sb("om", [P, 8])
        wave = sb("wave", [P, 2, 8])

        w1_a = sb("w1_a", [P, E, FF])
        w2_a = sb("w2_a", [P, E, KF, D])
        w1_b = sb("w1_b", [P, E, FF])
        w2_b = sb("w2_b", [P, E, KF, D])
        b1_all = sb("b1_all", [P, E, FF])
        b2_all = sb("b2_all", [P, E, D])
        b1_cols = sb("b1_cols", [P, KF, E])
        idle = att[:].rearrange("p z u t -> p (z u t)")[:, 0:2 * KF * P].rearrange("p (k d) -> p k d", d=P)
        wave_a = w1_b[:].rearrange("p e f -> p (e f)")[:, 0:NB * 3 * P].rearrange("p (b t) -> p b t", b=NB)
        wave_b = w2_b[:].rearrange("p e k d -> p (e k d)")[:, 0:NB * 3 * P].rearrange("p (b t) -> p b t", b=NB)
        q_slab = w1_b[:].rearrange("p e f -> p (e f)").bitcast(BF16).rearrange("p (u h t) -> p u h t", u=2, h=HEADS)
        k_slab = w2_b[:].rearrange("p e k d -> p (e k d)").bitcast(BF16).rearrange("p (u h t) -> p u h t", u=2, h=HEADS)
        q_parts = [buf[:].bitcast(BF16)[:, T * z:T * (z + 1)] for buf, z in ((buf_a, 0), (buf_a, 1), (buf_b, 0))]
        k_parts = [buf[:].bitcast(BF16)[:, T * z:T * (z + 1)] for buf, z in ((buf_b, 1), (buf_c, 0), (buf_c, 1))]

        w5 = sb("w5", [P, E * 3 * P + 3 * FF])
        w12 = w5[:, 0:E * 2 * P].rearrange("p (e h) -> p e h", e=E)
        w3 = w5[:, E * 2 * P:E * 3 * P].rearrange("p (e d) -> p e d", e=E)
        w_s1, w_s2 = (w5[:, E * 3 * P + z * FF:E * 3 * P + (z + 1) * FF] for z in range(2))
        w_s3 = w5[:, E * 3 * P + 2 * FF:].rearrange("p (k d) -> p k d", k=KF)
        probs_t = w5[:, 0:2 * CH].rearrange("p (u t) -> p u t", u=2)
        heads_t = w5[:, 4 * CH:6 * CH].rearrange("p (z t) -> p z t", z=2)
        v_seq = w5[:, 6 * CH:6 * CH + 4 * HEADS * (HD + 1)].rearrange("p (u t h d) -> p u t h d", u=2, t=2, h=HEADS)

        own6 = att[:].rearrange("p z u t -> p (z u t)")
        rope = own6[:, 0:4 * L].rearrange("p (z t) -> p z t", z=4)
        own6 = own6[:, 4 * L:4 * L + 8 * D]
        w_qkv, w_rot = own6[:, 0:3 * D], own6[:, 3 * D:5 * D]
        bv6, pb6, w_p6 = (own6[:, z * D:(z + 1) * D] for z in (5, 6, 7))
        b_qk = sb("b_qk", [P, 3])
        b_rot = sb("b_rot", [P, 2])
        pair_turn = sb("pair_turn", [P, P])
        low = sb("low", [P, 4, 2])
        inv_sum = sb("inv_sum", [P, HEADS])
        wr = [sb(f"wr{n}", [P, E]) for n in range(4)]
        rbias = [None] + [sb(f"rbias{n}", [P, E]) for n in (1, 2, 3)]

        desc = sb("desc", [P, E])
        thr = sb("thr", [P, 40])
        col_no = sb("col_no", [P, P])
        row_no = sb("row_no", [P, 1])
        tile_seq = sb("tile_seq", [P, 2 * NTILE])
        past = sb("past", [P, 40])
        tile_no = sb("tile_no", [1, 40])
        rt = sb("rt", [P, 24, E * NTILE])
        rs = sb("rs", [P, 24, NTILE])
        row_f = sb("row_f", [P, 4, 40])
        row_in = sb("row_in", [P, 40], I32)
        row_out = sb("row_out", [P, 40], I32)
        place_hot = buf_c[:].bitcast(BF16).rearrange("p (i s) -> p i s", s=P)
        tile_hot = xt[:].bitcast(BF16)[:, 0:3 * 2 * NTILE * 40].rearrange("p (z i j) -> p z i j", z=3, j=40)
        eid_f = sb("eid_f", [1, 40, E])
        eid_s = sb("eid_s", [1, 40])
        eid = sb("eid", [1, 40], I32)

        xs = sb("xs", [P, 4, D])
        xst = sb("xst", [P, 2, P])
        hid = sb("hid", [P, 2, FF])
        hidt = sb("hidt", [P, 2, FF])
        ys = sb("ys", [P, 4, D])

        def probs(i):
            return (hid, hidt)[i // 2 % 2][:, i % 2, :]

        q_dram = nc.dram_tensor("q_dram", [3, D, T], BF16, kind="Internal").ap()
        k_dram = nc.dram_tensor("k_dram", [3, D, T], BF16, kind="Internal").ap()
        bias_dram = nc.dram_tensor("bias_dram", [P * BIASW], F32, kind="Internal").ap()
        x_rows_dram = nc.dram_tensor("x_rows_dram", [P + T, D], F32, kind="Internal").ap()
        y_rows = nc.dram_tensor("y_rows", [P + 2 * T + 4 * P, D], F32, kind="Internal").ap()

        def bank(n, lo=0, hi=CH):
            return psum[:, n, lo:hi]

        def tile_cols(i):
            return slice(i * P, (i + 1) * P)

        def chunk_cols(c):
            return slice(c * CH, (c + 1) * CH)

        def em(r):
            return rt[:, r, :].rearrange("p (e i) -> p e i", e=E)

        def by_tile(r):
            return rt[:, r, :].rearrange("p (e i) -> p i e", e=E)

        def over_e(ap):
            return ap.rearrange("p (o i) -> p o i", o=1).to_broadcast([P, E, NTILE])

        def over_i(ap):
            return ap.rearrange("p (e o) -> p e o", o=1).to_broadcast([P, E, NTILE])

        def x_rows(i):
            return x_sb[:, i, :]

        def x_chunk(c):
            return x_sb[:, TPC * c:TPC * (c + 1), :].rearrange("p i d -> p (i d)")

        x_flat = a["L0_attn_x"].rearrange("b l d -> (b l) d").rearrange("(i p) d -> p i d", p=P)
        out_flat = out.rearrange("b l d -> (b l) d").rearrange("(i p) d -> p i d", p=P)

        CONSTS = 12

        block = ctx.enter_context(nc.Block())

        class Chain:
            def __init__(self, eng, name):
                self.eng, self.sem, self.n = eng, S(name), 0

            def __call__(self, ins):
                ins.then_inc(self.sem, 1)
                self.n += 1

            def wait(self):
                self.eng.wait_ge(self.sem, self.n)

            def link(self, ins):
                self(ins)
                self.wait()

        def norm_no(n, tag):
            return n + 1 + (n > 0 or tag == "r")

        moe_cfg = {
            1: dict(k=2, w1=w1_a, w2=w2_a, bias=True, act=ACT.Relu, r=0),
            3: dict(k=1, w1=w1_b, w2=w2_b, bias=False, act=ACT.Gelu, r=1),
            7: dict(k=1, w1=w1_a, w2=w2_a, bias=True, act=ACT.Relu, r=3),
        }

        moe_cfg[1].update(order=1, t0=0, k0=0)
        moe_cfg[3].update(order=2, t0=moe_tiles(2), k0=2)
        moe_cfg[7].update(order=3, t0=moe_tiles(2) + moe_tiles(1), k0=3)

        def sp_moe(sp, n):
            k, k0, nt, t0 = moe_cfg[n]["k"], moe_cfg[n]["k0"], moe_tiles(moe_cfg[n]["k"]), moe_cfg[n]["t0"]

            for c in range(NCH):
                sp.wait_ge(S("xn"), NTILE * n + TPC * (c + 1))
                sp.dma_start(x_rows_dram[P + c * CH:P + (c + 1) * CH, :].rearrange("(i p) d -> p i d", p=P),
                             xn[:, TPC * c:TPC * (c + 1), :]).then_inc(S("x_out"), 16)
            for u in range(4):
                sp.wait_ge(S(f"y_out{u}"), (t0 + nt) * 4)
            for c in range(NCH):
                for kk in range(k):
                    dst = (buf_a, buf_b)[kk][:, chunk_cols(c)].rearrange("p (i d) -> p i d", d=D)
                    src = y_rows[P + kk * T + c * CH:P + kk * T + (c + 1) * CH, :].rearrange("(i p) d -> p i d", p=P)
                    sp.dma_start(dst, src).then_inc(S(f"back{c}"), 16)

        def sp_block6(sp):
            def leave(c):
                for name, parts, dram in (("q6", q_parts, q_dram), ("k6", k_parts, k_dram)):
                    sp.wait_ge(S(name), c + 1)
                    for part in range(3):
                        sp.dma_start(dram[part, :, chunk_cols(c)], parts[part][:, chunk_cols(c)]).then_inc(S("qk_out"), 16)

            def load(s, u):
                for slab, dram, terms in ((q_slab, q_dram, Q_TERMS), (k_slab, k_dram, K_TERMS)):
                    for t, part in enumerate(terms):
                        sp.dma_start(slab[HD * t:HD * (t + 1), u, :, :],
                                     dram[part][:, bass.ds(s * L, L)].rearrange("(h d) t -> d h t", d=HD))\
                            .then_inc(S(f"slab_in{u}"), 16)

            leave(0)
            sp.wait_ge(S("slab_zero"), 2)
            sp.wait_ge(S("qk_out"), 16 * 6)
            load(0, 0)
            load(1, 1)
            for c in range(1, NCH):
                leave(c)
            sp.wait_ge(S("qk_out"), 16 * 6 * NCH)
            with sp.Fori(1, NB // 2) as g:
                for u in range(2):
                    sp.wait_ge(S("s6"), g * (2 * HEADS) - (1 - u) * HEADS)
                    load(g * 2 + u, u)

        @block.sync
        def _(sp):
            for c in range(NCH):
                sp.dma_start(x_sb[:, TPC * c:TPC * (c + 1), :], x_flat[:, TPC * c:TPC * (c + 1), :])\
                    .then_inc(S(f"x_in{c}"), 16)
            for name, w in (("L0_attn_WqT", w_q), ("L0_attn_WvT", w_v), ("L0_attn_WgT", w_g), ("L0_attn_WoT", w_o)):
                sp.dma_start(w[:], a[name]).then_inc(S("w0_in"), 16)
            for col, name in enumerate(("L0_attn_ln_gamma", "L0_attn_ln_beta")):
                sp.dma_start(gb[:, col:col + 1], a[name].rearrange("(p o) -> p o", o=1)).then_inc(S("w0_in"), 16)
            sp.dma_start(wr[0][:], a["L0_ffn_Wg"]).then_inc(S("wr_in"), 16)
            sp.dma_start(wr[1][:], a["L1_ffn_Wr"]).then_inc(S("wr_in"), 16)
            sp.dma_start(wr[2][:], a["L2_ffn_router_wT"]).then_inc(S("wr_in"), 16)
            sp.dma_start(wr[3][:], a["L3_ffn_Wr"]).then_inc(S("wr_in"), 16)
            for n, name in ((1, "L1_ffn_br"), (2, "L2_ffn_expert_bias"), (3, "L3_ffn_br")):
                sp.dma_start(rbias[n][:], a[name].rearrange("(o e) -> o e", o=1).to_broadcast([P, E]))\
                    .then_inc(S("wr_in"), 16)
            sp.dma_start(w_qk1[:], a["L1_attn_wqk"]).then_inc(S("w2_in"), 16)
            sp.dma_start(w_v1[:], a["L1_attn_wv"]).then_inc(S("w2_in"), 16)
            sp.dma_start(cols1[:, 0:1], a["L1_attn_bqk"].rearrange("(p o) -> p o", o=1)).then_inc(S("w2_in"), 16)
            sp.dma_start(cols1[:, 1:3], a["L1_attn_gammaT"]).then_inc(S("w2_in"), 16)
            sp.dma_start(cols1[:, 3:5], a["L1_attn_betaT"]).then_inc(S("w2_in"), 16)
            sp.dma_start(bv1[:], a["L1_attn_bv"].rearrange("(o d) -> o d", o=1).to_broadcast([P, D])).then_inc(S("w2_in"), 16)
            sp.dma_start(table[:], a["L1_attn_rel_bias"].rearrange("(b o) -> b o", o=1)).then_inc(S("w2_in"), 16)
            sp.dma_start(bucket[:], a["const_bucket"]).then_inc(S("w2_in"), 16)
            sp.dma_start(w1_a[:], a["L0_ffn_W1"].rearrange("e p f -> p e f")).then_inc(S("w_moe1_in"), 16)
            sp.dma_start(w2_a[:], a["L0_ffn_W2"].rearrange("e (k p) d -> p e k d", p=P)).then_inc(S("w_moe1_in"), 16)
            sp.dma_start(b1_all[:], a["L0_ffn_b1"].rearrange("(o e) f -> o e f", o=1).to_broadcast([P, E, FF]))\
                .then_inc(S("w_moe1_in"), 16)
            sp.dma_start(b2_all[:], a["L0_ffn_b2"].rearrange("(o e) f -> o e f", o=1).to_broadcast([P, E, D]))\
                .then_inc(S("w_moe1_in"), 16)
            sp.dma_start(w1_b[:], a["L1_ffn_W1"].rearrange("e p f -> p e f")).then_inc(S("w_moe3_in"), 16)
            sp.dma_start(w2_b[:], a["L1_ffn_W2"].rearrange("e (k p) d -> p e k d", p=P)).then_inc(S("w_moe3_in"), 16)
            sp.dma_start(w_b2[:], a["L2_attn_B_weightT"]).then_inc(S("w4_in"), 16)
            sp.dma_start(om[:, 0:1], a["L2_attn_omega_raw"].rearrange("(p o) -> p o", o=1)).then_inc(S("w4_in"), 16)
            for dst, name in ((w12[:], "L2_ffn_w12T"), (w3[:], "L2_ffn_w3T"), (w_s1[:], "L2_ffn_shared_w1T"),
                              (w_s2[:], "L2_ffn_shared_w2T"),
                              (w_s3[:], a["L2_ffn_shared_w3T"].rearrange("(k p) d -> p k d", p=P))):
                sp.dma_start(dst, a[name] if isinstance(name, str) else name).then_inc(S("w5_in"), 16)
            sp.wait_ge(S("consts"), CONSTS)
            sp.dma_start(x_rows_dram[0:P, :], ones[:]).then_inc(S("x_out"), 16)
            if STAGES > 2:
                sp.wait_ge(S("bias_row"), 1)
                sp.dma_start(bias_dram.rearrange("(p m) -> p m", m=BIASW), bias_row[:]).then_inc(S("bias_out"), 16)
                sp.wait_ge(S("bias_out"), 16)
                skew = bias_dram[P - 1:P - 1 + P * (BIASW - 1)].rearrange("(p m) -> p m", m=BIASW - 1)
                sp.dma_start(rel[:], skew[:, 0:L]).then_inc(S("rel_in"), 16)
            if STAGES > 1:
                sp_moe(sp, 1)
                for dst, src in ((w1_a[:], a["L3_ffn_W1"].rearrange("e p f -> p e f")),
                                 (w2_a[:], a["L3_ffn_W2"].rearrange("e (k p) d -> p e k d", p=P)),
                                 (b1_all[:], a["L3_ffn_b1"].rearrange("(o e) f -> o e f", o=1).to_broadcast([P, E, FF])),
                                 (b2_all[:], a["L3_ffn_b2"].rearrange("(o e) d -> o e d", o=1).to_broadcast([P, E, D])),
                                 (b1_cols[:], a["L3_ffn_b1T"].rearrange("(k p) e -> p k e", p=P))):
                    sp.dma_start(dst, src).then_inc(S("w_moe7_in"), 16)
            if STAGES > 3:
                sp_moe(sp, 3)
            if STAGES > 6:
                sp.wait_ge(S("offsets"), 1)
                for dst, src in ((w_qkv, a["L3_attn_qkv_wT"]), (b_qk[:], a["L3_attn_qkv_bT"]), (pair_turn[:], a["const_pair"]),
                                 (rope, a["const_rope"]),
                                 (bv6, a["L3_attn_qkv_b"][2 * D:3 * D].rearrange("(o d) -> o d", o=1).to_broadcast([P, D])),
                                 (pb6, a["L3_attn_proj_b"].rearrange("(o d) -> o d", o=1).to_broadcast([P, D])),
                                 (w_p6, a["L3_attn_proj_wT"])):
                    sp.dma_start(dst, src).then_inc(S("w6_in"), 16)
            if STAGES > 6:
                sp_block6(sp)
            if STAGES > 7:
                sp_moe(sp, 7)
            sp.wait_ge(S(f"x_done{STAGES - 1}"), NCH)
            sp.dma_start(out_flat, x_sb[:]).then_inc(S("stored"), 16)
            sp.wait_ge(S("stored"), 16)
            sp.wait_ge(S("x_out"), 16)

        def pool_moe(gp, n):
            cfg = moe_cfg[n]
            nt, t0, order = moe_tiles(cfg["k"]), cfg["t0"], cfg["order"]

            def gather(j):
                if j >= 4:
                    gp.wait_ge(S("moe_xst_ps"), t0 + j - 3)
                gp.indirect_dma_start(
                    out=xs[:, j % 4, :], out_offset=None, in_=x_rows_dram[:, :],
                    in_offset=bass.IndirectOffsetOnAxis(ap=row_in[:, j:j + 1], axis=0)).then_inc(S(f"xs_in{j % 4}"), 16)

            def send(j):
                gp.wait_ge(S("moe_y_sb"), t0 + j + 1)
                if j >= 4:
                    gp.wait_ge(S(f"y_out{j % 4}"), t0 * 4 + j // 4 * 16)
                gp.indirect_dma_start(
                    out=y_rows[:, :], out_offset=bass.IndirectOffsetOnAxis(ap=row_out[:, j:j + 1], axis=0),
                    in_=ys[:, j % 4, :], in_offset=None).then_inc(S(f"y_out{j % 4}"), 16)

            gp.wait_ge(S("x_out"), 16 + 16 * NCH * order)
            gp.wait_ge(S("row_ids"), 2 * order)
            for j in range(4):
                gather(j)
            for j in range(nt):
                send(j)
                if j + 4 < nt:
                    gather(j + 4)

        def pool_block6(gp):
            gp.wait_ge(S("x_done4"), NCH)
            gp.memset(q_slab.rearrange("p u h t -> p (u h t)"), 0.0).then_inc(S("slab_zero"), 1)
            gp.memset(k_slab.rearrange("p u h t -> p (u h t)"), 0.0).then_inc(S("slab_zero"), 1)

        @block.gpsimd
        def _(gp):
            gp.memset(ident[:], 0.0).then_inc(S("consts"), 1)
            gp.memset(ones[:], 1.0).then_inc(S("consts"), 1)
            gp.wait_ge(S("consts"), 2)
            gp.affine_select(out=ident[:], in_=ident[:], compare_op=ALU.not_equal, fill=1.0, base=0,
                             pattern=[[-1, P]], channel_multiplier=1).then_inc(S("consts"), 1)
            gp.affine_select(out=before[:], in_=ones[:], compare_op=ALU.is_gt, fill=0.0, base=0,
                             pattern=[[1, P]], channel_multiplier=-1).then_inc(S("consts"), 1)
            gp.affine_select(out=causal[:], in_=ones[:], compare_op=ALU.is_ge, fill=0.0, base=0,
                             pattern=[[1, P]], channel_multiplier=-1).then_inc(S("consts"), 1)
            gp.iota(desc[:], [[-1, E]], base=E, channel_multiplier=0, allow_small_or_imprecise_dtypes=True)\
                .then_inc(S("consts"), 1)
            for dst, pattern, base, step in ((thr[:], [[P, 40]], 0, 0), (col_no[:], [[1, P]], 0, 0), (row_no[:], [[0, 1]], 0, 1),
                                             (tile_seq[:], [[1, 2 * NTILE]], 1, 0), (past[:], [[0, 10], [P, 4]], P + 2 * T, 1)):
                gp.iota(dst, pattern, base=base, channel_multiplier=step, allow_small_or_imprecise_dtypes=True)\
                    .then_inc(S("consts"), 1)
            gp.iota(tile_no[:], [[1, 40]], base=0, channel_multiplier=0, allow_small_or_imprecise_dtypes=True)\
                .then_inc(S("consts"), 1)
            gp.dma_start(lam_col[:, 0:1], a["L0_attn_beta"].rearrange("(h o) -> h o", o=1).to_broadcast([RH, D // RH]))\
                .then_inc(S("lam_in"), 16)
            if STAGES > 1:
                pool_moe(gp, 1)
            if STAGES > 3:
                pool_moe(gp, 3)
            if STAGES > 6:
                pool_block6(gp)
            if STAGES > 7:
                pool_moe(gp, 7)

        def act_norm(act, n, tag="x"):
            act.wait_ge(S("var"), norm_no(n, tag))
            act.activation(lnt[:, 7, :], lnt[:, 6, :], ACT.Sqrt).then_inc(S("sd"), 1)

        def act_xt(act, n, c):
            act.wait_ge(S("xt_ps"), NCH * n + c + 1)
            act.activation(xt[:, chunk_cols(c)], bank(c % 2), ACT.Copy).then_inc(S("xt"), 1)

        def act_block0(act):
            act_norm(act, 0)

            def silu(c):
                act.wait_ge(S("g_ps"), c + 1)
                act.activation(buf_a[:, chunk_cols(c)], bank(4), ACT.Silu).then_inc(S("gate"), 1)

            def ret_rows(c):
                act.wait_ge(S("ret_ps"), c + 1)
                act.activation(buf_c[:, chunk_cols(c)], bank(5), ACT.Copy).then_inc(S("ret_rows"), 1)

            act_xt(act, 0, 0)
            for c in range(NCH):
                if c + 1 < NCH:
                    act_xt(act, 0, c + 1)
                silu(c)
                if c >= 1:
                    ret_rows(c - 1)
            ret_rows(NCH - 1)
            act_norm(act, 0, "r")
            for c in range(NCH):
                act.wait_ge(S("rn_ps"), c + 1)
                act.activation(buf_b[:, chunk_cols(c)], bank(c % 2), ACT.Identity, scale=gb[:, 0:1], bias=gb[:, 1:2])\
                    .then_inc(S("rn"), 1)

        def act_moe(act, n):
            cfg = moe_cfg[n]
            nt, t0 = moe_tiles(cfg["k"]), cfg["t0"]
            act_norm(act, n)
            for c in range(NCH):
                act_xt(act, n, c)
            if n == 1:
                act.wait_ge(S("gap1"), 1)
                act.activation(rs[:, 11, :], rs[:, 10, :], ACT.Exp).then_inc(S("gap_exp1"), 1)
            if n == 3:
                act.wait_ge(S("logits3"), 1)
                act.activation(rt[:, 0, :], rt[:, 7, :], ACT.Sigmoid).then_inc(S("scores3"), 1)

            used = NTILE * cfg["k"]
            act.wait_ge(S("tile_hot"), moe_cfg[n]["order"])
            act.activation(tile_hot[:, 2, 0:used, 0:nt], tile_hot[:, 0, 0:used, 0:nt], ACT.Copy, scale=row_no[:, 0:1])\
                .then_inc(S("hot_row"), 1)

            def rows(j, u):
                act.wait_ge(S("moe_xst_ps"), j + (t0 + 1))
                if not (isinstance(j, int) and j < 2):
                    act.wait_ge(S("moe_h_ps"), j + (t0 - 1))
                act.activation(xst[:, u, :], bank(u, 0, P), ACT.Copy).then_inc(S("moe_xst"), 1)

            def hidden(j, u):
                act.wait_ge(S("moe_ht_ps"), j + (t0 + 1))
                if not (isinstance(j, int) and j < 2):
                    act.wait_ge(S("moe_y_ps"), j + (t0 - 1))
                act.activation(hidt[:, u, :], bank(4 + u), cfg["act"]).then_inc(S("moe_ht"), 1)

            rows(0, 0)
            rows(1, 1)

            def steps(g, last=False):
                for u in range(4):
                    j = g * 4 + u
                    hidden(j, u % 2)
                    if not (last and u >= 2):
                        rows(j + 2, u % 2)

            steps(0)
            with act.Fori(1, nt // 4 - 1) as g:
                steps(g)
            steps(nt // 4 - 1, last=True)

        def act_block2(act):
            act_norm(act, 2)

            def qk(c):
                if c >= 2:
                    act.wait_ge(S("k2"), c - 1)
                act.wait_ge(S("qk_ps2"), c + 1)
                act.activation(hid[:, c % 2, :], bank(2 + c % 2), ACT.Silu, bias=cols1[:, 0:1]).then_inc(S("qk2"), 1)

            def values(c):
                act.wait_ge(S("v_lin2"), c + 1)
                act.activation(buf_c[:, chunk_cols(c)], hidt[:, c % 2, :], ACT.Silu).then_inc(S("v2"), 1)

            act_xt(act, 2, 0)
            for c in range(NCH):
                if c + 1 < NCH:
                    act_xt(act, 2, c + 1)
                qk(c)
                if c >= 1:
                    values(c - 1)
            values(NCH - 1)
            for b in range(NB):
                if b >= 2:
                    act.wait_ge(S("phi2"), b - 1)
                act.wait_ge(S("z2"), b + 1)
                act.activation(att_g[:, b % 2, :], att_z[:, b % 2, :], ACT.Gelu).then_inc(S("gelu2"), 1)

        def act_block4(act):
            act.activation(om[:, 1:2], om[:, 0:1], ACT.Abs).then_inc(S("abs4"), 1)
            act.wait_ge(S("abs4"), 1)
            act.activation(om[:, 2:3], om[:, 1:2], ACT.Exp, scale=-1.0).then_inc(S("exp4"), 1)
            act.wait_ge(S("exp4"), 1)
            act.activation(om[:, 3:4], om[:, 2:3], ACT.Ln, bias=1.0).then_inc(S("ln4"), 1)
            act_norm(act, 4)
            act_xt(act, 4, 0)
            for c in range(NCH):
                if c + 1 < NCH:
                    act_xt(act, 4, c + 1)
                if c == 0:
                    act.wait_ge(S("pads4"), 2)
                act.wait_ge(S("force_ps4"), c + 1)
                act.activation(wave_a[:, 2 * c:2 * c + 2, P:], bank(2 + c % 2).rearrange("p (b t) -> p b t", t=L),
                               ACT.Copy, scale=float(np.float32(DT) ** 2)).then_inc(S("force4"), 1)

        def act_proj6(act):
            for c in range(NCH):
                act.wait_ge(S("ot_ps6"), c + 1)
                act.activation(buf_a[:, chunk_cols(c)], bank(c % 2), ACT.Copy).then_inc(S("ot6"), 1)

        def act_block5(act):
            act_norm(act, 5)
            for c in range(NCH):
                act_xt(act, 5, c)
            act.wait_ge(S("logit_ps"), 3)
            act.activation(em(0), bank(2, 0, NTILE * E).rearrange("p (i e) -> p e i", e=E), ACT.Sigmoid)\
                .then_inc(S("scores5"), 1)

            def chunk(c):
                for m in range(UNITS):
                    n, u = UNITS * c + m, m % 2
                    if not (isinstance(c, int) and n < 2):
                        act.wait_ge(S("h5"), n - 1)
                    act.wait_ge(S("up5"), n + 1)
                    act.activation(hid[:, u, :], bank(u), ACT.Silu).then_inc(S("silu5"), 1)

            chunk(0)
            with act.Fori(1, NCH) as c:
                chunk(c)

        def act_block6(act):
            act_norm(act, 6)
            act_xt(act, 6, 0)
            for c in range(NCH):
                if c + 1 < NCH:
                    act_xt(act, 6, c + 1)
                for src, part, ready, done in ((hid, 0, "f6", "p0_6"), (hidt, 1, "r6", "p1_6")):
                    for z, parts in enumerate((q_parts, k_parts)):
                        act.wait_ge(S(ready), 2 * c + z + 1)
                        act.activation(parts[part][:, chunk_cols(c)], src[:, z, :], ACT.Copy).then_inc(S(done), 1)

            def steps(g, first=False):
                for i in range(2 * HEADS):
                    n = g * (2 * HEADS) + i
                    act.wait_ge(S("low6"), n + 1)
                    if not (first and i < 4):
                        act.wait_ge(S("t6"), n - 3)
                    for t in range(2):
                        last = act.activation(probs(i)[:, t * L:(t + 1) * L], bank(i % 4, t * L, (t + 1) * L), ACT.Exp,
                                              scale=-1.0, bias=low[:, i % 4, t:t + 1])
                    last.then_inc(S("exp6"), 1)
                    if i % 8 == 1 and not (first and i == 1):
                        z = (i - 9) // 8
                        leave(g * 2 + z // 2, z % 2, n - 1)

            def leave(s, half, heads):
                act.wait_ge(S("pv6"), heads)
                if not (isinstance(s, int) and s < 1):
                    act.wait_ge(S("tok6"), s * 2 + (half - 1))
                act.activation(heads_t[:, half, :], bank(4), ACT.Copy).then_inc(S("heads6"), 1)

            steps(0, first=True)
            with act.Fori(1, NB // 2) as g:
                steps(g)
            leave(NB - 1, 1, NB * HEADS)

        @block.scalar
        def _(act):
            act.wait_ge(S("lam_in"), 16)
            act.activation(lam_col[:, 1:2], lam_col[:, 0:1], ACT.Exp, scale=-math.log(2.0)).then_inc(S("lam_exp"), 1)
            act_block0(act)
            if STAGES > 1:
                act_moe(act, 1)
            if STAGES > 2:
                act_block2(act)
            if STAGES > 3:
                act_moe(act, 3)
            if STAGES > 4:
                act_block4(act)
            if STAGES > 5:
                act_block5(act)
            if STAGES > 6:
                act_block6(act)
                act_proj6(act)
            if STAGES > 7:
                act_moe(act, 7)

        def pe_xt(pe, n, c):
            pe.wait_ge(S("xn"), NTILE * n + TPC * (c + 1))
            if c >= 2:
                pe.wait_ge(S("xt"), NCH * n + c - 1)
            for j in range(TPC):
                last = pe.transpose(bank(c % 2, j * P, (j + 1) * P), xn[:, TPC * c + j, :], ident[:])
            last.then_inc(S("xt_ps"), 1)

        def pe_block0(pe):
            pe.wait_ge(S("w0_in"), 16 * 6)

            def project(c):
                pe.wait_ge(S("xt"), NCH * 0 + c + 1)
                for w, b, used, done in ((w_v, 3, "state", "v_ps"), (w_q, 2, "ret", "q_ps"), (w_g, 4, "gate", "g_ps")):
                    if c >= 1:
                        pe.wait_ge(S(used), 2 * c if used == "state" else c)
                    pe.matmul(bank(b), w[:], xt[:, chunk_cols(c)], start=True, stop=True).then_inc(S(done), 1)

            def turn(c):
                pe.wait_ge(S("ret"), c + 1)
                if c >= 1:
                    pe.wait_ge(S("ret_rows"), c)
                for j in range(TPC):
                    last = pe.transpose(bank(5, j * P, (j + 1) * P), buf_b[:, tile_cols(TPC * c + j)], ident[:])
                last.then_inc(S("ret_ps"), 1)

            pe_xt(pe, 0, 0)
            for c in range(NCH):
                if c + 1 < NCH:
                    pe_xt(pe, 0, c + 1)
                project(c)
                if c >= 1:
                    turn(c - 1)
            turn(NCH - 1)
            def turn_back(c):
                pe.wait_ge(S("rn_rows"), TPC * (c + 1))
                if c >= 2:
                    pe.wait_ge(S("rn"), c - 1)
                for j in range(TPC):
                    last = pe.transpose(bank(c % 2, j * P, (j + 1) * P), xn[:, TPC * c + j, :], ident[:])
                last.then_inc(S("rn_ps"), 1)

            turn_back(0)
            for c in range(NCH):
                if c + 1 < NCH:
                    turn_back(c + 1)
                pe.wait_ge(S("gated"), c + 1)
                if c >= 2:
                    pe.wait_ge(S("x_done0"), c - 1)
                for j in range(TPC):
                    last = pe.matmul(bank(2 + c % 2, j * P, (j + 1) * P), buf_b[:, tile_cols(TPC * c + j)], w_o[:],
                                     start=True, stop=True)
                last.then_inc(S("o_ps"), 1)

        def pe_route(pe, n, w):
            if n == 1:
                pe.wait_ge(S("wr_in"), 16 * 7)
            pe_xt(pe, n, 0)
            for c in range(NCH):
                if c + 1 < NCH:
                    pe_xt(pe, n, c + 1)
                pe.wait_ge(S("xt"), NCH * n + c + 1)
                for i in range(TPC * c, TPC * (c + 1)):
                    last = pe.matmul(bank(2, i * E, (i + 1) * E), xt[:, tile_cols(i)], w[:], start=True, stop=True)
            last.then_inc(S("logit_ps"), 1)

        def pe_moe(pe, n):
            cfg = moe_cfg[n]
            nt, t0 = moe_tiles(cfg["k"]), cfg["t0"]
            w1, w2 = cfg["w1"], cfg["w2"]
            pe_route(pe, n, wr[cfg["r"]])
            pe.wait_ge(S(f"chosen{n}"), 1)
            pe.matmul(bank(3, 0, P), before[:], rt[:, 3, :], start=True, stop=True)
            pe.matmul(bank(3, P, 2 * P), ones[:], rt[:, 3, :], start=True, stop=True).then_inc(S(f"rank_ps{n}"), 1)
            order, used = moe_cfg[n]["order"], NTILE * cfg["k"]
            pe.wait_ge(S("hot_row"), order)
            pe.wait_ge(S("hot_seq"), order)
            for i in range(used):
                if i % NTILE == 0:
                    pe.wait_ge(S("place_hot"), cfg["k0"] + i // NTILE + 1)
                last = pe.matmul(bank(4, 0, 2 * nt), place_hot[:, i, :], tile_hot[:, 1:3, i, 0:nt],
                                 start=(i == 0), stop=(i == used - 1))
            last.then_inc(S("row_ps"), 1)
            pe.wait_ge(S(f"eid{n}"), 1)
            pe.wait_ge(S(f"w_moe{n}_in"), 16 * {1: 4, 3: 2, 7: 5}[n])

            def turn_rows(g, u4, u):
                pe.wait_ge(S(f"xs_in{u4}"), g * 16 + (t0 * 4 + 16))
                pe.transpose(bank(u, 0, P), xs[:, u4, 0:D], ident[:]).then_inc(S("moe_xst_ps"), 1)

            def expert(j):
                return pe.value_load(eid[0:1, bass.ds(j, 1)], min_val=0, max_val=E - 1)

            def up(j, u, e):
                pe.wait_ge(S("moe_xst"), j + (t0 + 1))
                pe.matmul(bank(2 + u), xst[:, u, :], w1[:, bass.ds(e, 1), :], start=True, stop=True)\
                    .then_inc(S("moe_h_ps"), 1)

            def turn_hidden(j, u):
                pe.wait_ge(S("moe_h"), j + (t0 + 1))
                if not (isinstance(j, int) and j < 2):
                    pe.wait_ge(S("moe_ht"), j + (t0 - 1))
                for k in range(KF):
                    last = pe.transpose(bank(4 + u, k * P, (k + 1) * P), hid[:, u, k * P:(k + 1) * P], ident[:])
                last.then_inc(S("moe_ht_ps"), 1)

            def down(j, u, e):
                if not (isinstance(j, int) and j < 2):
                    pe.wait_ge(S("moe_y_sb"), j + (t0 - 1))
                pe.wait_ge(S("moe_ht"), j + (t0 + 1))
                for k in range(KF):
                    last = pe.matmul(bank(6 + u, 0, D), hidt[:, u, k * P:(k + 1) * P], w2[:, bass.ds(e, 1), k, :],
                                     start=(k == 0), stop=(k == KF - 1))
                last.then_inc(S("moe_y_ps"), 1)

            turn_rows(0, 0, 0)
            turn_rows(0, 1, 1)
            up(0, 0, expert(0))

            def steps(g, last=False):
                e = expert(g * 4)
                for u in range(4):
                    j = g * 4 + u
                    turn_hidden(j, u % 2)
                    if not (last and u == 3):
                        e_next = expert(j + 1)
                        up(j + 1, (u + 1) % 2, e_next)
                    down(j, u % 2, e)
                    e = e_next
                    if not (last and u >= 2):
                        turn_rows(g + (u + 2) // 4, (u + 2) % 4, u % 2)

            steps(0)
            with pe.Fori(1, nt // 4 - 1) as g:
                steps(g)
            steps(nt // 4 - 1, last=True)

        def pe_rel_bias(pe):
            pe.wait_ge(S("table"), 1)
            pe.matmul(bank(7, 0, BIASW), table_all[:], bucket[:], start=True, stop=True).then_inc(S("bias_ps"), 1)

        def pe_block2(pe):
            pe_xt(pe, 2, 0)
            for c in range(NCH):
                if c + 1 < NCH:
                    pe_xt(pe, 2, c + 1)
                pe.wait_ge(S("xt"), NCH * 2 + c + 1)
                if c >= 2:
                    pe.wait_ge(S("qk2"), c - 1)
                pe.matmul(bank(2 + c % 2), w_qk1[:], xt[:, chunk_cols(c)], start=True, stop=True).then_inc(S("qk_ps2"), 1)
                if c >= 2:
                    pe.wait_ge(S("v_lin2"), c - 1)
                for j in range(TPC):
                    last = pe.matmul(bank(4 + c % 2, j * P, (j + 1) * P), xt[:, tile_cols(TPC * c + j)], w_v1[:],
                                     start=True, stop=True)
                last.then_inc(S("v_ps2"), 1)

            def scores(b):
                if b >= 2:
                    pe.wait_ge(S("z2"), b - 1)
                pe.wait_ge(S("k2"), b // 2 + 1)
                t0 = b * L
                pe.matmul(bank(6 + b % 2, 0, L), buf_b[:, t0:t0 + P], buf_a[:, t0:t0 + L], start=True, stop=True)
                pe.matmul(bank(6 + b % 2, L, L + P), buf_b[:, t0 + P:t0 + L], buf_a[:, t0 + P:t0 + L],
                          start=True, stop=True).then_inc(S("s_ps2"), 1)

            scores(0)
            for b in range(NB):
                if b + 1 < NB:
                    scores(b + 1)
                pe.wait_ge(S("v2"), b // 2 + 1)
                if b >= 2:
                    pe.wait_ge(S("x_add2"), b - 1)
                pe.wait_ge(S("phi2"), b + 1)
                i = 2 * b
                o = 2 + b % 2
                pe.matmul(bank(o, 0, P), att_z[:, b % 2, 0:P], buf_c[:, tile_cols(i)], start=True, stop=True)
                pe.matmul(bank(o, P, 2 * P), att_z[:, b % 2, P:2 * P], buf_c[:, tile_cols(i)], start=True, stop=False)
                pe.matmul(bank(o, P, 2 * P), att_z[:, b % 2, 2 * P:3 * P], buf_c[:, tile_cols(i + 1)],
                          start=False, stop=True).then_inc(S("o_ps2"), 1)

        def pe_block4(pe):
            pe_xt(pe, 4, 0)
            for c in range(NCH):
                if c + 1 < NCH:
                    pe_xt(pe, 4, c + 1)
                pe.wait_ge(S("xt"), NCH * 4 + c + 1)
                if c >= 2:
                    pe.wait_ge(S("force4"), c - 1)
                pe.matmul(bank(2 + c % 2), w_b2[:], xt[:, chunk_cols(c)], start=True, stop=True).then_inc(S("force_ps4"), 1)
            for c in range(NCH):
                pe.wait_ge(S("solved4"), c // 2 + 1)
                for j in range(TPC):
                    b, h = 2 * c + j // 2, j % 2
                    last = pe.transpose(bank(4 + c, j * P, (j + 1) * P), wave_b[:, b, (1 + h) * P:(2 + h) * P], ident[:])
                last.then_inc(S("v_ps4"), 1)

        def pe_block5(pe):
            pe_route(pe, 5, wr[2])
            pe.wait_ge(S("w5_in"), 16 * 5)
            pe.wait_ge(S("scores5"), 1)

            def up(c, m):
                n, u = UNITS * c + m, m % 2
                if not (isinstance(c, int) and n < 2):
                    pe.wait_ge(S("h5"), n - 1)
                wa = w_s1[:, tile_cols(m)] if m < KF else w12[:, m - KF, 0:P]
                wb = w_s2[:, tile_cols(m)] if m < KF else w12[:, m - KF, P:2 * P]
                rhs = xt[:, bass.ds(c * CH, CH)]
                pe.matmul(bank(u), wa, rhs, start=True, stop=True)
                pe.matmul(bank(4 + u), wb, rhs, start=True, stop=True).then_inc(S("up5"), 1)

            def down(c, m):
                n, u, e = UNITS * c + m, m % 2, m - KF
                first = isinstance(c, int) and c == 0
                if m == 0 and not first:
                    pe.wait_ge(S("acc5"), (E + 1) * c)
                if e >= 2:
                    pe.wait_ge(S("acc5"), (E + 1) * c + e)
                pe.wait_ge(S("h5"), n + 1)
                for j in range(TPC):
                    if m < KF:
                        last = pe.matmul(bank(3, j * P, (j + 1) * P), hidt[:, u, tile_cols(j)], w_s3[:, m, :],
                                         start=(m == 0 and j == 0), stop=(m == KF - 1), skip_group_check=True)
                    else:
                        last = pe.matmul(bank(6 + e % 2, j * P, (j + 1) * P), hidt[:, u, tile_cols(j)], w3[:, e, :],
                                         start=True, stop=True)
                last.then_inc(S("down5"), 1)

            def chunk(c):
                up(c, 0)
                for m in range(UNITS):
                    if m + 1 < UNITS:
                        up(c, m + 1)
                    down(c, m)

            chunk(0)
            with pe.Fori(1, NCH) as c:
                chunk(c)

        def pe_offsets(pe):
            pe.wait_ge(S("w_moe7_in"), 16 * 5)
            for e in range(E):
                pe.wait_ge(S("idle"), e + 1)
                for k in range(KF):
                    last = pe.matmul(bank(6 + e // 4, (e % 4) * P, (e % 4 + 1) * P), idle[:, (e % 2) * KF + k, :],
                                     w2_a[:, e, k, :], start=(k == 0), stop=(k == KF - 1))
                last.then_inc(S("idle_ps"), 1)

        def pe_block6(pe):
            pe.wait_ge(S("w_rot"), 2)
            pe.wait_ge(S("w6_in"), 16 * 7)
            pe.matmul(bank(7, 0, 2), pair_turn[:], b_qk[:, 0:2], start=True, stop=True).then_inc(S("b_rot_ps"), 1)
            pe_xt(pe, 6, 0)
            for c in range(NCH):
                if c + 1 < NCH:
                    pe_xt(pe, 6, c + 1)
                pe.wait_ge(S("xt"), NCH * 6 + c + 1)
                for b, w, free in ((2, w_qkv[:, 0:D], 0), (3, w_rot[:, 0:D], 0),
                                   (4, w_qkv[:, D:2 * D], 1), (5, w_rot[:, D:2 * D], 1)):
                    if c >= 1:
                        pe.wait_ge(S("f6"), 2 * c - 1 + free)
                    pe.matmul(bank(b), w, xt[:, chunk_cols(c)], start=True, stop=True).then_inc(S("qk_ps6"), 1)
                if c >= 1:
                    pe.wait_ge(S("v6"), c)
                for j in range(TPC):
                    last = pe.matmul(bank(6, j * P, (j + 1) * P), xt[:, tile_cols(TPC * c + j)], w_qkv[:, 2 * D:3 * D],
                                     start=True, stop=True)
                last.then_inc(S("v_ps6"), 1)
            pe.wait_ge(S("v6"), NCH)

            def score(g, i, skip=False):
                g, i = (g + 1, i - 2 * HEADS) if i >= 2 * HEADS else (g, i)
                n, u, h = g * (2 * HEADS) + i, i // HEADS, i % HEADS
                if h == 0:
                    pe.wait_ge(S(f"slab_in{u}"), g * (16 * 12) + 16 * 12)
                if not (isinstance(n, int) and n < 4):
                    pe.wait_ge(S("exp6"), n - 3)
                for t in range(2):
                    last = pe.matmul(bank(i % 4, t * L, (t + 1) * L), q_slab[:, u, h, t * P:(t + 1) * P], k_slab[:, u, h, :],
                                     start=True, stop=True)
                last.then_inc(S("s6"), 1)

            def turn(g, i):
                g, i = (g + 1, i - 2 * HEADS) if i >= 2 * HEADS else (g, i)
                n = g * (2 * HEADS) + i
                pe.wait_ge(S("exp6"), n + 1)
                if not (isinstance(n, int) and n < 2):
                    pe.wait_ge(S("pt6"), n - 1)
                for t in range(2):
                    for kt in range(2):
                        last = pe.transpose(bank(6 + i % 2, kt * L + t * P, kt * L + (t + 1) * P),
                                            probs(i)[:, t * L + kt * P:t * L + (kt + 1) * P], ident[:])
                last.then_inc(S("t6"), 1)

            def weigh(g, i):
                n, u, h = g * (2 * HEADS) + i, i // HEADS, i % HEADS
                s = g * 2 + u
                if h == 0:
                    pe.wait_ge(S("v_seq6"), s + 1)
                if h % 8 == 0 and not (isinstance(s, int) and s == 0 and h == 0):
                    pe.wait_ge(S("heads6"), s * 2 + h // 8)
                pe.wait_ge(S("pt6"), n + 1)
                for kt in range(2):
                    last = pe.matmul(psum[32 * (h % 4):32 * (h % 4) + HD + 1, 4,
                                          (h // 4 % 2) * L:(h // 4 % 2 + 1) * L],
                                     v_seq[:, u, kt, h, :], probs_t[:, i % 2, kt * L:(kt + 1) * L],
                                     start=(kt == 0), stop=(kt == 1), tile_position=(0, 32 * (h % 4)))
                last.then_inc(S("pv6"), 1)

            def back(s, half):
                pe.wait_ge(S("heads6"), s * 2 + (half + 1))
                if not (isinstance(s, int) and s < 1 and half == 0):
                    pe.wait_ge(S("o6"), s * 2 + half)
                for t in range(2):
                    for z in range(2):
                        last = pe.transpose(bank(5, (2 * t + z) * P, (2 * t + z + 1) * P),
                                            heads_t[:, half, z * L + t * P:z * L + (t + 1) * P], ident[:])
                last.then_inc(S("tok6"), 1)

            pe.wait_ge(S("clear6"), 1)
            score(0, 0)
            score(0, 1)
            score(0, 2)
            turn(0, 0)

            def steps(g, last=False):
                for i in range(2 * HEADS):
                    if not (last and i + 3 >= 2 * HEADS):
                        score(g, i + 3)
                    if not (last and i + 1 >= 2 * HEADS):
                        turn(g, i + 1)
                    weigh(g, i)
                    if i % 8 == 3 and not (isinstance(g, int) and g == 0 and i == 3):
                        z = (i - 11) // 8
                        back(g * 2 + z // 2, z % 2)

            steps(0)
            with pe.Fori(1, NB // 2 - 1) as g:
                steps(g)
            steps(NB // 2 - 1, last=True)
            back(NB - 1, 1)

            for c in range(NCH):
                pe.wait_ge(S("o6"), 4 * c + 4)
                if c >= 2:
                    pe.wait_ge(S("ot6"), c - 1)
                for j in range(TPC):
                    last = pe.transpose(bank(c % 2, j * P, (j + 1) * P), xn[:, TPC * c + j, :], ident[:])
                last.then_inc(S("ot_ps6"), 1)
                pe.wait_ge(S("ot6"), c + 1)
                if c >= 2:
                    pe.wait_ge(S("x_done6"), c - 1)
                for j in range(TPC):
                    last = pe.matmul(bank(2 + c % 2, j * P, (j + 1) * P), buf_a[:, tile_cols(TPC * c + j)], w_p6,
                                     start=True, stop=True)
                last.then_inc(S("proj_ps6"), 1)

        @block.tensor
        def _(pe):
            pe.wait_ge(S("consts"), CONSTS)
            pe_block0(pe)
            if STAGES > 2:
                pe_rel_bias(pe)
            if STAGES > 1:
                pe_moe(pe, 1)
            if STAGES > 2:
                pe_block2(pe)
            if STAGES > 3:
                pe_moe(pe, 3)
            if STAGES > 4:
                pe_block4(pe)
            if STAGES > 6:
                pe_offsets(pe)
            if STAGES > 5:
                pe_block5(pe)
            if STAGES > 6:
                pe_block6(pe)
            if STAGES > 7:
                pe_moe(pe, 7)

        def dve_stats(v, ch, n, c, dst, src):
            for i in range(TPC * c, TPC * (c + 1)):
                last = v.bn_stats(dst[:, i, :], src(i))
            ch(last)

        def dve_var(v, ch, n, st, tag="x"):
            ch.wait()
            me, mo, qe, qo = st[:, :, 1], st[:, :, 4], st[:, :, 2], st[:, :, 5]
            ch(v.tensor_tensor(lnt[:, 1, :], me, mo, ALU.add))
            ch(v.tensor_tensor(lnt[:, 2, :], me, mo, ALU.subtract))
            ch.link(v.tensor_tensor(lnt[:, 3, :], qe, qo, ALU.add))
            ch(v.tensor_scalar(lnt[:, 0, :], lnt[:, 1, :], 0.5, None, ALU.mult))
            ch.link(v.tensor_tensor(lnt[:, 4, :], lnt[:, 2, :], lnt[:, 2, :], ALU.mult))
            ch.link(v.scalar_tensor_tensor(out=lnt[:, 2, :], in0=lnt[:, 4, :], scalar=D / 4.0, in1=lnt[:, 3, :],
                                           op0=ALU.mult, op1=ALU.add))
            v.tensor_scalar(lnt[:, 6, :], lnt[:, 2, :], 1.0 / D, EPS, ALU.mult, ALU.add).then_inc(S("var"), 1)
            v.wait_ge(S("sd"), norm_no(n, tag))
            ch.link(v.reciprocal(lnt[:, 5, :], lnt[:, 7, :]))

        def dve_norm(v, ch, n, src, done):
            for i in range(NTILE):
                v.tensor_scalar(xn[:, i, :], src(i), lnt[:, 0, i:i + 1], lnt[:, 5, i:i + 1], ALU.subtract, ALU.mult)\
                    .then_inc(S(done), 1)

        def dve_block0(v, ch):
            v.wait_ge(S("lam_exp"), 1)
            ch.link(v.tensor_scalar(lam_col[:, 2:3], lam_col[:, 1:2], -1.0, 1.0, ALU.mult, ALU.add))
            ch.link(v.tensor_scalar(lam_col[:, 3:4], lam_col[:, 2:3], float(np.finfo(np.float32).tiny),
                                    float(np.float32(1.0 - 1e-9)), ALU.max, ALU.min))
            v.wait_ge(S("consts"), CONSTS)
            for r in range(L // P):
                ch(v.tensor_scalar(lam[:, tile_cols(r)], ones[:], lam_col[:, 3:4], None, ALU.mult))
            for c in range(NCH):
                v.wait_ge(S(f"x_in{c}"), 16)
                dve_stats(v, ch, 0, c, stats, x_rows)
            dve_var(v, ch, 0, stats)
            dve_norm(v, ch, 0, x_rows, "xn")
            for c in range(NCH):
                v.wait_ge(S("v_ps"), c + 1)
                if c >= 1:
                    v.wait_ge(S("ret"), c)
                for s in range(CH // L):
                    v.tensor_tensor_scan(state[:, s * L:(s + 1) * L], lam[:],
                                         bank(3, s * L, (s + 1) * L), 0.0, ALU.mult, ALU.add).then_inc(S("state"), 1)
                v.wait_ge(S("state"), 2 * c + 2)
                v.wait_ge(S("q_ps"), c + 1)
                v.tensor_tensor(buf_b[:, chunk_cols(c)], state[:], bank(2), ALU.mult).then_inc(S("ret"), 1)
                if c >= 1:
                    v.wait_ge(S("ret_rows"), c)
                    dve_stats(v, ch, 0, c - 1, stats2, lambda i: buf_c[:, tile_cols(i)])
            v.wait_ge(S("ret_rows"), NCH)
            dve_stats(v, ch, 0, NCH - 1, stats2, lambda i: buf_c[:, tile_cols(i)])
            dve_var(v, ch, 0, stats2, "r")
            dve_norm(v, ch, 0, lambda i: buf_c[:, tile_cols(i)], "rn_rows")
            def finish(c):
                v.wait_ge(S("o_ps"), c + 1)
                v.tensor_tensor(x_chunk(c), x_chunk(c), bank(2 + c % 2), ALU.add).then_inc(S("x_done0"), 1)
                v.wait_ge(S("x_done0"), c + 1)
                dve_stats(v, ch, 1, c, stats, x_rows)

            for c in range(NCH):
                v.wait_ge(S("rn"), c + 1)
                v.wait_ge(S("gate"), c + 1)
                v.tensor_tensor(buf_b[:, chunk_cols(c)], buf_b[:, chunk_cols(c)], buf_a[:, chunk_cols(c)], ALU.mult)\
                    .then_inc(S("gated"), 1)
                if c >= 1:
                    finish(c - 1)
            finish(NCH - 1)

        def dve_choose(v, ch, logits, best, top, one_hot):
            ch.link(v.tensor_reduce(rs[:, best, :], by_tile(logits), AX.X, ALU.max))
            ch.link(v.tensor_tensor(em(6), em(logits), over_e(rs[:, best, :]), ALU.is_equal))
            ch.link(v.tensor_tensor(em(6), em(6), over_i(desc[:]), ALU.mult))
            ch.link(v.tensor_reduce(rs[:, top, :], by_tile(6), AX.X, ALU.max))
            ch.link(v.tensor_tensor(em(one_hot), over_i(desc[:]), over_e(rs[:, top, :]), ALU.is_equal))

        def dve_slots(v, ch, n, k):
            nt, order = moe_tiles(k), moe_cfg[n]["order"]
            v.wait_ge(S(f"rank_ps{n}"), 1)
            counts = bank(3, P, 2 * P)
            ch(v.tensor_tensor_scan(rt[:, 8, :], ones[:], counts, 0.0, ALU.mult, ALU.add))
            ch.link(v.tensor_reduce(rs[:, 4, 0:E], counts.rearrange("p (e i) -> p e i", e=E), AX.X, ALU.add))
            ch(v.tensor_tensor(em(9), over_i(rs[:, 4, 0:E]), over_e(thr[:, 0:NTILE]), ALU.is_gt))
            ch.link(v.tensor_tensor_scan(rs[:, 5, 0:E], ones[:, 0:E], rs[:, 4, 0:E], 0.0, ALU.mult, ALU.add))
            ch(v.tensor_tensor(rs[:, 5, 8:16], rs[:, 5, 0:E], rs[:, 4, 0:E], ALU.subtract))
            ch.link(v.tensor_reduce(rs[:, 6, 0:E], em(9), AX.X, ALU.add))
            ch.link(v.tensor_tensor_scan(rs[:, 7, 0:E], ones[:, 0:E], rs[:, 6, 0:E], 0.0, ALU.mult, ALU.add))
            ch(v.tensor_tensor(rs[:, 8, 0:E], rs[:, 7, 0:E], rs[:, 6, 0:E], ALU.subtract))
            ends = rs[0:1, 7, 0:E].rearrange("p (o e) -> p o e", o=1).to_broadcast([1, nt, E])
            nos = tile_no[:, 0:nt].rearrange("p (j o) -> p j o", o=1).to_broadcast([1, nt, E])
            ch.link(v.tensor_tensor(eid_f[:, 0:nt, :], ends, nos, ALU.is_le))
            ch.link(v.tensor_reduce(eid_s[:, 0:nt], eid_f[:, 0:nt, :], AX.X, ALU.add))
            v.tensor_scalar(eid[:, 0:nt], eid_s[:, 0:nt], float(E - 1), None, ALU.min).then_inc(S(f"eid{n}"), 1)
            ch(v.scalar_tensor_tensor(out=rs[:, 9, 0:E], in0=rs[:, 8, 0:E], scalar=float(P), in1=rs[:, 5, 8:16],
                                      op0=ALU.mult, op1=ALU.subtract))
            ch.link(v.tensor_tensor(em(9), em(8), counts.rearrange("p (e i) -> p e i", e=E), ALU.subtract))
            ch.link(v.tensor_tensor(em(8), em(9), over_i(rs[:, 9, 0:E]), ALU.add))
            ch.link(v.tensor_tensor(rt[:, 9, :], rt[:, 8, :], bank(3, 0, P), ALU.add))
            for c in range(k):
                ch.link(v.tensor_tensor(rt[:, 8, :], rt[:, 9, :], rt[:, 1 + c, :] if k > 1 else rt[:, 3, :], ALU.mult))
                ch.link(v.tensor_reduce(rs[:, 16 + c, :], by_tile(8), AX.X, ALU.add))
            used = k * NTILE
            slot, place, start = (rs[:, 16 + 2 * z:18 + 2 * z, :].rearrange("p k i -> p (k i)")[:, 0:used] for z in range(3))
            ch.link(v.tensor_scalar(place, slot, 0.5 - P / 2, ROUND128, ALU.add, ALU.add))
            ch.link(v.tensor_scalar(start, place, -ROUND128, None, ALU.add))
            ch.link(v.tensor_tensor(place, slot, start, ALU.subtract))

            def rows_by(ap, cols):
                return ap.rearrange("p (i o) -> p i o", o=1).to_broadcast([P, ap.shape[1], cols])

            def cols_by(ap, rows):
                return ap.rearrange("p (o j) -> p o j", o=1).to_broadcast([P, rows, ap.shape[1]])

            v.tensor_tensor(tile_hot[:, 0, 0:used, 0:nt], rows_by(start, nt), cols_by(thr[:, 0:nt], used), ALU.is_equal)\
                .then_inc(S("tile_hot"), 1)
            v.wait_ge(S("tile_hot"), order)
            v.tensor_tensor(tile_hot[:, 1, 0:used, 0:nt], tile_hot[:, 0, 0:used, 0:nt], rows_by(tile_seq[:, 0:used], nt),
                            ALU.mult).then_inc(S("hot_seq"), 1)
            for c in range(k):
                i = slice(c * NTILE, (c + 1) * NTILE)
                v.tensor_tensor(place_hot[:, i, :], rows_by(place[:, i], P), cols_by(col_no[:], NTILE), ALU.is_equal)\
                    .then_inc(S("place_hot"), 1)
            v.wait_ge(S("row_ps"), order)
            seq, low_part = bank(4, 0, nt), bank(4, nt, 2 * nt)
            ch(v.tensor_scalar(row_f[:, 3, 0:nt], low_part, 1.0, None, ALU.mult))
            ch.link(v.tensor_scalar(row_f[:, 0, 0:nt], seq, float(P), None, ALU.mult))
            ch(v.scalar_tensor_tensor(out=row_f[:, 1, 0:nt], in0=seq, scalar=0.0, in1=past[:, 0:nt],
                                      op0=ALU.is_equal, op1=ALU.mult))
            ch.link(v.tensor_tensor(row_f[:, 2, 0:nt], row_f[:, 0, 0:nt], row_f[:, 3, 0:nt], ALU.add))
            ch(v.tensor_scalar(row_f[:, 0, 0:nt], row_f[:, 2, 0:nt], float(P + T), -float(T), ALU.is_ge, ALU.mult))
            v.tensor_tensor(row_out[:, 0:nt], row_f[:, 2, 0:nt], row_f[:, 1, 0:nt], ALU.add).then_inc(S("row_ids"), 1)
            ch.wait()
            v.tensor_tensor(row_in[:, 0:nt], row_f[:, 2, 0:nt], row_f[:, 0, 0:nt], ALU.add).then_inc(S("row_ids"), 1)
            v.wait_ge(S(f"eid{n}"), 1)

        def dve_moe(v, ch, n):
            cfg = moe_cfg[n]
            k, nt, k0, t0 = cfg["k"], moe_tiles(cfg["k"]), cfg["k0"], cfg["t0"]
            dve_var(v, ch, n, stats)
            dve_norm(v, ch, n, x_rows, "xn")
            v.wait_ge(S("logit_ps"), (n + 1) // 2)
            logits_ps = bank(2, 0, NTILE * E).rearrange("p (i e) -> p e i", e=E)
            if n == 7:
                ch.link(v.tensor_tensor(em(0), logits_ps, over_i(rbias[3][:]), ALU.add))
                dve_choose(v, ch, 0, 0, 1, 3)
                v.sem_inc(S(f"chosen{n}"), 1)
            elif n == 1:
                ch.link(v.tensor_copy(em(0), logits_ps))
                dve_choose(v, ch, 0, 0, 1, 1)
                ch.link(v.scalar_tensor_tensor(out=em(5), in0=em(1), scalar=NEG, in1=em(0), op0=ALU.mult, op1=ALU.add))
                dve_choose(v, ch, 5, 2, 3, 2)
                v.tensor_tensor(rt[:, 3, :], rt[:, 1, :], rt[:, 2, :], ALU.add).then_inc(S(f"chosen{n}"), 1)
                v.tensor_tensor(rs[:, 10, :], rs[:, 2, :], rs[:, 0, :], ALU.subtract).then_inc(S("gap1"), 1)
            elif n == 3:
                v.tensor_tensor(em(7), logits_ps, over_i(rbias[1][:]), ALU.add).then_inc(S("logits3"), 1)
                v.wait_ge(S("scores3"), 1)
                dve_choose(v, ch, 0, 14, 1, 3)
                ch(v.tensor_copy(rs[:, 15, :], rs[:, 14, :]))
                ch.wait()
                v.sem_inc(S(f"chosen{n}"), 1)
            dve_slots(v, ch, n, k)
            if n == 1:
                v.wait_ge(S("gap_exp1"), 1)
                ch.link(v.tensor_scalar(rs[:, 12, :], rs[:, 11, :], 1.0, None, ALU.add))
                ch.link(v.reciprocal(rs[:, 14, :], rs[:, 12, :]))
                ch.link(v.tensor_tensor(rs[:, 15, :], rs[:, 11, :], rs[:, 14, :], ALU.mult))

            def expert(j):
                return v.value_load(eid[0:1, bass.ds(j, 1)], min_val=0, max_val=E - 1) if cfg["bias"] else None

            def hidden(j, u, e):
                if not (isinstance(j, int) and j < 2):
                    v.wait_ge(S("moe_ht_ps"), j + (t0 - 1))
                v.wait_ge(S("moe_h_ps"), j + (t0 + 1))
                if cfg["bias"]:
                    ins = v.tensor_tensor(hid[:, u, :], bank(2 + u), b1_all[:, bass.ds(e, 1), :], ALU.add)
                else:
                    ins = v.tensor_copy(hid[:, u, :], bank(2 + u))
                ins.then_inc(S("moe_h"), 1)

            def result(g, j, u4, e):
                if not isinstance(g, int) or g > 0:
                    v.wait_ge(S(f"y_out{u4}"), g * 16 + t0 * 4)
                v.wait_ge(S("moe_y_ps"), j + (t0 + 1))
                if cfg["bias"]:
                    ins = v.tensor_tensor(ys[:, u4, :], bank(6 + u4 % 2, 0, D), b2_all[:, bass.ds(e, 1), :], ALU.add)
                else:
                    ins = v.tensor_copy(ys[:, u4, :], bank(6 + u4 % 2, 0, D))
                ins.then_inc(S("moe_y_sb"), 1)

            hidden(0, 0, expert(0))

            def steps(g, last=False):
                e = expert(g * 4)
                for u in range(4):
                    if not (last and u == 3):
                        e_next = expert(g * 4 + u + 1)
                        hidden(g * 4 + u + 1, (u + 1) % 2, e_next)
                    result(g, g * 4 + u, u, e)
                    e = e_next

            steps(0)
            with v.Fori(1, nt // 4 - 1) as g:
                steps(g)
            steps(nt // 4 - 1, last=True)

            for c in range(NCH):
                v.wait_ge(S(f"back{c}"), 16 * (k0 + k))
                for kk in range(k):
                    for i in range(TPC * c, TPC * (c + 1)):
                        back = (buf_a, buf_b)[kk][:, tile_cols(i)]
                        if n == 7:
                            ch(v.tensor_tensor(x_sb[:, i, :], x_sb[:, i, :], back, ALU.add))
                        else:
                            ch(v.scalar_tensor_tensor(out=x_sb[:, i, :], in0=back, scalar=rs[:, 14 + kk, i:i + 1],
                                                      in1=x_sb[:, i, :], op0=ALU.mult, op1=ALU.add))
                    ch.wait()
                v.sem_inc(S(f"x_done{n}"), 1)
                if n < 7:
                    dve_stats(v, ch, n + 1, c, stats, x_rows)

        def dve_rel_bias(v, ch):
            v.wait_ge(S("w2_in"), 16 * 8)
            v.wait_ge(S("consts"), CONSTS)
            v.tensor_scalar(table_all[:], ones[0:NBUCKET, :], table[:, 0:1], None, ALU.mult).then_inc(S("table"), 1)
            v.wait_ge(S("bias_ps"), 1)
            v.tensor_scalar(bias_row[:], bank(7, 0, BIASW), math.sqrt(D) / STD, -MU / STD, ALU.mult, ALU.add)\
                .then_inc(S("bias_row"), 1)

        def dve_block2(v, ch):
            dve_var(v, ch, 2, stats)
            dve_norm(v, ch, 2, x_rows, "xn")
            for c in range(NCH):
                if c >= 2:
                    v.wait_ge(S("v2"), c - 1)
                v.wait_ge(S("v_ps2"), c + 1)
                v.tensor_tensor(hidt[:, c % 2, :].rearrange("p (i d) -> p i d", d=D),
                                bank(4 + c % 2).rearrange("p (i d) -> p i d", d=D),
                                bv1[:].rearrange("p (o d) -> p o d", o=1).to_broadcast([P, TPC, D]), ALU.add)\
                    .then_inc(S("v_lin2"), 1)
                v.wait_ge(S("qk2"), c + 1)
                v.tensor_scalar(buf_a[:, chunk_cols(c)], hid[:, c % 2, :], cols1[:, 1:2], cols1[:, 3:4], ALU.mult, ALU.add)\
                    .then_inc(S("k2_q"), 1)
                v.wait_ge(S("k2_q"), c + 1)
                v.tensor_scalar(buf_b[:, chunk_cols(c)], hid[:, c % 2, :], cols1[:, 2:3], cols1[:, 4:5], ALU.mult, ALU.add)\
                    .then_inc(S("k2"), 1)

            v.wait_ge(S("rel_in"), 16)

            def zed(b):
                u = b % 2
                if b >= 2:
                    v.wait_ge(S("o_ps2"), b - 1)
                v.wait_ge(S("s_ps2"), b + 1)
                scale = 1.0 / L / STD
                ch(v.scalar_tensor_tensor(out=att_z[:, u, 0:L], in0=bank(6 + u, 0, L), scalar=scale, in1=rel[:],
                                          op0=ALU.mult, op1=ALU.add))
                ch.link(v.scalar_tensor_tensor(out=att_z[:, u, L:L + P], in0=bank(6 + u, L, L + P), scalar=scale,
                                               in1=rel[:, 0:P], op0=ALU.mult, op1=ALU.add))
                v.tensor_scalar(att_z[:, u, :], att_z[:, u, :], TINY, None, ALU.add).then_inc(S("z2"), 1)
                v.wait_ge(S("z2"), b + 1)
                ch.link(v.reciprocal(att_r[:, u, :], att_z[:, u, :]))
                ch.link(v.tensor_tensor(att_r[:, u, 0:P], att_r[:, u, 0:P], causal[:], ALU.mult))
                ch.link(v.tensor_tensor(att_r[:, u, L:L + P], att_r[:, u, L:L + P], causal[:], ALU.mult))

            def phi(b):
                u = b % 2
                v.wait_ge(S("gelu2"), b + 1)
                v.tensor_tensor(att_z[:, u, :], att_g[:, u, :], att_r[:, u, :], ALU.mult).then_inc(S("phi2"), 1)

            def add(b):
                v.wait_ge(S("o_ps2"), b + 1)
                rows = x_sb[:, 2 * b:2 * b + 2, :].rearrange("p i d -> p (i d)")
                v.tensor_tensor(rows, rows, bank(2 + b % 2, 0, 2 * P), ALU.add).then_inc(S("x_add2"), 1)
                if b % 2:
                    v.wait_ge(S("x_add2"), b + 1)
                    v.sem_inc(S("x_done2"), 1)
                    dve_stats(v, ch, 3, b // 2, stats, x_rows)

            zed(0)
            phi(0)
            for b in range(NB):
                if b + 1 < NB:
                    zed(b + 1)
                    phi(b + 1)
                add(b)


        def dve_block4(v, ch):
            v.wait_ge(S("ln4"), 1)
            ch.link(v.tensor_scalar(om[:, 4:5], om[:, 0:1], 0.0, None, ALU.max))
            ch.link(v.tensor_tensor(om[:, 5:6], om[:, 4:5], om[:, 3:4], ALU.add))
            ch.link(v.tensor_scalar(wave[:, 0, 0:1], om[:, 5:6], float(np.float32(DT) ** 2) / 2, None, ALU.mult))
            for k in range(8):
                d = wave[:, 0, k:k + 1]
                ch.link(v.tensor_scalar(wave[:, 1, k:k + 1], d, -2.0, 2.0, ALU.mult, ALU.add))
                if k < 7:
                    ch.link(v.tensor_scalar(om[:, 6:7], d, -2.0, 4.0, ALU.mult, ALU.add))
                    ch.link(v.tensor_tensor(wave[:, 0, k + 1:k + 2], d, om[:, 6:7], ALU.mult))
            v.memset(wave_a[:, :, 0:P], 0.0).then_inc(S("pads4"), 1)
            v.memset(wave_b[:, :, 0:P], 0.0).then_inc(S("pads4"), 1)
            dve_var(v, ch, 4, stats)
            dve_norm(v, ch, 4, x_rows, "xn")
            src, dst = wave_a, wave_b
            NH = NB // 2
            marks = [0, 0]

            def step(h, ins):
                ch(ins)
                marks[h] = ch.n

            for k in range(7):
                s_ = 1 << k
                two_c = wave[:, 1, k:k + 1]
                for part in range(2):
                    for h in range(2):
                        q = slice(NH * h, NH * (h + 1))
                        if k == 0 and part == 0:
                            v.wait_ge(S("force4"), 2 * h + 2)
                        else:
                            v.wait_ge(S("dve_steps"), marks[h])
                        if part == 0:
                            step(h, v.scalar_tensor_tensor(out=dst[:, q, P:], in0=src[:, q, P - s_:3 * P - s_], scalar=two_c,
                                                           in1=src[:, q, P:], op0=ALU.mult, op1=ALU.add))
                        else:
                            lo = P if s_ < P // 2 else 2 * P
                            step(h, v.tensor_tensor(dst[:, q, lo:], dst[:, q, lo:], src[:, q, lo - 2 * s_:3 * P - 2 * s_],
                                                    ALU.add))
                src, dst = dst, src
            for h in range(2):
                q = slice(NH * h, NH * (h + 1))
                v.wait_ge(S("dve_steps"), marks[h])
                v.scalar_tensor_tensor(out=src[:, q, 2 * P:], in0=src[:, q, P:2 * P], scalar=wave[:, 1, 7:8],
                                       in1=src[:, q, 2 * P:], op0=ALU.mult, op1=ALU.add).then_inc(S("solved4"), 1)
            assert src is wave_b
            for c in range(NCH):
                v.wait_ge(S("v_ps4"), c + 1)
                v.tensor_tensor(x_chunk(c), x_chunk(c), bank(4 + c), ALU.add).then_inc(S("x_done4"), 1)
                v.wait_ge(S("x_done4"), c + 1)
                dve_stats(v, ch, 5, c, stats, x_rows)

        def dve_offsets(v, ch):
            v.wait_ge(S("w_moe7_in"), 16 * 5)
            for e in range(E):
                if e >= 2:
                    v.wait_ge(S("idle_ps"), e - 1)
                for k in range(KF):
                    last = v.tensor_scalar(idle[:, (e % 2) * KF + k, :], ones[:], b1_cols[:, k, e:e + 1], 0.0,
                                           ALU.mult, ALU.max)
                    ch(last)
                ch.wait()
                v.sem_inc(S("idle"), 1)
            v.wait_ge(S("idle_ps"), E)
            total = idle[:, 0, :]
            by_expert = psum[:, 6:8, :].rearrange("p b (e d) -> p d (b e)", e=4)
            ch(v.tensor_reduce(total, by_expert, AX.X, ALU.add))
            ch(v.tensor_reduce(idle[:, 1, :], b2_all[:].rearrange("p e d -> p d e"), AX.X, ALU.add))
            ch.wait()
            ch.link(v.tensor_tensor(idle[:, 2, :], total, idle[:, 1, :], ALU.add))
            for half in range(2):
                ch(v.tensor_tensor(b2_all[:, 4 * half:4 * half + 4, :],
                                   idle[:, 2:3, :].to_broadcast([P, 4, D]),
                                   bank(6 + half).rearrange("p (e d) -> p e d", e=4), ALU.subtract))
            ch.wait()
            v.sem_inc(S("offsets"), 1)

        def dve_block5(v, ch):
            dve_var(v, ch, 5, stats)
            dve_norm(v, ch, 5, x_rows, "xn")
            v.wait_ge(S("scores5"), 1)
            ch.link(v.tensor_tensor(em(7), em(0), over_i(rbias[2][:]), ALU.add))
            dve_choose(v, ch, 7, 0, 1, 1)
            ch.link(v.scalar_tensor_tensor(out=em(5), in0=em(1), scalar=NEG, in1=em(7), op0=ALU.mult, op1=ALU.add))
            dve_choose(v, ch, 5, 2, 3, 2)
            ch.link(v.tensor_tensor(rt[:, 9, :], rt[:, 1, :], rt[:, 2, :], ALU.add))
            ch.link(v.tensor_tensor(rt[:, 10, :], rt[:, 0, :], rt[:, 9, :], ALU.mult))

            def product(c, m):
                n, u = c * UNITS + m, m % 2
                v.wait_ge(S("silu5"), n + 1)
                if not (isinstance(n, int) and n < 2):
                    v.wait_ge(S("down5"), n - 1)
                v.tensor_tensor(hidt[:, u, :], hid[:, u, :], bank(4 + u), ALU.mult).then_inc(S("h5"), 1)

            def add(c, m):
                n = c * UNITS + m
                v.wait_ge(S("down5"), n + 1)
                if not (isinstance(c, int) and c == 0 and m < KF):
                    v.wait_ge(S("acc5"), c * (E + 1) + (m - KF + 1 if m >= KF else 0))
                rows = x_sb[:, bass.ds(c * TPC, TPC), :]
                if m < KF:
                    v.tensor_tensor(rows, rows, bank(3).rearrange("p (i d) -> p i d", d=D), ALU.add)\
                        .then_inc(S("acc5"), 1)
                    return
                e = m - KF
                for j in range(TPC):
                    row = x_sb[:, bass.ds(c * TPC + j, 1), :].rearrange("p o d -> p (o d)")
                    last = v.scalar_tensor_tensor(out=row, in0=bank(6 + e % 2, j * P, (j + 1) * P),
                                                  scalar=rt[:, 10, bass.ds(c * TPC + (e * NTILE + j), 1)],
                                                  in1=row, op0=ALU.mult, op1=ALU.add)
                last.then_inc(S("acc5"), 1)

            def chunk(c):
                for m in range(UNITS):
                    product(c, m)
                    if m > KF - 1 and m - 1 >= KF - 1:
                        add(c, m - 1)
                add(c, UNITS - 1)

            chunk(0)
            with v.Fori(1, NCH) as c:
                chunk(c)
            v.wait_ge(S("acc5"), NCH * (E + 1))
            v.sem_inc(S("x_done5"), NCH)
            for c in range(NCH):
                dve_stats(v, ch, 6, c, stats, x_rows)

        def dve_block6(v, ch):
            v.wait_ge(S("w6_in"), 16 * 7)
            pairs = w_qkv[:, 0:2 * D].rearrange("p (i z) -> p z i", z=2)
            turned = w_rot.rearrange("p (i z) -> p z i", z=2)
            v.tensor_scalar(turned[:, 0, :], pairs[:, 1, :], -1.0, None, ALU.mult).then_inc(S("w_rot"), 1)
            v.tensor_copy(turned[:, 1, :], pairs[:, 0, :]).then_inc(S("w_rot"), 1)
            dve_var(v, ch, 6, stats)
            dve_norm(v, ch, 6, x_rows, "xn")
            v.wait_ge(S("b_rot_ps"), 1)
            v.tensor_copy(b_rot[:], bank(7, 0, 2)).then_inc(S("b_rot"), 1)
            v.wait_ge(S("b_rot"), 1)
            both = [P, 2, L]

            def two(ap):
                return ap.rearrange("p (b t) -> p b t", t=L)

            for c in range(NCH):
                for z in range(2):
                    v.wait_ge(S("qk_ps6"), 4 * c + 2 * z + 2)
                    cos, sin = (rope[:, 2 * z + y:2 * z + y + 1, :].to_broadcast(both) for y in range(2))
                    ch(v.scalar_tensor_tensor(out=two(hid[:, z, :]), in0=two(bank(2 + 2 * z)), scalar=b_qk[:, z:z + 1],
                                              in1=cos, op0=ALU.add, op1=ALU.mult))
                    ch.link(v.scalar_tensor_tensor(out=two(hidt[:, z, :]), in0=two(bank(3 + 2 * z)),
                                                   scalar=b_rot[:, z:z + 1], in1=sin, op0=ALU.add, op1=ALU.mult))
                    v.tensor_tensor(hid[:, z, :], hid[:, z, :], hidt[:, z, :], ALU.add).then_inc(S("f6"), 1)
                for z, parts in enumerate((q_parts, k_parts)):
                    v.wait_ge(S("f6"), 2 * c + z + 1)
                    v.wait_ge(S("p0_6"), 2 * c + z + 1)
                    v.tensor_tensor(hidt[:, z, :], hid[:, z, :], parts[0][:, chunk_cols(c)], ALU.subtract)\
                        .then_inc(S("r6"), 1)
                v.wait_ge(S("v_ps6"), c + 1)
                v.wait_ge(S("xt_ps"), 6 * NCH + c + 1)
                v.tensor_tensor(xn[:, TPC * c:TPC * (c + 1), :],
                                bank(6).rearrange("p (i d) -> p i d", d=D),
                                bv6.rearrange("p (o d) -> p o d", o=1).to_broadcast([P, TPC, D]), ALU.add)\
                    .then_inc(S("v6"), 1)
                for z, (parts, done) in enumerate(((q_parts, "q6"), (k_parts, "k6"))):
                    v.wait_ge(S("r6"), 2 * c + z + 1)
                    v.wait_ge(S("p1_6"), 2 * c + z + 1)
                    v.tensor_tensor(parts[2][:, chunk_cols(c)], hidt[:, z, :], parts[1][:, chunk_cols(c)], ALU.subtract)\
                        .then_inc(S(done), 1)
                    v.wait_ge(S(done), c + 1)
            v.wait_ge(S("v6"), NCH)
            v.memset(bank(4), 0.0).then_inc(S("clear6"), 1)
            v.memset(v_seq.rearrange("p u t h d -> p (u t h d)"), 1.0).then_inc(S("v_ones"), 1)
            v.wait_ge(S("v_ones"), 1)

            def values(g, u):
                s = g * 2 + u
                if not (isinstance(s, int) and s < 2):
                    v.wait_ge(S("pv6"), s * HEADS - HEADS)
                for t in range(2):
                    last = v.tensor_scalar(v_seq[:, u, t, :, 0:HD],
                                           xn[:, bass.ds(s * 2 + t, 1), :].rearrange("p o (h d) -> p (o h) d", h=HEADS),
                                           ones[:, 0:1], None, ALU.mult)
                last.then_inc(S("v_seq6"), 1)

            def lows(g, i):
                g, i = (g + 1, i - 2 * HEADS) if i >= 2 * HEADS else (g, i)
                n = g * (2 * HEADS) + i
                if not (isinstance(n, int) and n < 4):
                    v.wait_ge(S("exp6"), n - 3)
                v.wait_ge(S("s6"), n + 1)
                v.tensor_reduce(low[:, i % 4, :], bank(i % 4).rearrange("p (t k) -> p t k", t=2), AX.X, ALU.min)\
                    .then_inc(S("low6"), 1)

            def weights(g, i):
                n = g * (2 * HEADS) + i
                v.wait_ge(S("t6"), n + 1)
                if not (isinstance(n, int) and n < 2):
                    v.wait_ge(S("pv6"), n - 1)
                v.tensor_copy(probs_t[:, i % 2, :], bank(6 + i % 2)).then_inc(S("pt6"), 1)

            def divide(s, half):
                v.wait_ge(S("tok6"), s * 2 + (half + 1))
                v.reciprocal(inv_sum[:], bank(5)[:, HD::32]).then_inc(S("inv6"), 1)
                v.wait_ge(S("inv6"), s * 2 + (half + 1))
                for t in range(2):
                    cols = slice(half * D // 2, (half + 1) * D // 2)
                    h = HEADS // 2
                    last = v.tensor_tensor(
                        xn[:, bass.ds(s * 2 + t, 1), cols].rearrange("p o (h d) -> p (o h) d", h=h),
                        bank(5, 2 * t * P, 2 * (t + 1) * P).rearrange("p (h z) -> p h z", z=32)[:, :, 0:HD],
                        inv_sum[:, t * h:(t + 1) * h].rearrange("p (h o) -> p h o", o=1).to_broadcast([P, h, HD]), ALU.mult)
                last.then_inc(S("o6"), 1)

            values(0, 0)
            values(0, 1)
            lows(0, 0)
            lows(0, 1)

            def steps(g, last=False):
                for i in range(2 * HEADS):
                    if not (last and i + 2 >= 2 * HEADS):
                        lows(g, i + 2)
                    weights(g, i)
                    if i % 8 == 4 and not (isinstance(g, int) and g == 0 and i == 4):
                        z = (i - 12) // 8
                        divide(g * 2 + z // 2, z % 2)
                    if i == HEADS + 1 and not last:
                        values(g + 1, 0)
                    if i == 1 and not (isinstance(g, int) and g == 0):
                        values(g, 1)

            steps(0)
            with v.Fori(1, NB // 2 - 1) as g:
                steps(g)
            steps(NB // 2 - 1, last=True)
            divide(NB - 1, 1)
            for c in range(NCH):
                v.wait_ge(S("proj_ps6"), c + 1)
                ch.link(v.tensor_tensor(x_chunk(c), x_chunk(c), bank(2 + c % 2), ALU.add))
                rows = x_sb[:, TPC * c:TPC * (c + 1), :]
                v.tensor_tensor(rows, rows, pb6.rearrange("p (o d) -> p o d", o=1).to_broadcast([P, TPC, D]), ALU.add)\
                    .then_inc(S("x_done6"), 1)
                v.wait_ge(S("x_done6"), c + 1)
                dve_stats(v, ch, 7, c, stats, x_rows)

        @block.vector
        def _(v):
            ch = Chain(v, "dve_steps")
            dve_block0(v, ch)
            if STAGES > 2:
                dve_rel_bias(v, ch)
            if STAGES > 1:
                dve_moe(v, ch, 1)
            if STAGES > 2:
                dve_block2(v, ch)
            if STAGES > 3:
                dve_moe(v, ch, 3)
            if STAGES > 4:
                dve_block4(v, ch)
            if STAGES > 6:
                dve_offsets(v, ch)
            if STAGES > 5:
                dve_block5(v, ch)
            if STAGES > 6:
                dve_block6(v, ch)
            if STAGES > 7:
                dve_moe(v, ch, 7)


_SHAPE = (NB, L, D)
_T = {"L0_attn_Wq", "L0_attn_Wv", "L0_attn_Wg", "L0_attn_Wo", "L2_ffn_router_w", "L2_attn_B_weight",
      "L1_attn_gamma", "L1_attn_beta", "L2_ffn_shared_w1", "L2_ffn_shared_w2", "L2_ffn_shared_w3",
      "L3_attn_qkv_w", "L3_attn_proj_w"}


def kernel(**inputs):
    import concourse.bacc as _bacc
    from concourse.bass_utils import run_bass_kernel_spmd as _run

    data = {(name + "T" if name in _T else name): (value.T if name in _T else value) for name, value in inputs.items()}
    data.update(const_bucket=bucket_rows(), const_pair=pair_matrix(), const_rope=rope_tables())
    if "L2_ffn_w12" in inputs:
        data["L2_ffn_w12T"] = inputs["L2_ffn_w12"].transpose(2, 0, 1)
        data["L2_ffn_w3T"] = inputs["L2_ffn_w3"].transpose(2, 0, 1)
    if "L3_attn_qkv_b" in inputs:
        data["L3_ffn_b1T"] = inputs["L3_ffn_b1"].T
        data["L3_attn_qkv_bT"] = inputs["L3_attn_qkv_b"].reshape(3, D).T
    nc = _bacc.Bacc("TRN2", target_bir_lowering=False, num_devices=1)
    arrays, aps = {}, {}
    for name, value in data.items():
        value = np.ascontiguousarray(value)
        arrays[f"in_{name}"] = value
        aps[name] = nc.dram_tensor(f"in_{name}", value.shape, mybir.dt.from_np(value.dtype), kind="ExternalInput").ap()
    out = nc.dram_tensor("out_x", _SHAPE, F32, kind="ExternalOutput").ap()
    build(nc, aps, out)
    r = _run(nc, [arrays], core_ids=[0])
    return r.results[0]["out_x"]
```

```python
from contextlib import ExitStack
import math

import numpy as np

import concourse.bass as bass
from concourse import mybir

F32 = mybir.dt.float32
BF16 = mybir.dt.bfloat16
I32 = mybir.dt.int32
ALU = mybir.AluOpType
ACT = mybir.ActivationFunctionType
AX = mybir.AxisListType

P = 128
D = 128
NB, L = 8, 256
T = NB * L
NTILE = T // P
CH = 512
NCH = T // CH
TPC = CH // P
E = 8
FF = 512
KF = FF // P
EPS = 1e-5
NEG = -3.0e38
HEADS, HD = 16, 8
Q_TERMS = (0, 0, 1, 1, 0, 2)
K_TERMS = (0, 1, 0, 1, 2, 0)
UNITS = KF + E
RH = 16
DT = 0.1

NBUCKET, MAX_DISTANCE = 32, 128
BIASW = 3 * P
ROUND128 = 1.5 * 2.0 ** 30
MU, STD = math.sqrt(0.5), math.sqrt(0.25 * math.pi)
TINY = 1e-30


def rope_tables():
    inv = 1.0 / 10000.0 ** (np.arange(0, HD, 2, dtype=np.float32) / HD)
    ang = np.arange(L, dtype=np.float32)[None, :] * np.concatenate([inv, inv]).astype(np.float32)[:, None]
    cos, sin = (np.tile(f(ang).astype(np.float32), (HEADS, 1)) for f in (np.cos, np.sin))
    scale = np.float32(HD ** -0.5)
    return np.ascontiguousarray(np.stack([-cos * scale, -sin * scale, cos, sin], axis=1))


def pair_matrix():
    m = np.zeros((P, P), np.float32)
    for i in range(0, P, 2):
        m[i + 1, i], m[i, i + 1] = -1.0, 1.0
    return m


def bucket_rows():
    n = np.maximum(np.arange(BIASW) - (P - 1), 0)
    exact = NBUCKET // 2
    ratio = (np.log(np.maximum(n, 1).astype(np.float32) / np.float32(exact))
             / np.float32(math.log(MAX_DISTANCE / exact)) * np.float32(NBUCKET - exact))
    large = np.minimum(exact + ratio.astype(np.int32), NBUCKET - 1)
    b = np.where(n < exact, n, large)
    return (b[None, :] == np.arange(NBUCKET)[:, None]).astype(np.float32)


def moe_tiles(k):
    n = k * T // P + E
    return (n + 3) // 4 * 4


def build(nc, a, out):
    ctx = ExitStack()

    def sb(name, shape, dt=F32):
        return ctx.enter_context(nc.sbuf_tensor(name, shape, dt))

    sems = {}

    def S(name):
        if name not in sems:
            sems[name] = ctx.enter_context(nc.semaphore(name))
        return sems[name]

    with ctx:
        x_sb = sb("x_sb", [P, NTILE, D])
        xn = sb("xn", [P, NTILE, D])
        xt = sb("xt", [P, T])
        buf_a = sb("buf_a", [P, T])
        buf_b = sb("buf_b", [P, T])
        buf_c = sb("buf_c", [P, T])
        ident = sb("ident", [P, P])
        ones = sb("ones", [P, P])
        before = sb("before", [P, P])
        stats = sb("stats", [P, NTILE, 6])
        stats2 = sb("stats2", [P, NTILE, 6])
        lnt = sb("lnt", [P, 8, NTILE])
        psum = ctx.enter_context(nc.psum_tensor("psum", [P, 8, CH], F32))

        w_q = sb("w_q", [P, D])
        w_v = sb("w_v", [P, D])
        w_g = sb("w_g", [P, D])
        w_o = sb("w_o", [P, D])
        state = sb("state", [P, CH])
        lam_col = sb("lam_col", [P, 4])
        lam = sb("lam", [P, L])
        gb = sb("gb", [P, 2])

        w_qk1 = sb("w_qk1", [P, D])
        w_v1 = sb("w_v1", [P, D])
        cols1 = sb("cols1", [P, 5])
        bv1 = sb("bv1", [P, D])
        table = sb("table", [NBUCKET, 1])
        table_all = sb("table_all", [NBUCKET, P])
        bucket = sb("bucket", [NBUCKET, BIASW])
        bias_row = sb("bias_row", [P, BIASW])
        rel = sb("rel", [P, L])
        causal = sb("causal", [P, P])
        att = sb("att", [P, 3, 2, 3 * P])
        att_z, att_g, att_r = (att[:, z] for z in range(3))

        w_b2 = sb("w_b2", [P, D])
        om = sb("om", [P, 8])
        wave = sb("wave", [P, 2, 8])

        w1_a = sb("w1_a", [P, E, FF])
        w2_a = sb("w2_a", [P, E, KF, D])
        w1_b = sb("w1_b", [P, E, FF])
        w2_b = sb("w2_b", [P, E, KF, D])
        b1_all = sb("b1_all", [P, E, FF])
        b2_all = sb("b2_all", [P, E, D])
        b1_cols = sb("b1_cols", [P, KF, E])
        idle = att[:].rearrange("p z u t -> p (z u t)")[:, 0:2 * KF * P].rearrange("p (k d) -> p k d", d=P)
        wave_a = w1_b[:].rearrange("p e f -> p (e f)")[:, 0:NB * 3 * P].rearrange("p (b t) -> p b t", b=NB)
        wave_b = w2_b[:].rearrange("p e k d -> p (e k d)")[:, 0:NB * 3 * P].rearrange("p (b t) -> p b t", b=NB)
        q_slab = w1_b[:].rearrange("p e f -> p (e f)").bitcast(BF16).rearrange("p (u h t) -> p u h t", u=2, h=HEADS)
        k_slab = w2_b[:].rearrange("p e k d -> p (e k d)").bitcast(BF16).rearrange("p (u h t) -> p u h t", u=2, h=HEADS)
        q_parts = [buf[:].bitcast(BF16)[:, T * z:T * (z + 1)] for buf, z in ((buf_a, 0), (buf_a, 1), (buf_b, 0))]
        k_parts = [buf[:].bitcast(BF16)[:, T * z:T * (z + 1)] for buf, z in ((buf_b, 1), (buf_c, 0), (buf_c, 1))]

        off_sum = sb("off_sum", [P, D])
        w5 = sb("w5", [P, E * 3 * P + 3 * FF])
        w12 = w5[:, 0:E * 2 * P].rearrange("p (e h) -> p e h", e=E)
        w3 = w5[:, E * 2 * P:E * 3 * P].rearrange("p (e d) -> p e d", e=E)
        w_s1, w_s2 = (w5[:, E * 3 * P + z * FF:E * 3 * P + (z + 1) * FF] for z in range(2))
        w_s3 = w5[:, E * 3 * P + 2 * FF:].rearrange("p (k d) -> p k d", k=KF)
        probs_t = w5[:, 0:2 * CH].rearrange("p (u t) -> p u t", u=2)
        heads_t = w5[:, 4 * CH:6 * CH].rearrange("p (z t) -> p z t", z=2)
        v_seq = w5[:, 6 * CH:6 * CH + 4 * HEADS * (HD + 1)].rearrange("p (u t h d) -> p u t h d", u=2, t=2, h=HEADS)

        own6 = att[:].rearrange("p z u t -> p (z u t)")
        rope = own6[:, 0:4 * L].rearrange("p (z t) -> p z t", z=4)
        own6 = own6[:, 4 * L:4 * L + 8 * D]
        w_qkv, w_rot = own6[:, 0:3 * D], own6[:, 3 * D:5 * D]
        bv6, pb6, w_p6 = (own6[:, z * D:(z + 1) * D] for z in (5, 6, 7))
        b_qk = sb("b_qk", [P, 3])
        b_rot = sb("b_rot", [P, 2])
        pair_turn = sb("pair_turn", [P, P])
        low = sb("low", [P, 4, 2])
        inv_sum = sb("inv_sum", [P, HEADS])
        wr = [sb(f"wr{n}", [P, E]) for n in range(4)]
        rbias = [None] + [sb(f"rbias{n}", [P, E]) for n in (1, 2, 3)]

        desc = sb("desc", [P, E])
        thr = sb("thr", [P, 40])
        col_no = sb("col_no", [P, P])
        row_no = sb("row_no", [P, 1])
        tile_seq = sb("tile_seq", [P, 2 * NTILE])
        past = sb("past", [P, 40])
        tile_no = sb("tile_no", [1, 44])
        rt = sb("rt", [P, 24, E * NTILE])
        rs = sb("rs", [P, 24, NTILE])
        row_f = sb("row_f", [P, 4, 40])
        row_in = sb("row_in", [P, 40], I32)
        row_out = sb("row_out", [P, 40], I32)
        place_hot = buf_c[:].bitcast(BF16).rearrange("p (i s) -> p i s", s=P)
        tile_hot = xt[:].bitcast(BF16)[:, 0:3 * 2 * NTILE * 40].rearrange("p (z i j) -> p z i j", z=3, j=40)
        eid_f = sb("eid_f", [1, 44, E])
        eid_s = sb("eid_s", [1, 2, 44])
        packed_f = sb("packed_f", [1, 4, 10])
        packed = sb("packed", [1, 10], I32)

        xs = sb("xs", [P, 4, D])
        xst = sb("xst", [P, 2, P])
        hid = sb("hid", [P, 2, FF])
        hidt = sb("hidt", [P, 2, FF])
        ys = sb("ys", [P, 4, D])

        def probs(i):
            return (hid, hidt)[i // 2 % 2][:, i % 2, :]

        q_dram = nc.dram_tensor("q_dram", [3, D, T], BF16, kind="Internal").ap()
        k_dram = nc.dram_tensor("k_dram", [3, D, T], BF16, kind="Internal").ap()
        bias_dram = nc.dram_tensor("bias_dram", [P * BIASW], F32, kind="Internal").ap()
        x_rows_dram = nc.dram_tensor("x_rows_dram", [P + T, D], F32, kind="Internal").ap()
        y_rows = nc.dram_tensor("y_rows", [P + 2 * T + 4 * P, D], F32, kind="Internal").ap()

        def bank(n, lo=0, hi=CH):
            return psum[:, n, lo:hi]

        def tile_cols(i):
            return slice(i * P, (i + 1) * P)

        def chunk_cols(c):
            return slice(c * CH, (c + 1) * CH)

        def em(r):
            return rt[:, r, :].rearrange("p (e i) -> p e i", e=E)

        def by_tile(r):
            return rt[:, r, :].rearrange("p (e i) -> p i e", e=E)

        def over_e(ap):
            return ap.rearrange("p (o i) -> p o i", o=1).to_broadcast([P, E, NTILE])

        def over_i(ap):
            return ap.rearrange("p (e o) -> p e o", o=1).to_broadcast([P, E, NTILE])

        def x_rows(i):
            return x_sb[:, i, :]

        def x_chunk(c):
            return x_sb[:, TPC * c:TPC * (c + 1), :].rearrange("p i d -> p (i d)")

        x_flat = a["L0_attn_x"].rearrange("b l d -> (b l) d").rearrange("(i p) d -> p i d", p=P)
        out_flat = out.rearrange("b l d -> (b l) d").rearrange("(i p) d -> p i d", p=P)

        CONSTS = 12

        block = ctx.enter_context(nc.Block())

        class Chain:
            def __init__(self, eng, name):
                self.eng, self.sem, self.n = eng, S(name), 0

            def __call__(self, ins):
                ins.then_inc(self.sem, 1)
                self.n += 1

            def wait(self):
                self.eng.wait_ge(self.sem, self.n)

            def link(self, ins):
                self(ins)
                self.wait()

        BY_ACT = (2, 4, 6)

        def copied(g, i):
            if i < 0:
                g, i = g - 1, i + 2 * HEADS
            own = [h for h in range(8) if (h in BY_ACT) == (i % 8 in BY_ACT)]
            count = i // 8 * len(own) + sum(h <= i % 8 for h in own)
            return S("pt_act6" if i % 8 in BY_ACT else "pt_dve6"), g * (4 * len(own)) + count

        BY_CHUNK = (2,)

        def norm_no(n, tag="x", c=0):
            return 1 + c + (n > 0 or tag == "r") + sum(NCH if m in BY_CHUNK else 1 for m in range(n))

        moe_cfg = {
            1: dict(k=2, w1=w1_a, w2=w2_a, bias=True, act=ACT.Relu, r=0),
            3: dict(k=1, w1=w1_b, w2=w2_b, bias=False, act=ACT.Gelu, r=1),
            7: dict(k=1, w1=w1_a, w2=w2_a, bias=True, act=ACT.Relu, r=3),
        }

        moe_cfg[1].update(order=1, t0=0, k0=0)
        moe_cfg[3].update(order=2, t0=moe_tiles(2), k0=2)
        moe_cfg[7].update(order=3, t0=moe_tiles(2) + moe_tiles(1), k0=3)

        def sp_moe(sp, n):
            k, k0, nt, t0 = moe_cfg[n]["k"], moe_cfg[n]["k0"], moe_tiles(moe_cfg[n]["k"]), moe_cfg[n]["t0"]

            for c in range(NCH):
                sp.wait_ge(S("xn"), NTILE * n + TPC * (c + 1))
                sp.dma_start(x_rows_dram[P + c * CH:P + (c + 1) * CH, :].rearrange("(i p) d -> p i d", p=P),
                             xn[:, TPC * c:TPC * (c + 1), :]).then_inc(S("x_out"), 16)
            for u in range(4):
                sp.wait_ge(S(f"y_out{u}"), (t0 + nt) * 4)
            for c in range(NCH):
                for kk in range(k):
                    dst = (buf_a, buf_b)[kk][:, chunk_cols(c)].rearrange("p (i d) -> p i d", d=D)
                    src = y_rows[P + kk * T + c * CH:P + kk * T + (c + 1) * CH, :].rearrange("(i p) d -> p i d", p=P)
                    sp.dma_start(dst, src).then_inc(S(f"back{c}"), 16)

        def sp_block6(sp):
            def leave(c):
                for name, parts, dram in (("q6", q_parts, q_dram), ("k6", k_parts, k_dram)):
                    sp.wait_ge(S(name), c + 1)
                    for part in range(3):
                        sp.dma_start(dram[part, :, chunk_cols(c)], parts[part][:, chunk_cols(c)]).then_inc(S("qk_out"), 16)

            def load(s, u):
                for slab, dram, terms in ((q_slab, q_dram, Q_TERMS), (k_slab, k_dram, K_TERMS)):
                    for t, part in enumerate(terms):
                        sp.dma_start(slab[HD * t:HD * (t + 1), u, :, :],
                                     dram[part][:, bass.ds(s * L, L)].rearrange("(h d) t -> d h t", d=HD))\
                            .then_inc(S(f"slab_in{u}"), 16)

            leave(0)
            sp.wait_ge(S("slab_zero"), 2)
            sp.wait_ge(S("qk_out"), 16 * 6)
            load(0, 0)
            load(1, 1)
            for c in range(1, NCH):
                leave(c)
            sp.wait_ge(S("qk_out"), 16 * 6 * NCH)
            with sp.Fori(1, NB // 2) as g:
                for u in range(2):
                    sp.wait_ge(S("s6"), g * (2 * HEADS) - (1 - u) * HEADS)
                    load(g * 2 + u, u)

        @block.sync
        def _(sp):
            for c in range(NCH):
                sp.dma_start(x_sb[:, TPC * c:TPC * (c + 1), :], x_flat[:, TPC * c:TPC * (c + 1), :])\
                    .then_inc(S(f"x_in{c}"), 16)
            for name, w in (("L0_attn_WqT", w_q), ("L0_attn_WvT", w_v), ("L0_attn_WgT", w_g), ("L0_attn_WoT", w_o)):
                sp.dma_start(w[:], a[name]).then_inc(S("w0_in"), 16)
            for col, name in enumerate(("L0_attn_ln_gamma", "L0_attn_ln_beta")):
                sp.dma_start(gb[:, col:col + 1], a[name].rearrange("(p o) -> p o", o=1)).then_inc(S("w0_in"), 16)
            sp.dma_start(wr[0][:], a["L0_ffn_Wg"]).then_inc(S("wr_in"), 16)
            sp.dma_start(wr[1][:], a["L1_ffn_Wr"]).then_inc(S("wr_in"), 16)
            sp.dma_start(wr[2][:], a["L2_ffn_router_wT"]).then_inc(S("wr_in"), 16)
            sp.dma_start(wr[3][:], a["L3_ffn_Wr"]).then_inc(S("wr_in"), 16)
            for n, name in ((1, "L1_ffn_br"), (2, "L2_ffn_expert_bias"), (3, "L3_ffn_br")):
                sp.dma_start(rbias[n][:], a[name].rearrange("(o e) -> o e", o=1).to_broadcast([P, E]))\
                    .then_inc(S("wr_in"), 16)
            sp.dma_start(w_qk1[:], a["L1_attn_wqk"]).then_inc(S("w2_in"), 16)
            sp.dma_start(w_v1[:], a["L1_attn_wv"]).then_inc(S("w2_in"), 16)
            sp.dma_start(cols1[:, 0:1], a["L1_attn_bqk"].rearrange("(p o) -> p o", o=1)).then_inc(S("w2_in"), 16)
            sp.dma_start(cols1[:, 1:3], a["L1_attn_gammaT"]).then_inc(S("w2_in"), 16)
            sp.dma_start(cols1[:, 3:5], a["L1_attn_betaT"]).then_inc(S("w2_in"), 16)
            sp.dma_start(bv1[:], a["L1_attn_bv"].rearrange("(o d) -> o d", o=1).to_broadcast([P, D])).then_inc(S("w2_in"), 16)
            sp.dma_start(table[:], a["L1_attn_rel_bias"].rearrange("(b o) -> b o", o=1)).then_inc(S("w2_in"), 16)
            sp.dma_start(bucket[:], a["const_bucket"]).then_inc(S("w2_in"), 16)
            sp.dma_start(w1_a[:], a["L0_ffn_W1"].rearrange("e p f -> p e f")).then_inc(S("w_moe1_in"), 16)
            sp.dma_start(w2_a[:], a["L0_ffn_W2"].rearrange("e (k p) d -> p e k d", p=P)).then_inc(S("w_moe1_in"), 16)
            sp.dma_start(b1_all[:], a["L0_ffn_b1"].rearrange("(o e) f -> o e f", o=1).to_broadcast([P, E, FF]))\
                .then_inc(S("w_moe1_in"), 16)
            sp.dma_start(b2_all[:], a["L0_ffn_b2"].rearrange("(o e) f -> o e f", o=1).to_broadcast([P, E, D]))\
                .then_inc(S("w_moe1_in"), 16)
            sp.dma_start(w1_b[:], a["L1_ffn_W1"].rearrange("e p f -> p e f")).then_inc(S("w_moe3_in"), 16)
            sp.dma_start(w2_b[:], a["L1_ffn_W2"].rearrange("e (k p) d -> p e k d", p=P)).then_inc(S("w_moe3_in"), 16)
            sp.dma_start(w_b2[:], a["L2_attn_B_weightT"]).then_inc(S("w4_in"), 16)
            sp.dma_start(om[:, 0:1], a["L2_attn_omega_raw"].rearrange("(p o) -> p o", o=1)).then_inc(S("w4_in"), 16)
            for dst, name in ((w12[:], "L2_ffn_w12T"), (w3[:], "L2_ffn_w3T"), (w_s1[:], "L2_ffn_shared_w1T"),
                              (w_s2[:], "L2_ffn_shared_w2T"),
                              (w_s3[:], a["L2_ffn_shared_w3T"].rearrange("(k p) d -> p k d", p=P))):
                sp.dma_start(dst, a[name] if isinstance(name, str) else name).then_inc(S("w5_in"), 16)
            sp.wait_ge(S("consts"), CONSTS)
            sp.dma_start(x_rows_dram[0:P, :], ones[:]).then_inc(S("x_out"), 16)
            sp.wait_ge(S("bias_row"), 1)
            sp.dma_start(bias_dram.rearrange("(p m) -> p m", m=BIASW), bias_row[:]).then_inc(S("bias_out"), 16)
            sp.wait_ge(S("bias_out"), 16)
            skew = bias_dram[P - 1:P - 1 + P * (BIASW - 1)].rearrange("(p m) -> p m", m=BIASW - 1)
            sp.dma_start(rel[:], skew[:, 0:L]).then_inc(S("rel_in"), 16)
            sp_moe(sp, 1)
            for dst, src in ((w1_a[:], a["L3_ffn_W1"].rearrange("e p f -> p e f")),
                             (w2_a[:], a["L3_ffn_W2"].rearrange("e (k p) d -> p e k d", p=P)),
                             (b1_all[:], a["L3_ffn_b1"].rearrange("(o e) f -> o e f", o=1).to_broadcast([P, E, FF])),
                             (b2_all[:], a["L3_ffn_b2"].rearrange("(o e) d -> o e d", o=1).to_broadcast([P, E, D])),
                             (b1_cols[:], a["L3_ffn_b1T"].rearrange("(k p) e -> p k e", p=P))):
                sp.dma_start(dst, src).then_inc(S("w_moe7_in"), 16)
            sp_moe(sp, 3)
            sp.wait_ge(S("offsets"), 1)
            for dst, src in ((w_qkv, a["L3_attn_qkv_wT"]), (b_qk[:], a["L3_attn_qkv_bT"]), (pair_turn[:], a["const_pair"]),
                             (rope, a["const_rope"]),
                             (bv6, a["L3_attn_qkv_b"][2 * D:3 * D].rearrange("(o d) -> o d", o=1).to_broadcast([P, D])),
                             (pb6, a["L3_attn_proj_b"].rearrange("(o d) -> o d", o=1).to_broadcast([P, D])),
                             (w_p6, a["L3_attn_proj_wT"])):
                sp.dma_start(dst, src).then_inc(S("w6_in"), 16)
            sp_block6(sp)
            sp_moe(sp, 7)
            for c in range(NCH):
                sp.wait_ge(S("x_done7"), c + 1)
                sp.dma_start(out_flat[:, TPC * c:TPC * (c + 1), :], x_sb[:, TPC * c:TPC * (c + 1), :])\
                    .then_inc(S("stored"), 16)
            sp.wait_ge(S("stored"), 16 * NCH)
            sp.wait_ge(S("x_out"), 16)

        def pool_moe(gp, n):
            cfg = moe_cfg[n]
            nt, t0, order = moe_tiles(cfg["k"]), cfg["t0"], cfg["order"]

            def gather(j):
                if j >= 4:
                    gp.wait_ge(S("moe_xst_ps"), t0 + j - 3)
                gp.indirect_dma_start(
                    out=xs[:, j % 4, :], out_offset=None, in_=x_rows_dram[:, :],
                    in_offset=bass.IndirectOffsetOnAxis(ap=row_in[:, j:j + 1], axis=0)).then_inc(S(f"xs_in{j % 4}"), 16)

            def send(j):
                gp.wait_ge(S("moe_y_sb"), t0 + j + 1)
                if j >= 4:
                    gp.wait_ge(S(f"y_out{j % 4}"), t0 * 4 + j // 4 * 16)
                gp.indirect_dma_start(
                    out=y_rows[:, :], out_offset=bass.IndirectOffsetOnAxis(ap=row_out[:, j:j + 1], axis=0),
                    in_=ys[:, j % 4, :], in_offset=None).then_inc(S(f"y_out{j % 4}"), 16)

            gp.wait_ge(S("x_out"), 16 + 16 * NCH * order)
            gp.wait_ge(S("row_ids"), 2 * order)
            ahead = 6
            for j in range(ahead):
                gather(j)
            for j in range(nt):
                if j + ahead < nt:
                    gather(j + ahead)
                send(j)

        def pool_block2(gp):
            for b in range(NB):
                gp.wait_ge(S("gelu2"), b + 1)
                for lo in (0, L):
                    part = att_g[:, b % 2, lo:lo + P]
                    gp.tensor_tensor(part, part, causal[:], ALU.mult).then_inc(S("masked2"), 1)

        def pool_block4(gp):
            gp.memset(wave_a[:, :, 0:P], 0.0).then_inc(S("pads4"), 1)
            gp.memset(wave_b[:, :, 0:P], 0.0).then_inc(S("pads4"), 1)

        def pool_block6(gp):
            gp.wait_ge(S("x_done4"), NCH)
            gp.memset(q_slab.rearrange("p u h t -> p (u h t)"), 0.0).then_inc(S("slab_zero"), 1)
            gp.memset(k_slab.rearrange("p u h t -> p (u h t)"), 0.0).then_inc(S("slab_zero"), 1)

        @block.gpsimd
        def _(gp):
            gp.memset(ident[:], 0.0).then_inc(S("consts"), 1)
            gp.memset(ones[:], 1.0).then_inc(S("consts"), 1)
            gp.wait_ge(S("consts"), 2)
            gp.affine_select(out=ident[:], in_=ident[:], compare_op=ALU.not_equal, fill=1.0, base=0,
                             pattern=[[-1, P]], channel_multiplier=1).then_inc(S("consts"), 1)
            gp.affine_select(out=before[:], in_=ones[:], compare_op=ALU.is_gt, fill=0.0, base=0,
                             pattern=[[1, P]], channel_multiplier=-1).then_inc(S("consts"), 1)
            gp.affine_select(out=causal[:], in_=ones[:], compare_op=ALU.is_ge, fill=0.0, base=0,
                             pattern=[[1, P]], channel_multiplier=-1).then_inc(S("consts"), 1)
            gp.iota(desc[:], [[-1, E]], base=E, channel_multiplier=0, allow_small_or_imprecise_dtypes=True)\
                .then_inc(S("consts"), 1)
            for dst, pattern, base, step in ((thr[:], [[P, 40]], 0, 0), (col_no[:], [[1, P]], 0, 0), (row_no[:], [[0, 1]], 0, 1),
                                             (tile_seq[:], [[1, 2 * NTILE]], 1, 0), (past[:], [[0, 10], [P, 4]], P + 2 * T, 1)):
                gp.iota(dst, pattern, base=base, channel_multiplier=step, allow_small_or_imprecise_dtypes=True)\
                    .then_inc(S("consts"), 1)
            gp.iota(tile_no[:], [[1, 44]], base=-1, channel_multiplier=0, allow_small_or_imprecise_dtypes=True)\
                .then_inc(S("consts"), 1)
            gp.dma_start(lam_col[:, 0:1], a["L0_attn_beta"].rearrange("(h o) -> h o", o=1).to_broadcast([RH, D // RH]))\
                .then_inc(S("lam_in"), 16)
            pool_moe(gp, 1)
            pool_block2(gp)
            pool_moe(gp, 3)
            pool_block4(gp)
            pool_block6(gp)
            pool_moe(gp, 7)

        def act_norm(act, n, tag="x", c=None):
            act.wait_ge(S("var"), norm_no(n, tag, c or 0))
            i = slice(0, NTILE) if c is None else slice(TPC * c, TPC * (c + 1))
            act.activation(lnt[:, 7, i], lnt[:, 6, i], ACT.Sqrt).then_inc(S("sd"), 1)

        def act_head(act, n):
            if n not in BY_CHUNK:
                act_norm(act, n)
            elif n not in (2, 4):
                for c in range(NCH - 1):
                    act_norm(act, n, c=c)
            act_xt(act, n, 0)
            if n in BY_CHUNK:
                act_norm(act, n, c=NCH - 1)

        def act_xt(act, n, c):
            act.wait_ge(S("xt_ps"), NCH * n + c + 1)
            act.activation(xt[:, chunk_cols(c)], bank(c % 2), ACT.Copy).then_inc(S("xt"), 1)

        def act_block0(act):
            act_norm(act, 0)

            def silu(c):
                act.wait_ge(S("g_ps"), c + 1)
                act.activation(buf_a[:, chunk_cols(c)], bank(4), ACT.Silu).then_inc(S("gate"), 1)

            def ret_rows(c):
                act.wait_ge(S("ret_ps"), c + 1)
                act.activation(buf_c[:, chunk_cols(c)], bank(5), ACT.Copy).then_inc(S("ret_rows"), 1)

            act_xt(act, 0, 0)
            for c in range(NCH):
                if c + 1 < NCH:
                    act_xt(act, 0, c + 1)
                silu(c)
                if c >= 1:
                    ret_rows(c - 1)
            ret_rows(NCH - 1)
            act_norm(act, 0, "r")
            for c in range(NCH):
                act.wait_ge(S("rn_ps"), c + 1)
                act.activation(buf_b[:, chunk_cols(c)], bank(c % 2), ACT.Identity, scale=gb[:, 0:1], bias=gb[:, 1:2])\
                    .then_inc(S("rn"), 1)

        def act_moe(act, n):
            cfg = moe_cfg[n]
            nt, t0 = moe_tiles(cfg["k"]), cfg["t0"]
            act_norm(act, n)
            for c in range(NCH):
                act_xt(act, n, c)
            if n == 1:
                act.wait_ge(S("gap1"), 1)
                act.activation(rs[:, 11, :], rs[:, 10, :], ACT.Exp).then_inc(S("gap_exp1"), 1)
            if n == 3:
                act.wait_ge(S("logits3"), 1)
                act.activation(rt[:, 0, :], rt[:, 7, :], ACT.Sigmoid).then_inc(S("scores3"), 1)

            used, order = NTILE * cfg["k"], cfg["order"]
            act.wait_ge(S("tile_hot"), moe_cfg[n]["order"])
            act.activation(tile_hot[:, 2, 0:used, 0:nt], tile_hot[:, 0, 0:used, 0:nt], ACT.Copy, scale=row_no[:, 0:1])\
                .then_inc(S("hot_row"), 1)
            if n == 1:
                act_omega(act)

            def rows(j, u):
                act.wait_ge(S("moe_xst_ps"), j + (t0 + 1))
                if not (isinstance(j, int) and j < 2):
                    act.wait_ge(S("moe_h_ps"), j + (t0 - 1))
                act.activation(xst[:, u, :], bank(u, 0, P), ACT.Copy).then_inc(S("moe_xst"), 1)

            def hidden(j, u):
                act.wait_ge(S("moe_ht_ps"), j + (t0 + 1))
                if not (isinstance(j, int) and j < 2):
                    act.wait_ge(S("moe_y_ps"), j + (t0 - 1))
                act.activation(hidt[:, u, :], bank(4 + u), cfg["act"]).then_inc(S("moe_ht"), 1)

            rows(0, 0)
            rows(1, 1)

            def steps(g, last=False):
                for u in range(4):
                    j = g * 4 + u
                    if not (last and u >= 2):
                        rows(j + 2, u % 2)
                    hidden(j, u % 2)

            steps(0)
            with act.Fori(1, nt // 4 - 1) as g:
                steps(g)
            steps(nt // 4 - 1, last=True)
            if n != 7:
                act.wait_ge(S("shares"), order)
                for c in range(NCH):
                    if c >= 2 and n + 1 in BY_CHUNK:
                        act_norm(act, n + 1, c=c - 2)
                    act.wait_ge(S(f"back{c}"), 16 * (cfg["k0"] + cfg["k"]))
                    for kk in range(cfg["k"]):
                        for i in range(TPC * c, TPC * (c + 1)):
                            buf = (buf_a, buf_b)[kk][:, tile_cols(i)]
                            last = act.activation(buf, buf, ACT.Copy, scale=rs[:, 14 + kk, i:i + 1])
                        last.then_inc(S("scaled"), 1)
                if n + 1 in BY_CHUNK:
                    act_norm(act, n + 1, c=2)

        def act_block2(act):

            def qk(c):
                if c >= 2:
                    act.wait_ge(S("k2"), c - 1)
                act.wait_ge(S("qk_ps2"), c + 1)
                act.activation(hid[:, c % 2, :], bank(2 + c % 2), ACT.Silu, bias=cols1[:, 0:1]).then_inc(S("qk2"), 1)

            def values(c):
                act.wait_ge(S("v_lin2"), c + 1)
                act.activation(buf_c[:, chunk_cols(c)], hidt[:, c % 2, :], ACT.Silu).then_inc(S("v2"), 1)

            act_head(act, 2)
            for c in range(NCH):
                if c + 1 < NCH:
                    act_xt(act, 2, c + 1)
                qk(c)
                if c >= 1:
                    values(c - 1)
            values(NCH - 1)
            for b in range(NB):
                if b >= 2:
                    act.wait_ge(S("phi2"), b - 1)
                act.wait_ge(S("z2"), b + 1)
                act.activation(att_g[:, b % 2, :], att_z[:, b % 2, :], ACT.Gelu).then_inc(S("gelu2"), 1)

        def act_omega(act):
            act.wait_ge(S("w4_in"), 16 * 2)
            act.activation(om[:, 1:2], om[:, 0:1], ACT.Abs).then_inc(S("abs4"), 1)
            act.wait_ge(S("abs4"), 1)
            act.activation(om[:, 2:3], om[:, 1:2], ACT.Exp, scale=-1.0).then_inc(S("exp4"), 1)
            act.wait_ge(S("exp4"), 1)
            act.activation(om[:, 3:4], om[:, 2:3], ACT.Ln, bias=1.0).then_inc(S("ln4"), 1)

        def act_block4(act):
            act_head(act, 4)
            for c in range(NCH):
                if c + 1 < NCH:
                    act_xt(act, 4, c + 1)
                if c == 0:
                    act.wait_ge(S("pads4"), 2)
                act.wait_ge(S("force_ps4"), c + 1)
                act.activation(wave_a[:, 2 * c:2 * c + 2, P:], bank(2 + c % 2).rearrange("p (b t) -> p b t", t=L),
                               ACT.Copy, scale=float(np.float32(DT) ** 2)).then_inc(S("force4"), 1)

        def act_offsets(act):
            act.wait_ge(S("w_moe7_in"), 16 * 5)
            for e in range(E):
                if e >= 2:
                    act.wait_ge(S("idle_ps"), e - 1)
                for k in range(KF):
                    last = act.activation(idle[:, (e % 2) * KF + k, :], ones[:], ACT.Relu, scale=b1_cols[:, k, e:e + 1])
                last.then_inc(S("idle"), 1)

        def act_proj6(act):
            for c in range(NCH):
                act.wait_ge(S("ot_ps6"), c + 1)
                act.activation(buf_a[:, chunk_cols(c)], bank(c % 2), ACT.Copy).then_inc(S("ot6"), 1)

        def act_block5(act):
            act_head(act, 5)
            for c in range(1, NCH):
                act_xt(act, 5, c)
            act.wait_ge(S("logit_ps"), 3)
            act.activation(em(0), bank(2, 0, NTILE * E).rearrange("p (i e) -> p e i", e=E), ACT.Sigmoid)\
                .then_inc(S("scores5"), 1)

            def chunk(c):
                for m in range(UNITS):
                    n, u = UNITS * c + m, m % 2
                    if not (isinstance(c, int) and n < 2):
                        act.wait_ge(S("h5"), n - 1)
                    act.wait_ge(S("up5"), n + 1)
                    act.activation(hid[:, u, :], bank(u), ACT.Silu).then_inc(S("silu5"), 1)

            chunk(0)
            with act.Fori(1, NCH) as c:
                chunk(c)

        def act_block6(act):
            act_head(act, 6)
            for c in range(NCH):
                if c + 1 < NCH:
                    act_xt(act, 6, c + 1)
                for src, part, ready, done in ((hid, 0, "f6", "p0_6"), (hidt, 1, "r6", "p1_6")):
                    for z, parts in enumerate((q_parts, k_parts)):
                        act.wait_ge(S(ready), 2 * c + z + 1)
                        act.activation(parts[part][:, chunk_cols(c)], src[:, z, :], ACT.Copy).then_inc(S(done), 1)

            def steps(g, first=False):
                for i in range(2 * HEADS):
                    n = g * (2 * HEADS) + i
                    act.wait_ge(S("low6"), n + 1)
                    if not (first and i < 4):
                        act.wait_ge(S("t6"), n - 3)
                    for t in range(2):
                        last = act.activation(probs(i)[:, t * L:(t + 1) * L], bank(i % 4, t * L, (t + 1) * L), ACT.Exp,
                                              scale=-1.0, bias=low[:, i % 4, t:t + 1])
                    last.then_inc(S("exp6"), 1)
                    if (i - 1) % 8 in BY_ACT:
                        act.wait_ge(S("t6"), n)
                        if not (first and i < 3):
                            act.wait_ge(S("pv6"), n - 2)
                        act.activation(probs_t[:, (i - 1) % 2, :], bank(6 + (i - 1) % 2), ACT.Copy)\
                            .then_inc(S("pt_act6"), 1)
                    if i % 8 == 1 and not (first and i == 1):
                        z = (i - 9) // 8
                        leave(g * 2 + z // 2, z % 2, n - 1)

            def leave(s, half, heads):
                act.wait_ge(S("pv6"), heads)
                if not (isinstance(s, int) and s < 1):
                    act.wait_ge(S("tok6"), s * 2 + (half - 1))
                act.activation(heads_t[:, half, :], bank(4), ACT.Copy).then_inc(S("heads6"), 1)

            steps(0, first=True)
            with act.Fori(1, NB // 2) as g:
                steps(g)
            leave(NB - 1, 1, NB * HEADS)

        @block.scalar
        def _(act):
            act.wait_ge(S("lam_in"), 16)
            act.activation(lam_col[:, 1:2], lam_col[:, 0:1], ACT.Exp, scale=-math.log(2.0)).then_inc(S("lam_exp"), 1)
            act_block0(act)
            act_moe(act, 1)
            act_block2(act)
            act_moe(act, 3)
            act_block4(act)
            act_offsets(act)
            act_block5(act)
            act_block6(act)
            act_proj6(act)
            act_moe(act, 7)

        def pe_xt(pe, n, c):
            pe.wait_ge(S("xn"), NTILE * n + TPC * (c + 1))
            if c >= 2:
                pe.wait_ge(S("xt"), NCH * n + c - 1)
            for j in range(TPC):
                last = pe.transpose(bank(c % 2, j * P, (j + 1) * P), xn[:, TPC * c + j, :], ident[:])
            last.then_inc(S("xt_ps"), 1)

        def pe_block0(pe):
            pe.wait_ge(S("w0_in"), 16 * 6)

            def project(c):
                pe.wait_ge(S("xt"), NCH * 0 + c + 1)
                for w, b, used, done in ((w_v, 3, "state", "v_ps"), (w_q, 2, "ret", "q_ps"), (w_g, 4, "gate", "g_ps")):
                    if c >= 1:
                        pe.wait_ge(S(used), 2 * c if used == "state" else c)
                    pe.matmul(bank(b), w[:], xt[:, chunk_cols(c)], start=True, stop=True).then_inc(S(done), 1)

            def turn(c):
                pe.wait_ge(S("ret"), c + 1)
                if c >= 1:
                    pe.wait_ge(S("ret_rows"), c)
                for j in range(TPC):
                    last = pe.transpose(bank(5, j * P, (j + 1) * P), buf_b[:, tile_cols(TPC * c + j)], ident[:])
                last.then_inc(S("ret_ps"), 1)

            pe_xt(pe, 0, 0)
            for c in range(NCH):
                if c + 1 < NCH:
                    pe_xt(pe, 0, c + 1)
                project(c)
                if c >= 1:
                    turn(c - 1)
            turn(NCH - 1)
            def turn_back(c):
                pe.wait_ge(S("rn_rows"), TPC * (c + 1))
                if c >= 2:
                    pe.wait_ge(S("rn"), c - 1)
                for j in range(TPC):
                    last = pe.transpose(bank(c % 2, j * P, (j + 1) * P), xn[:, TPC * c + j, :], ident[:])
                last.then_inc(S("rn_ps"), 1)

            turn_back(0)
            for c in range(NCH):
                if c + 1 < NCH:
                    turn_back(c + 1)
                pe.wait_ge(S("gated"), c + 1)
                if c >= 2:
                    pe.wait_ge(S("x_done0"), c - 1)
                for j in range(TPC):
                    last = pe.matmul(bank(2 + c % 2, j * P, (j + 1) * P), buf_b[:, tile_cols(TPC * c + j)], w_o[:],
                                     start=True, stop=True)
                last.then_inc(S("o_ps"), 1)

        def pe_route(pe, n, w):
            if n == 1:
                pe.wait_ge(S("wr_in"), 16 * 7)
            pe_xt(pe, n, 0)
            for c in range(NCH):
                if c + 1 < NCH:
                    pe_xt(pe, n, c + 1)
                pe.wait_ge(S("xt"), NCH * n + c + 1)
                for i in range(TPC * c, TPC * (c + 1)):
                    last = pe.matmul(bank(2, i * E, (i + 1) * E), xt[:, tile_cols(i)], w[:], start=True, stop=True)
            last.then_inc(S("logit_ps"), 1)

        def pe_moe(pe, n):
            cfg = moe_cfg[n]
            nt, t0 = moe_tiles(cfg["k"]), cfg["t0"]
            w1, w2 = cfg["w1"], cfg["w2"]
            pe_route(pe, n, wr[cfg["r"]])
            pe.wait_ge(S(f"chosen{n}"), 1)
            pe.matmul(bank(3, 0, P), before[:], rt[:, 3, :], start=True, stop=True)
            pe.matmul(bank(3, P, 2 * P), ones[:], rt[:, 3, :], start=True, stop=True).then_inc(S(f"rank_ps{n}"), 1)
            order, used = moe_cfg[n]["order"], NTILE * cfg["k"]
            pe.wait_ge(S("hot_row"), order)
            pe.wait_ge(S("hot_seq"), order)
            for i in range(used):
                if i % NTILE == 0:
                    pe.wait_ge(S("place_hot"), cfg["k0"] + i // NTILE + 1)
                last = pe.matmul(bank(4, 0, 2 * nt), place_hot[:, i, :], tile_hot[:, 1:3, i, 0:nt],
                                 start=(i == 0), stop=(i == used - 1))
            last.then_inc(S("row_ps"), 1)
            pe.wait_ge(S(f"eid{n}"), 1)
            pe.wait_ge(S(f"w_moe{n}_in"), 16 * {1: 4, 3: 2, 7: 5}[n])

            def turn_rows(g, u4, u):
                pe.wait_ge(S(f"xs_in{u4}"), g * 16 + (t0 * 4 + 16))
                pe.transpose(bank(u, 0, P), xs[:, u4, 0:D], ident[:]).then_inc(S("moe_xst_ps"), 1)

            def experts(g):
                word = pe.value_load(packed[0:1, bass.ds(g, 1)], min_val=0, max_val=E ** 6 - 1)
                return [(word >> (3 * i)) & (E - 1) for i in range(6)]

            def up(j, u, e):
                pe.wait_ge(S("moe_xst"), j + (t0 + 1))
                pe.matmul(bank(2 + u), xst[:, u, :], w1[:, bass.ds(e, 1), :], start=True, stop=True)\
                    .then_inc(S("moe_h_ps"), 1)

            def turn_hidden(j, u):
                pe.wait_ge(S("moe_h"), j + (t0 + 1))
                if not (isinstance(j, int) and j < 2):
                    pe.wait_ge(S("moe_ht"), j + (t0 - 1))
                for k in range(KF):
                    last = pe.transpose(bank(4 + u, k * P, (k + 1) * P), hid[:, u, k * P:(k + 1) * P], ident[:])
                last.then_inc(S("moe_ht_ps"), 1)

            def down(j, u, e):
                if not (isinstance(j, int) and j < 2):
                    pe.wait_ge(S("moe_y_sb"), j + (t0 - 1))
                pe.wait_ge(S("moe_ht"), j + (t0 + 1))
                for k in range(KF):
                    last = pe.matmul(bank(6 + u, 0, D), hidt[:, u, k * P:(k + 1) * P], w2[:, bass.ds(e, 1), k, :],
                                     start=(k == 0), stop=(k == KF - 1))
                last.then_inc(S("moe_y_ps"), 1)

            turn_rows(0, 0, 0)
            turn_rows(0, 1, 1)
            up(0, 0, experts(0)[1])

            def steps(g, first=False, last=False):
                e = experts(g)
                for u in range(4):
                    j = g * 4 + u
                    if not (last and u == 3):
                        up(j + 1, (u + 1) % 2, e[u + 2])
                    if not (last and u >= 2):
                        turn_rows(g + (u + 2) // 4, (u + 2) % 4, u % 2)
                    turn_hidden(j, u % 2)
                    if not (first and u == 0):
                        down(j - 1, (u + 1) % 2, e[u])
                if last:
                    down(j, 1, e[4])

            steps(0, first=True)
            with pe.Fori(1, nt // 4 - 1) as g:
                steps(g)
            steps(nt // 4 - 1, last=True)

        def pe_rel_bias(pe):
            pe.wait_ge(S("table"), 1)
            pe.matmul(bank(7, 0, BIASW), table_all[:], bucket[:], start=True, stop=True).then_inc(S("bias_ps"), 1)

        def pe_block2(pe):
            pe_xt(pe, 2, 0)
            for c in range(NCH):
                if c + 1 < NCH:
                    pe_xt(pe, 2, c + 1)
                pe.wait_ge(S("xt"), NCH * 2 + c + 1)
                if c >= 2:
                    pe.wait_ge(S("qk2"), c - 1)
                pe.matmul(bank(2 + c % 2), w_qk1[:], xt[:, chunk_cols(c)], start=True, stop=True).then_inc(S("qk_ps2"), 1)
                if c >= 2:
                    pe.wait_ge(S("v_lin2"), c - 1)
                for j in range(TPC):
                    last = pe.matmul(bank(4 + c % 2, j * P, (j + 1) * P), xt[:, tile_cols(TPC * c + j)], w_v1[:],
                                     start=True, stop=True)
                last.then_inc(S("v_ps2"), 1)

            def scores(b):
                if b >= 2:
                    pe.wait_ge(S("z2"), b - 1)
                pe.wait_ge(S("k2"), b // 2 + 1)
                t0 = b * L
                pe.matmul(bank(6 + b % 2, 0, L), buf_b[:, t0:t0 + P], buf_a[:, t0:t0 + L], start=True, stop=True)
                pe.matmul(bank(6 + b % 2, L, L + P), buf_b[:, t0 + P:t0 + L], buf_a[:, t0 + P:t0 + L],
                          start=True, stop=True).then_inc(S("s_ps2"), 1)

            scores(0)
            for b in range(NB):
                if b + 1 < NB:
                    scores(b + 1)
                pe.wait_ge(S("v2"), b // 2 + 1)
                if b >= 2:
                    pe.wait_ge(S("x_add2"), b - 1)
                pe.wait_ge(S("phi2"), b + 1)
                i = 2 * b
                o = 2 + b % 2
                pe.matmul(bank(o, 0, P), att_z[:, b % 2, 0:P], buf_c[:, tile_cols(i)], start=True, stop=True)
                pe.matmul(bank(o, P, 2 * P), att_z[:, b % 2, P:2 * P], buf_c[:, tile_cols(i)], start=True, stop=False)
                pe.matmul(bank(o, P, 2 * P), att_z[:, b % 2, 2 * P:3 * P], buf_c[:, tile_cols(i + 1)],
                          start=False, stop=True).then_inc(S("o_ps2"), 1)

        def pe_block4(pe):
            pe_xt(pe, 4, 0)
            for c in range(NCH):
                if c + 1 < NCH:
                    pe_xt(pe, 4, c + 1)
                pe.wait_ge(S("xt"), NCH * 4 + c + 1)
                if c >= 2:
                    pe.wait_ge(S("force4"), c - 1)
                pe.matmul(bank(2 + c % 2), w_b2[:], xt[:, chunk_cols(c)], start=True, stop=True).then_inc(S("force_ps4"), 1)
            pe_offsets(pe)
            for c in range(NCH):
                pe.wait_ge(S("solved4"), c // 2 + 1)
                for j in range(TPC):
                    b, h = 2 * c + j // 2, j % 2
                    last = pe.transpose(bank(4 + c, j * P, (j + 1) * P), wave_b[:, b, (1 + h) * P:(2 + h) * P], ident[:])
                last.then_inc(S("v_ps4"), 1)

        def pe_block5(pe):
            pe_route(pe, 5, wr[2])
            pe.wait_ge(S("w5_in"), 16 * 5)
            pe.wait_ge(S("scores5"), 1)

            def up(c, m):
                n, u = UNITS * c + m, m % 2
                if not (isinstance(c, int) and n < 2):
                    pe.wait_ge(S("h5"), n - 1)
                wa = w_s1[:, tile_cols(m)] if m < KF else w12[:, m - KF, 0:P]
                wb = w_s2[:, tile_cols(m)] if m < KF else w12[:, m - KF, P:2 * P]
                rhs = xt[:, bass.ds(c * CH, CH)]
                pe.matmul(bank(u), wa, rhs, start=True, stop=True)
                pe.matmul(bank(4 + u), wb, rhs, start=True, stop=True).then_inc(S("up5"), 1)

            def down(c, m):
                n, u, e = UNITS * c + m, m % 2, m - KF
                first = isinstance(c, int) and c == 0
                if m == 0 and not first:
                    pe.wait_ge(S("acc5"), (E + 1) * c)
                if e >= 2:
                    pe.wait_ge(S("acc5"), (E + 1) * c + e)
                pe.wait_ge(S("h5"), n + 1)
                for j in range(TPC):
                    if m < KF:
                        last = pe.matmul(bank(3, j * P, (j + 1) * P), hidt[:, u, tile_cols(j)], w_s3[:, m, :],
                                         start=(m == 0 and j == 0), stop=(m == KF - 1), skip_group_check=True)
                    else:
                        last = pe.matmul(bank(6 + e % 2, j * P, (j + 1) * P), hidt[:, u, tile_cols(j)], w3[:, e, :],
                                         start=True, stop=True)
                last.then_inc(S("down5"), 1)

            def chunk(c):
                up(c, 0)
                for m in range(UNITS):
                    if m + 1 < UNITS:
                        up(c, m + 1)
                    down(c, m)

            chunk(0)
            with pe.Fori(1, NCH) as c:
                chunk(c)

        def pe_offsets(pe):
            pe.wait_ge(S("xt"), 5 * NCH)
            pe.wait_ge(S("force4"), NCH)
            pe.wait_ge(S("w_moe7_in"), 16 * 5)
            for e in range(E):
                pe.wait_ge(S("idle"), e + 1)
                for k in range(KF):
                    lhs, rhs = idle[:, (e % 2) * KF + k, :], w2_a[:, e, k, :]
                    pe.matmul(bank(e // 4, (e % 4) * P, (e % 4 + 1) * P), lhs, rhs, start=(k == 0), stop=(k == KF - 1))
                    last = pe.matmul(bank(2, 0, D), lhs, rhs, start=(e == 0 and k == 0), stop=False)
                last.then_inc(S("idle_ps"), 1)
            for e in range(E):
                last = pe.matmul(bank(2, 0, D), ident[:], b2_all[:, e, :], start=False, stop=(e == E - 1))
            last.then_inc(S("idle_ps"), 1)

        def pe_block6(pe):
            pe_xt(pe, 6, 0)
            pe.wait_ge(S("w_rot"), 2)
            pe.wait_ge(S("w6_in"), 16 * 7)
            pe.matmul(bank(7, 0, 2), pair_turn[:], b_qk[:, 0:2], start=True, stop=True).then_inc(S("b_rot_ps"), 1)
            for c in range(NCH):
                if c + 1 < NCH:
                    pe_xt(pe, 6, c + 1)
                pe.wait_ge(S("xt"), NCH * 6 + c + 1)
                for b, w, free in ((2, w_qkv[:, 0:D], 0), (3, w_rot[:, 0:D], 0),
                                   (4, w_qkv[:, D:2 * D], 1), (5, w_rot[:, D:2 * D], 1)):
                    if c >= 1:
                        pe.wait_ge(S("f6"), 2 * c - 1 + free)
                    pe.matmul(bank(b), w, xt[:, chunk_cols(c)], start=True, stop=True).then_inc(S("qk_ps6"), 1)
                if c >= 1:
                    pe.wait_ge(S("v6"), c)
                for j in range(TPC):
                    last = pe.matmul(bank(6, j * P, (j + 1) * P), xt[:, tile_cols(TPC * c + j)], w_qkv[:, 2 * D:3 * D],
                                     start=True, stop=True)
                last.then_inc(S("v_ps6"), 1)
            pe.wait_ge(S("v6"), NCH)

            def score(g, i, skip=False):
                g, i = (g + 1, i - 2 * HEADS) if i >= 2 * HEADS else (g, i)
                n, u, h = g * (2 * HEADS) + i, i // HEADS, i % HEADS
                if h == 0:
                    pe.wait_ge(S(f"slab_in{u}"), g * (16 * 12) + 16 * 12)
                if not (isinstance(n, int) and n < 4):
                    pe.wait_ge(S("exp6"), n - 3)
                for t in range(2):
                    last = pe.matmul(bank(i % 4, t * L, (t + 1) * L), q_slab[:, u, h, t * P:(t + 1) * P], k_slab[:, u, h, :],
                                     start=True, stop=True)
                last.then_inc(S("s6"), 1)

            def turn(g, i):
                g, i = (g + 1, i - 2 * HEADS) if i >= 2 * HEADS else (g, i)
                n = g * (2 * HEADS) + i
                pe.wait_ge(S("exp6"), n + 1)
                if not (isinstance(n, int) and n < 2):
                    pe.wait_ge(*copied(g, i - 2))
                for t in range(2):
                    for kt in range(2):
                        last = pe.transpose(bank(6 + i % 2, kt * L + t * P, kt * L + (t + 1) * P),
                                            probs(i)[:, t * L + kt * P:t * L + (kt + 1) * P], ident[:])
                last.then_inc(S("t6"), 1)

            def weigh(g, i):
                n, u, h = g * (2 * HEADS) + i, i // HEADS, i % HEADS
                s = g * 2 + u
                if h == 0:
                    pe.wait_ge(S("v_seq6"), s + 1)
                if h % 8 == 0 and not (isinstance(s, int) and s == 0 and h == 0):
                    pe.wait_ge(S("heads6"), s * 2 + h // 8)
                pe.wait_ge(*copied(g, i))
                for kt in range(2):
                    last = pe.matmul(psum[32 * (h % 4):32 * (h % 4) + HD + 1, 4,
                                          (h // 4 % 2) * L:(h // 4 % 2 + 1) * L],
                                     v_seq[:, u, kt, h, :], probs_t[:, i % 2, kt * L:(kt + 1) * L],
                                     start=(kt == 0), stop=(kt == 1), tile_position=(0, 32 * (h % 4)))
                last.then_inc(S("pv6"), 1)

            def back(s, half):
                pe.wait_ge(S("heads6"), s * 2 + (half + 1))
                if not (isinstance(s, int) and s < 1 and half == 0):
                    pe.wait_ge(S("o6"), s * 2 + half)
                for t in range(2):
                    for z in range(2):
                        last = pe.transpose(bank(5, (2 * t + z) * P, (2 * t + z + 1) * P),
                                            heads_t[:, half, z * L + t * P:z * L + (t + 1) * P], ident[:])
                last.then_inc(S("tok6"), 1)

            pe.wait_ge(S("clear6"), 1)
            score(0, 0)
            score(0, 1)
            score(0, 2)
            turn(0, 0)

            def steps(g, last=False):
                for i in range(2 * HEADS):
                    if not (last and i + 3 >= 2 * HEADS):
                        score(g, i + 3)
                    if not (last and i + 1 >= 2 * HEADS):
                        turn(g, i + 1)
                    weigh(g, i)
                    if i % 8 == 3 and not (isinstance(g, int) and g == 0 and i == 3):
                        z = (i - 11) // 8
                        back(g * 2 + z // 2, z % 2)

            steps(0)
            with pe.Fori(1, NB // 2 - 1) as g:
                steps(g)
            steps(NB // 2 - 1, last=True)
            back(NB - 1, 1)

            for c in range(NCH):
                pe.wait_ge(S("o6"), 4 * c + 4)
                if c >= 2:
                    pe.wait_ge(S("ot6"), c - 1)
                for j in range(TPC):
                    last = pe.transpose(bank(c % 2, j * P, (j + 1) * P), xn[:, TPC * c + j, :], ident[:])
                last.then_inc(S("ot_ps6"), 1)
                pe.wait_ge(S("ot6"), c + 1)
                if c >= 2:
                    pe.wait_ge(S("x_done6"), c - 1)
                for j in range(TPC):
                    last = pe.matmul(bank(2 + c % 2, j * P, (j + 1) * P), buf_a[:, tile_cols(TPC * c + j)], w_p6,
                                     start=True, stop=True)
                last.then_inc(S("proj_ps6"), 1)

        @block.tensor
        def _(pe):
            pe.wait_ge(S("consts"), CONSTS)
            pe_block0(pe)
            pe_rel_bias(pe)
            pe_moe(pe, 1)
            pe_block2(pe)
            pe_moe(pe, 3)
            pe_block4(pe)
            pe_block5(pe)
            pe_block6(pe)
            pe_moe(pe, 7)

        def dve_stats(v, ch, n, c, dst, src):
            for i in range(TPC * c, TPC * (c + 1)):
                last = v.bn_stats(dst[:, i, :], src(i))
            ch(last)

        def dve_var(v, ch, n, st, tag="x", c=None):
            ch.wait()
            i = slice(0, NTILE) if c is None else slice(TPC * c, TPC * (c + 1))
            me, mo, qe, qo = st[:, i, 1], st[:, i, 4], st[:, i, 2], st[:, i, 5]
            ch(v.tensor_tensor(lnt[:, 1, i], me, mo, ALU.add))
            ch(v.tensor_tensor(lnt[:, 2, i], me, mo, ALU.subtract))
            ch.link(v.tensor_tensor(lnt[:, 3, i], qe, qo, ALU.add))
            ch(v.tensor_scalar(lnt[:, 0, i], lnt[:, 1, i], 0.5, None, ALU.mult))
            ch.link(v.tensor_tensor(lnt[:, 4, i], lnt[:, 2, i], lnt[:, 2, i], ALU.mult))
            ch.link(v.scalar_tensor_tensor(out=lnt[:, 2, i], in0=lnt[:, 4, i], scalar=D / 4.0, in1=lnt[:, 3, i],
                                           op0=ALU.mult, op1=ALU.add))
            v.tensor_scalar(lnt[:, 6, i], lnt[:, 2, i], 1.0 / D, EPS, ALU.mult, ALU.add).then_inc(S("var"), 1)

        def dve_norm(v, ch, n, src, done, tag="x", c=None):
            first, end = (0, NTILE) if c is None else (TPC * c, TPC * (c + 1))
            v.wait_ge(S("sd"), norm_no(n, tag, c or 0))
            ch.link(v.reciprocal(lnt[:, 5, first:end], lnt[:, 7, first:end]))
            for i in range(first, end):
                v.tensor_scalar(xn[:, i, :], src(i), lnt[:, 0, i:i + 1], lnt[:, 5, i:i + 1], ALU.subtract, ALU.mult)\
                    .then_inc(S(done), 1)

        def dve_whole(v, ch, n):
            if n not in BY_CHUNK:
                dve_var(v, ch, n, stats)
                dve_norm(v, ch, n, x_rows, "xn")

        def dve_next(v, ch, n, c):
            dve_stats(v, ch, n, c, stats, x_rows)
            if n in BY_CHUNK:
                dve_var(v, ch, n, stats, c=c)
                if c > 0:
                    dve_norm(v, ch, n, x_rows, "xn", c=c - 1)
                if c == NCH - 1:
                    dve_norm(v, ch, n, x_rows, "xn", c=c)

        def dve_block0(v, ch):
            v.wait_ge(S("lam_exp"), 1)
            ch.link(v.tensor_scalar(lam_col[:, 2:3], lam_col[:, 1:2], -1.0, 1.0, ALU.mult, ALU.add))
            ch.link(v.tensor_scalar(lam_col[:, 3:4], lam_col[:, 2:3], float(np.finfo(np.float32).tiny),
                                    float(np.float32(1.0 - 1e-9)), ALU.max, ALU.min))
            v.wait_ge(S("consts"), CONSTS)
            for r in range(L // P):
                ch(v.tensor_scalar(lam[:, tile_cols(r)], ones[:], lam_col[:, 3:4], None, ALU.mult))
            for c in range(NCH):
                v.wait_ge(S(f"x_in{c}"), 16)
                dve_stats(v, ch, 0, c, stats, x_rows)
            dve_var(v, ch, 0, stats)
            dve_norm(v, ch, 0, x_rows, "xn")
            for c in range(NCH):
                v.wait_ge(S("v_ps"), c + 1)
                if c >= 1:
                    v.wait_ge(S("ret"), c)
                for s in range(CH // L):
                    v.tensor_tensor_scan(state[:, s * L:(s + 1) * L], lam[:],
                                         bank(3, s * L, (s + 1) * L), 0.0, ALU.mult, ALU.add).then_inc(S("state"), 1)
                v.wait_ge(S("state"), 2 * c + 2)
                v.wait_ge(S("q_ps"), c + 1)
                v.tensor_tensor(buf_b[:, chunk_cols(c)], state[:], bank(2), ALU.mult).then_inc(S("ret"), 1)
                if c >= 1:
                    v.wait_ge(S("ret_rows"), c)
                    dve_stats(v, ch, 0, c - 1, stats2, lambda i: buf_c[:, tile_cols(i)])
            v.wait_ge(S("ret_rows"), NCH)
            dve_stats(v, ch, 0, NCH - 1, stats2, lambda i: buf_c[:, tile_cols(i)])
            dve_var(v, ch, 0, stats2, "r")
            dve_norm(v, ch, 0, lambda i: buf_c[:, tile_cols(i)], "rn_rows", "r")
            def finish(c):
                v.wait_ge(S("o_ps"), c + 1)
                v.tensor_tensor(x_chunk(c), x_chunk(c), bank(2 + c % 2), ALU.add).then_inc(S("x_done0"), 1)
                v.wait_ge(S("x_done0"), c + 1)
                dve_stats(v, ch, 1, c, stats, x_rows)

            for c in range(NCH):
                v.wait_ge(S("rn"), c + 1)
                v.wait_ge(S("gate"), c + 1)
                v.tensor_tensor(buf_b[:, chunk_cols(c)], buf_b[:, chunk_cols(c)], buf_a[:, chunk_cols(c)], ALU.mult)\
                    .then_inc(S("gated"), 1)
                if c >= 1:
                    finish(c - 1)
            finish(NCH - 1)

        def dve_choose(v, ch, logits, best, top, one_hot):
            ch.link(v.tensor_reduce(rs[:, best, :], by_tile(logits), AX.X, ALU.max))
            ch.link(v.tensor_tensor(em(6), em(logits), over_e(rs[:, best, :]), ALU.is_equal))
            ch.link(v.tensor_tensor(em(6), em(6), over_i(desc[:]), ALU.mult))
            ch.link(v.tensor_reduce(rs[:, top, :], by_tile(6), AX.X, ALU.max))
            ch.link(v.tensor_tensor(em(one_hot), over_i(desc[:]), over_e(rs[:, top, :]), ALU.is_equal))

        def dve_slots(v, ch, n, k):
            nt, order = moe_tiles(k), moe_cfg[n]["order"]
            v.wait_ge(S(f"rank_ps{n}"), 1)
            counts = bank(3, P, 2 * P)
            ch(v.tensor_tensor_scan(rt[:, 8, :], ones[:], counts, 0.0, ALU.mult, ALU.add))
            ch.link(v.tensor_reduce(rs[:, 4, 0:E], counts.rearrange("p (e i) -> p e i", e=E), AX.X, ALU.add))
            ch(v.tensor_tensor(em(9), over_i(rs[:, 4, 0:E]), over_e(thr[:, 0:NTILE]), ALU.is_gt))
            ch.link(v.tensor_tensor_scan(rs[:, 5, 0:E], ones[:, 0:E], rs[:, 4, 0:E], 0.0, ALU.mult, ALU.add))
            ch(v.tensor_tensor(rs[:, 5, 8:16], rs[:, 5, 0:E], rs[:, 4, 0:E], ALU.subtract))
            ch.link(v.tensor_reduce(rs[:, 6, 0:E], em(9), AX.X, ALU.add))
            ch.link(v.tensor_tensor_scan(rs[:, 7, 0:E], ones[:, 0:E], rs[:, 6, 0:E], 0.0, ALU.mult, ALU.add))
            ch(v.tensor_tensor(rs[:, 8, 0:E], rs[:, 7, 0:E], rs[:, 6, 0:E], ALU.subtract))
            some = nt + 4
            ends = rs[0:1, 7, 0:E].rearrange("p (o e) -> p o e", o=1).to_broadcast([1, some, E])
            nos = tile_no[:, 0:some].rearrange("p (j o) -> p j o", o=1).to_broadcast([1, some, E])
            ch.link(v.tensor_tensor(eid_f[:, 0:some, :], ends, nos, ALU.is_le))
            ch.link(v.tensor_reduce(eid_s[:, 0, 0:some], eid_f[:, 0:some, :], AX.X, ALU.add))
            ch.link(v.tensor_scalar(eid_s[:, 1, 0:some], eid_s[:, 0, 0:some], float(E - 1), None, ALU.min))
            groups = nt // 4
            part = eid_s[:, 1, 5:nt + 2:4]
            for i in (4, 3, 2, 1, 0):
                done = packed[:, 0:groups] if i == 0 else packed_f[:, i - 1, 0:groups]
                ins = v.scalar_tensor_tensor(out=done, in0=part, scalar=float(E), in1=eid_s[:, 1, i:i + nt - 3:4],
                                             op0=ALU.mult, op1=ALU.add)
                if i:
                    ch.link(ins)
                else:
                    ins.then_inc(S(f"eid{n}"), 1)
                part = done
            ch(v.scalar_tensor_tensor(out=rs[:, 9, 0:E], in0=rs[:, 8, 0:E], scalar=float(P), in1=rs[:, 5, 8:16],
                                      op0=ALU.mult, op1=ALU.subtract))
            ch.link(v.tensor_tensor(em(9), em(8), counts.rearrange("p (e i) -> p e i", e=E), ALU.subtract))
            ch.link(v.tensor_tensor(em(8), em(9), over_i(rs[:, 9, 0:E]), ALU.add))
            ch.link(v.tensor_tensor(rt[:, 9, :], rt[:, 8, :], bank(3, 0, P), ALU.add))
            for c in range(k):
                ch.link(v.tensor_tensor(rt[:, 8, :], rt[:, 9, :], rt[:, 1 + c, :] if k > 1 else rt[:, 3, :], ALU.mult))
                ch.link(v.tensor_reduce(rs[:, 16 + c, :], by_tile(8), AX.X, ALU.add))
            used = k * NTILE
            slot, place, start = (rs[:, 16 + 2 * z:18 + 2 * z, :].rearrange("p k i -> p (k i)")[:, 0:used] for z in range(3))
            ch.link(v.tensor_scalar(place, slot, 0.5 - P / 2, ROUND128, ALU.add, ALU.add))
            ch.link(v.tensor_scalar(start, place, -ROUND128, None, ALU.add))
            ch.link(v.tensor_tensor(place, slot, start, ALU.subtract))

            def rows_by(ap, cols):
                return ap.rearrange("p (i o) -> p i o", o=1).to_broadcast([P, ap.shape[1], cols])

            def cols_by(ap, rows):
                return ap.rearrange("p (o j) -> p o j", o=1).to_broadcast([P, rows, ap.shape[1]])

            v.tensor_tensor(tile_hot[:, 0, 0:used, 0:nt], rows_by(start, nt), cols_by(thr[:, 0:nt], used), ALU.is_equal)\
                .then_inc(S("tile_hot"), 1)
            v.wait_ge(S("tile_hot"), order)
            v.tensor_tensor(tile_hot[:, 1, 0:used, 0:nt], tile_hot[:, 0, 0:used, 0:nt], rows_by(tile_seq[:, 0:used], nt),
                            ALU.mult).then_inc(S("hot_seq"), 1)
            for c in range(k):
                i = slice(c * NTILE, (c + 1) * NTILE)
                v.tensor_tensor(place_hot[:, i, :], rows_by(place[:, i], P), cols_by(col_no[:], NTILE), ALU.is_equal)\
                    .then_inc(S("place_hot"), 1)
            v.wait_ge(S("row_ps"), order)
            seq, low_part = bank(4, 0, nt), bank(4, nt, 2 * nt)
            ch(v.tensor_scalar(row_f[:, 3, 0:nt], low_part, 1.0, None, ALU.mult))
            ch.link(v.tensor_scalar(row_f[:, 0, 0:nt], seq, float(P), None, ALU.mult))
            ch(v.scalar_tensor_tensor(out=row_f[:, 1, 0:nt], in0=seq, scalar=0.0, in1=past[:, 0:nt],
                                      op0=ALU.is_equal, op1=ALU.mult))
            ch.link(v.tensor_tensor(row_f[:, 2, 0:nt], row_f[:, 0, 0:nt], row_f[:, 3, 0:nt], ALU.add))
            ch(v.tensor_scalar(row_f[:, 0, 0:nt], row_f[:, 2, 0:nt], float(P + T), -float(T), ALU.is_ge, ALU.mult))
            v.tensor_tensor(row_out[:, 0:nt], row_f[:, 2, 0:nt], row_f[:, 1, 0:nt], ALU.add).then_inc(S("row_ids"), 1)
            ch.wait()
            v.tensor_tensor(row_in[:, 0:nt], row_f[:, 2, 0:nt], row_f[:, 0, 0:nt], ALU.add).then_inc(S("row_ids"), 1)
            v.wait_ge(S(f"eid{n}"), 1)

        def dve_omega(v, ch):
            v.wait_ge(S("ln4"), 1)
            ch.link(v.tensor_scalar(om[:, 4:5], om[:, 0:1], 0.0, None, ALU.max))
            ch.link(v.tensor_tensor(om[:, 5:6], om[:, 4:5], om[:, 3:4], ALU.add))
            ch.link(v.tensor_scalar(wave[:, 0, 0:1], om[:, 5:6], float(np.float32(DT) ** 2) / 2, None, ALU.mult))
            for k in range(8):
                d = wave[:, 0, k:k + 1]
                ch.link(v.tensor_scalar(wave[:, 1, k:k + 1], d, -2.0, 2.0, ALU.mult, ALU.add))
                if k < 7:
                    ch.link(v.tensor_scalar(om[:, 6:7], d, -2.0, 4.0, ALU.mult, ALU.add))
                    ch.link(v.tensor_tensor(wave[:, 0, k + 1:k + 2], d, om[:, 6:7], ALU.mult))

        def dve_moe(v, ch, n):
            cfg = moe_cfg[n]
            k, nt, k0, t0 = cfg["k"], moe_tiles(cfg["k"]), cfg["k0"], cfg["t0"]
            dve_var(v, ch, n, stats)
            dve_norm(v, ch, n, x_rows, "xn")
            v.wait_ge(S("logit_ps"), (n + 1) // 2)
            logits_ps = bank(2, 0, NTILE * E).rearrange("p (i e) -> p e i", e=E)
            if n == 7:
                ch.link(v.tensor_tensor(em(0), logits_ps, over_i(rbias[3][:]), ALU.add))
                dve_choose(v, ch, 0, 0, 1, 3)
                v.sem_inc(S(f"chosen{n}"), 1)
            elif n == 1:
                ch.link(v.tensor_copy(em(0), logits_ps))
                dve_choose(v, ch, 0, 0, 1, 1)
                ch.link(v.scalar_tensor_tensor(out=em(5), in0=em(1), scalar=NEG, in1=em(0), op0=ALU.mult, op1=ALU.add))
                dve_choose(v, ch, 5, 2, 3, 2)
                v.tensor_tensor(rt[:, 3, :], rt[:, 1, :], rt[:, 2, :], ALU.add).then_inc(S(f"chosen{n}"), 1)
                v.tensor_tensor(rs[:, 10, :], rs[:, 2, :], rs[:, 0, :], ALU.subtract).then_inc(S("gap1"), 1)
            elif n == 3:
                v.tensor_tensor(em(7), logits_ps, over_i(rbias[1][:]), ALU.add).then_inc(S("logits3"), 1)
                v.wait_ge(S("scores3"), 1)
                dve_choose(v, ch, 0, 14, 1, 3)
                v.sem_inc(S("shares"), 1)
                v.sem_inc(S(f"chosen{n}"), 1)
            dve_slots(v, ch, n, k)
            if n == 1:
                v.wait_ge(S("gap_exp1"), 1)
                ch.link(v.tensor_scalar(rs[:, 12, :], rs[:, 11, :], 1.0, None, ALU.add))
                ch.link(v.reciprocal(rs[:, 14, :], rs[:, 12, :]))
                v.tensor_tensor(rs[:, 15, :], rs[:, 11, :], rs[:, 14, :], ALU.mult).then_inc(S("shares"), 1)

            def experts(g):
                if not cfg["bias"]:
                    return [None] * 6
                word = v.value_load(packed[0:1, bass.ds(g, 1)], min_val=0, max_val=E ** 6 - 1)
                return [(word >> (3 * i)) & (E - 1) for i in range(6)]

            def hidden(j, u, e):
                if not (isinstance(j, int) and j < 2):
                    v.wait_ge(S("moe_ht_ps"), j + (t0 - 1))
                v.wait_ge(S("moe_h_ps"), j + (t0 + 1))
                if cfg["bias"]:
                    ins = v.tensor_tensor(hid[:, u, :], bank(2 + u), b1_all[:, bass.ds(e, 1), :], ALU.add)
                else:
                    ins = v.tensor_copy(hid[:, u, :], bank(2 + u))
                ins.then_inc(S("moe_h"), 1)

            def result(g, j, u4, e):
                if not isinstance(g, int) or g > 0:
                    v.wait_ge(S(f"y_out{u4}"), g * 16 + t0 * 4)
                v.wait_ge(S("moe_y_ps"), j + (t0 + 1))
                if cfg["bias"]:
                    ins = v.tensor_tensor(ys[:, u4, :], bank(6 + u4 % 2, 0, D), b2_all[:, bass.ds(e, 1), :], ALU.add)
                else:
                    ins = v.tensor_copy(ys[:, u4, :], bank(6 + u4 % 2, 0, D))
                ins.then_inc(S("moe_y_sb"), 1)

            if n == 3:
                dve_omega(v, ch)
            hidden(0, 0, experts(0)[1])

            def steps(g, first=False, last=False):
                e = experts(g)
                for u in range(4):
                    if not (last and u == 3):
                        hidden(g * 4 + u + 1, (u + 1) % 2, e[u + 2])
                    if u > 0:
                        result(g, g * 4 + u - 1, u - 1, e[u])
                    elif not first:
                        result(g - 1, g * 4 - 1, 3, e[u])
                if last:
                    result(g, g * 4 + 3, 3, e[4])

            steps(0, first=True)
            with v.Fori(1, nt // 4 - 1) as g:
                steps(g)
            steps(nt // 4 - 1, last=True)

            for c in range(NCH):
                v.wait_ge(S(f"back{c}"), 16 * (k0 + k))
                for kk in range(k):
                    if n != 7:
                        v.wait_ge(S("scaled"), 4 * k0 + k * c + kk + 1)
                    ch.link(v.tensor_tensor(x_chunk(c), x_chunk(c), (buf_a, buf_b)[kk][:, chunk_cols(c)], ALU.add))
                v.sem_inc(S(f"x_done{n}"), 1)
                if n < 7:
                    dve_next(v, ch, n + 1, c)

        def dve_rel_bias(v, ch):
            v.wait_ge(S("w2_in"), 16 * 8)
            v.wait_ge(S("consts"), CONSTS)
            v.tensor_scalar(table_all[:], ones[0:NBUCKET, :], table[:, 0:1], None, ALU.mult).then_inc(S("table"), 1)
            v.wait_ge(S("bias_ps"), 1)
            v.tensor_scalar(bias_row[:], bank(7, 0, BIASW), math.sqrt(D) / STD, -MU / STD, ALU.mult, ALU.add)\
                .then_inc(S("bias_row"), 1)

        def dve_block2(v, ch):
            dve_whole(v, ch, 2)
            for c in range(NCH):
                if c >= 2:
                    v.wait_ge(S("v2"), c - 1)
                v.wait_ge(S("v_ps2"), c + 1)
                v.tensor_tensor(hidt[:, c % 2, :].rearrange("p (i d) -> p i d", d=D),
                                bank(4 + c % 2).rearrange("p (i d) -> p i d", d=D),
                                bv1[:].rearrange("p (o d) -> p o d", o=1).to_broadcast([P, TPC, D]), ALU.add)\
                    .then_inc(S("v_lin2"), 1)
                v.wait_ge(S("qk2"), c + 1)
                v.tensor_scalar(buf_a[:, chunk_cols(c)], hid[:, c % 2, :], cols1[:, 1:2], cols1[:, 3:4], ALU.mult, ALU.add)\
                    .then_inc(S("k2_q"), 1)
                v.wait_ge(S("k2_q"), c + 1)
                v.tensor_scalar(buf_b[:, chunk_cols(c)], hid[:, c % 2, :], cols1[:, 2:3], cols1[:, 4:5], ALU.mult, ALU.add)\
                    .then_inc(S("k2"), 1)

            v.wait_ge(S("rel_in"), 16)

            def zed(b):
                u = b % 2
                if b >= 2:
                    v.wait_ge(S("o_ps2"), b - 1)
                v.wait_ge(S("s_ps2"), b + 1)
                scale = 1.0 / L / STD
                ch(v.scalar_tensor_tensor(out=att_z[:, u, 0:L], in0=bank(6 + u, 0, L), scalar=scale, in1=rel[:],
                                          op0=ALU.mult, op1=ALU.add))
                ch.link(v.scalar_tensor_tensor(out=att_z[:, u, L:L + P], in0=bank(6 + u, L, L + P), scalar=scale,
                                               in1=rel[:, 0:P], op0=ALU.mult, op1=ALU.add))
                v.tensor_scalar(att_z[:, u, :], att_z[:, u, :], TINY, None, ALU.add).then_inc(S("z2"), 1)
                v.wait_ge(S("z2"), b + 1)
                ch.link(v.reciprocal(att_r[:, u, :], att_z[:, u, :]))

            def phi(b):
                u = b % 2
                v.wait_ge(S("gelu2"), b + 1)
                v.wait_ge(S("masked2"), 2 * b + 2)
                v.tensor_tensor(att_z[:, u, :], att_g[:, u, :], att_r[:, u, :], ALU.mult).then_inc(S("phi2"), 1)

            def add(b):
                v.wait_ge(S("o_ps2"), b + 1)
                rows = x_sb[:, 2 * b:2 * b + 2, :].rearrange("p i d -> p (i d)")
                v.tensor_tensor(rows, rows, bank(2 + b % 2, 0, 2 * P), ALU.add).then_inc(S("x_add2"), 1)
                if b % 2:
                    v.wait_ge(S("x_add2"), b + 1)
                    v.sem_inc(S("x_done2"), 1)
                    dve_next(v, ch, 3, b // 2)

            zed(0)
            phi(0)
            for b in range(NB):
                if b + 1 < NB:
                    zed(b + 1)
                    phi(b + 1)
                add(b)


        def dve_block4(v, ch):
            dve_whole(v, ch, 4)
            v.wait_ge(S("pads4"), 2)
            src, dst = wave_a, wave_b
            NH = NB // 2
            marks = [0, 0]

            def step(h, ins):
                ch(ins)
                marks[h] = ch.n

            for k in range(7):
                s_ = 1 << k
                two_c = wave[:, 1, k:k + 1]
                for part in range(2):
                    for h in range(2):
                        q = slice(NH * h, NH * (h + 1))
                        if k == 0 and part == 0:
                            v.wait_ge(S("force4"), 2 * h + 2)
                        else:
                            v.wait_ge(S("dve_steps"), marks[h])
                        if part == 0:
                            step(h, v.scalar_tensor_tensor(out=dst[:, q, P:], in0=src[:, q, P - s_:3 * P - s_], scalar=two_c,
                                                           in1=src[:, q, P:], op0=ALU.mult, op1=ALU.add))
                        else:
                            lo = P if s_ < P // 2 else 2 * P
                            step(h, v.tensor_tensor(dst[:, q, lo:], dst[:, q, lo:], src[:, q, lo - 2 * s_:3 * P - 2 * s_],
                                                    ALU.add))
                src, dst = dst, src
            for h in range(2):
                q = slice(NH * h, NH * (h + 1))
                v.wait_ge(S("dve_steps"), marks[h])
                v.scalar_tensor_tensor(out=src[:, q, 2 * P:], in0=src[:, q, P:2 * P], scalar=wave[:, 1, 7:8],
                                       in1=src[:, q, 2 * P:], op0=ALU.mult, op1=ALU.add).then_inc(S("solved4"), 1)
            assert src is wave_b
            dve_offsets(v, ch)
            for c in range(NCH):
                v.wait_ge(S("v_ps4"), c + 1)
                v.tensor_tensor(x_chunk(c), x_chunk(c), bank(4 + c), ALU.add).then_inc(S("x_done4"), 1)
                v.wait_ge(S("x_done4"), c + 1)
                dve_next(v, ch, 5, c)

        def dve_offsets(v, ch):
            v.wait_ge(S("idle_ps"), E + 1)
            ch.link(v.tensor_copy(off_sum[:], bank(2, 0, D)))
            for half in range(2):
                ch(v.tensor_tensor(b2_all[:, 4 * half:4 * half + 4, :],
                                   off_sum[:].rearrange("p (o d) -> p o d", o=1).to_broadcast([P, 4, D]),
                                   bank(half).rearrange("p (e d) -> p e d", e=4), ALU.subtract))
            ch.wait()
            v.sem_inc(S("offsets"), 1)

        def dve_block5(v, ch):
            dve_whole(v, ch, 5)
            v.wait_ge(S("scores5"), 1)
            ch.link(v.tensor_tensor(em(7), em(0), over_i(rbias[2][:]), ALU.add))
            dve_choose(v, ch, 7, 0, 1, 1)
            ch.link(v.scalar_tensor_tensor(out=em(5), in0=em(1), scalar=NEG, in1=em(7), op0=ALU.mult, op1=ALU.add))
            dve_choose(v, ch, 5, 2, 3, 2)
            ch.link(v.tensor_tensor(rt[:, 9, :], rt[:, 1, :], rt[:, 2, :], ALU.add))
            ch.link(v.tensor_tensor(rt[:, 10, :], rt[:, 0, :], rt[:, 9, :], ALU.mult))

            def product(c, m):
                n, u = c * UNITS + m, m % 2
                v.wait_ge(S("silu5"), n + 1)
                if not (isinstance(n, int) and n < 2):
                    v.wait_ge(S("down5"), n - 1)
                v.tensor_tensor(hidt[:, u, :], hid[:, u, :], bank(4 + u), ALU.mult).then_inc(S("h5"), 1)

            def add(c, m):
                n = c * UNITS + m
                v.wait_ge(S("down5"), n + 1)
                if not (isinstance(c, int) and c == 0 and m < KF):
                    v.wait_ge(S("acc5"), c * (E + 1) + (m - KF + 1 if m >= KF else 0))
                rows = x_sb[:, bass.ds(c * TPC, TPC), :]
                if m < KF:
                    v.tensor_tensor(rows, rows, bank(3).rearrange("p (i d) -> p i d", d=D), ALU.add)\
                        .then_inc(S("acc5"), 1)
                    return
                e = m - KF
                for j in range(TPC):
                    row = x_sb[:, bass.ds(c * TPC + j, 1), :].rearrange("p o d -> p (o d)")
                    last = v.scalar_tensor_tensor(out=row, in0=bank(6 + e % 2, j * P, (j + 1) * P),
                                                  scalar=rt[:, 10, bass.ds(c * TPC + (e * NTILE + j), 1)],
                                                  in1=row, op0=ALU.mult, op1=ALU.add)
                last.then_inc(S("acc5"), 1)

            def chunk(c, last=False):
                for m in range(UNITS):
                    product(c, m)
                    if last and m < NCH - 1:
                        v.wait_ge(S("acc5"), (E + 1) * (m + 1))
                        dve_next(v, ch, 6, m)
                    if m > KF - 1 and m - 1 >= KF - 1:
                        add(c, m - 1)
                add(c, UNITS - 1)

            chunk(0)
            with v.Fori(1, NCH - 1) as c:
                chunk(c)
            chunk(NCH - 1, last=True)
            v.wait_ge(S("acc5"), NCH * (E + 1))
            v.sem_inc(S("x_done5"), NCH)
            dve_next(v, ch, 6, NCH - 1)

        def dve_block6(v, ch):
            v.wait_ge(S("w6_in"), 16 * 7)
            pairs = w_qkv[:, 0:2 * D].rearrange("p (i z) -> p z i", z=2)
            turned = w_rot.rearrange("p (i z) -> p z i", z=2)
            v.tensor_scalar(turned[:, 0, :], pairs[:, 1, :], -1.0, None, ALU.mult).then_inc(S("w_rot"), 1)
            v.tensor_copy(turned[:, 1, :], pairs[:, 0, :]).then_inc(S("w_rot"), 1)
            dve_whole(v, ch, 6)
            v.wait_ge(S("b_rot_ps"), 1)
            v.tensor_copy(b_rot[:], bank(7, 0, 2)).then_inc(S("b_rot"), 1)
            v.wait_ge(S("b_rot"), 1)
            both = [P, 2, L]

            def two(ap):
                return ap.rearrange("p (b t) -> p b t", t=L)

            for c in range(NCH):
                for z in range(2):
                    v.wait_ge(S("qk_ps6"), 4 * c + 2 * z + 2)
                    cos, sin = (rope[:, 2 * z + y:2 * z + y + 1, :].to_broadcast(both) for y in range(2))
                    ch(v.scalar_tensor_tensor(out=two(hid[:, z, :]), in0=two(bank(2 + 2 * z)), scalar=b_qk[:, z:z + 1],
                                              in1=cos, op0=ALU.add, op1=ALU.mult))
                    ch.link(v.scalar_tensor_tensor(out=two(hidt[:, z, :]), in0=two(bank(3 + 2 * z)),
                                                   scalar=b_rot[:, z:z + 1], in1=sin, op0=ALU.add, op1=ALU.mult))
                    v.tensor_tensor(hid[:, z, :], hid[:, z, :], hidt[:, z, :], ALU.add).then_inc(S("f6"), 1)
                for z, parts in enumerate((q_parts, k_parts)):
                    v.wait_ge(S("f6"), 2 * c + z + 1)
                    v.wait_ge(S("p0_6"), 2 * c + z + 1)
                    v.tensor_tensor(hidt[:, z, :], hid[:, z, :], parts[0][:, chunk_cols(c)], ALU.subtract)\
                        .then_inc(S("r6"), 1)
                v.wait_ge(S("v_ps6"), c + 1)
                v.wait_ge(S("xt_ps"), 6 * NCH + c + 1)
                v.tensor_tensor(xn[:, TPC * c:TPC * (c + 1), :],
                                bank(6).rearrange("p (i d) -> p i d", d=D),
                                bv6.rearrange("p (o d) -> p o d", o=1).to_broadcast([P, TPC, D]), ALU.add)\
                    .then_inc(S("v6"), 1)
                for z, (parts, done) in enumerate(((q_parts, "q6"), (k_parts, "k6"))):
                    v.wait_ge(S("r6"), 2 * c + z + 1)
                    v.wait_ge(S("p1_6"), 2 * c + z + 1)
                    v.tensor_tensor(parts[2][:, chunk_cols(c)], hidt[:, z, :], parts[1][:, chunk_cols(c)], ALU.subtract)\
                        .then_inc(S(done), 1)
                    v.wait_ge(S(done), c + 1)
            v.wait_ge(S("v6"), NCH)
            v.memset(bank(4), 0.0).then_inc(S("clear6"), 1)
            v.memset(v_seq.rearrange("p u t h d -> p (u t h d)"), 1.0).then_inc(S("v_ones"), 1)
            v.wait_ge(S("v_ones"), 1)

            def values(g, u):
                s = g * 2 + u
                if not (isinstance(s, int) and s < 2):
                    v.wait_ge(S("pv6"), s * HEADS - HEADS)
                for t in range(2):
                    last = v.tensor_scalar(v_seq[:, u, t, :, 0:HD],
                                           xn[:, bass.ds(s * 2 + t, 1), :].rearrange("p o (h d) -> p (o h) d", h=HEADS),
                                           ones[:, 0:1], None, ALU.mult)
                last.then_inc(S("v_seq6"), 1)

            def lows(g, i):
                g, i = (g + 1, i - 2 * HEADS) if i >= 2 * HEADS else (g, i)
                n = g * (2 * HEADS) + i
                if not (isinstance(n, int) and n < 4):
                    v.wait_ge(S("exp6"), n - 3)
                v.wait_ge(S("s6"), n + 1)
                v.tensor_reduce(low[:, i % 4, :], bank(i % 4).rearrange("p (t k) -> p t k", t=2), AX.X, ALU.min)\
                    .then_inc(S("low6"), 1)

            def weights(g, i):
                n = g * (2 * HEADS) + i
                v.wait_ge(S("t6"), n + 1)
                if not (isinstance(n, int) and n < 2):
                    v.wait_ge(S("pv6"), n - 1)
                v.tensor_copy(probs_t[:, i % 2, :], bank(6 + i % 2)).then_inc(S("pt_dve6"), 1)

            def divide(s, half):
                v.wait_ge(S("tok6"), s * 2 + (half + 1))
                v.reciprocal(inv_sum[:], bank(5)[:, HD::32]).then_inc(S("inv6"), 1)
                v.wait_ge(S("inv6"), s * 2 + (half + 1))
                for t in range(2):
                    cols = slice(half * D // 2, (half + 1) * D // 2)
                    h = HEADS // 2
                    last = v.tensor_tensor(
                        xn[:, bass.ds(s * 2 + t, 1), cols].rearrange("p o (h d) -> p (o h) d", h=h),
                        bank(5, 2 * t * P, 2 * (t + 1) * P).rearrange("p (h z) -> p h z", z=32)[:, :, 0:HD],
                        inv_sum[:, t * h:(t + 1) * h].rearrange("p (h o) -> p h o", o=1).to_broadcast([P, h, HD]), ALU.mult)
                last.then_inc(S("o6"), 1)

            values(0, 0)
            values(0, 1)
            lows(0, 0)
            lows(0, 1)

            def steps(g, last=False):
                for i in range(2 * HEADS):
                    if not (last and i + 2 >= 2 * HEADS):
                        lows(g, i + 2)
                    if i % 8 not in BY_ACT:
                        weights(g, i)
                    if i % 8 == 4 and not (isinstance(g, int) and g == 0 and i == 4):
                        z = (i - 12) // 8
                        divide(g * 2 + z // 2, z % 2)
                    if i == HEADS + 1 and not last:
                        values(g + 1, 0)
                    if i == 1 and not (isinstance(g, int) and g == 0):
                        values(g, 1)

            steps(0)
            with v.Fori(1, NB // 2 - 1) as g:
                steps(g)
            steps(NB // 2 - 1, last=True)
            divide(NB - 1, 1)
            for c in range(NCH):
                v.wait_ge(S("proj_ps6"), c + 1)
                ch.link(v.tensor_tensor(x_chunk(c), x_chunk(c), bank(2 + c % 2), ALU.add))
                rows = x_sb[:, TPC * c:TPC * (c + 1), :]
                v.tensor_tensor(rows, rows, pb6.rearrange("p (o d) -> p o d", o=1).to_broadcast([P, TPC, D]), ALU.add)\
                    .then_inc(S("x_done6"), 1)
                v.wait_ge(S("x_done6"), c + 1)
                dve_next(v, ch, 7, c)

        @block.vector
        def _(v):
            ch = Chain(v, "dve_steps")
            dve_block0(v, ch)
            dve_rel_bias(v, ch)
            dve_moe(v, ch, 1)
            dve_block2(v, ch)
            dve_moe(v, ch, 3)
            dve_block4(v, ch)
            dve_block5(v, ch)
            dve_block6(v, ch)
            dve_moe(v, ch, 7)


_SHAPE = (NB, L, D)
_T = {"L0_attn_Wq", "L0_attn_Wv", "L0_attn_Wg", "L0_attn_Wo", "L2_ffn_router_w", "L2_attn_B_weight",
      "L1_attn_gamma", "L1_attn_beta", "L2_ffn_shared_w1", "L2_ffn_shared_w2", "L2_ffn_shared_w3",
      "L3_attn_qkv_w", "L3_attn_proj_w"}


def kernel(**inputs):
    import concourse.bacc as _bacc
    from concourse.bass_utils import run_bass_kernel_spmd as _run

    data = {(name + "T" if name in _T else name): (value.T if name in _T else value) for name, value in inputs.items()}
    data.update(const_bucket=bucket_rows(), const_pair=pair_matrix(), const_rope=rope_tables())
    data["L2_ffn_w12T"] = inputs["L2_ffn_w12"].transpose(2, 0, 1)
    data["L2_ffn_w3T"] = inputs["L2_ffn_w3"].transpose(2, 0, 1)
    data["L3_ffn_b1T"] = inputs["L3_ffn_b1"].T
    data["L3_attn_qkv_bT"] = inputs["L3_attn_qkv_b"].reshape(3, D).T
    nc = _bacc.Bacc("TRN2", target_bir_lowering=False, num_devices=1)
    arrays, aps = {}, {}
    for name, value in data.items():
        value = np.ascontiguousarray(value)
        arrays[f"in_{name}"] = value
        aps[name] = nc.dram_tensor(f"in_{name}", value.shape, mybir.dt.from_np(value.dtype), kind="ExternalInput").ap()
    out = nc.dram_tensor("out_x", _SHAPE, F32, kind="ExternalOutput").ap()
    build(nc, aps, out)
    r = _run(nc, [arrays], core_ids=[0])
    return r.results[0]["out_x"]
```
